# Optimizing a Trainium2 kernel written in Bass

```python
import numpy as np
import jax
import jax.numpy as jnp

def _softmax(x, axis=-1):
    return jax.nn.softmax(x, axis=axis)

def _gelu(x):
    return jax.nn.gelu(x, approximate=True)

def _silu(x):
    return jax.nn.silu(x)

def _sigmoid(x):
    return jax.nn.sigmoid(x)

def _layernorm(x, axis=-1, eps=1e-05):
    m = jnp.mean(x, axis=axis, keepdims=True)
    v = jnp.var(x, axis=axis, keepdims=True)
    return (x - m) / jnp.sqrt(v + eps)

def _scatter_add(tgt, idx, src, axis=0):
    return tgt.at[idx].add(src)

def _segment_sum(src, seg, n):
    return jax.ops.segment_sum(src, seg, n)
kernel_name = 'mk_recurrent_d1_jaxref_r8_1e04d5'

def setup_inputs(seed: int=0):
    np.random.seed(seed)
    _w = jnp.asarray

    def _L0_attn_setup():
        import jax, jax.numpy as jnp
        import numpy as np
        HIDDEN = 256
        NKH, NVH, HD, K = (16, 32, 128, 4)
        KDIM = NKH * HD
        VDIM = NVH * HD
        CONV = 2 * KDIM + VDIM
        EXP = NVH // NKH

        def _l2norm(a):
            n = jnp.sqrt(jnp.sum(a * a, axis=-1, keepdims=True))
            return a / jnp.maximum(n, 1e-12)

        def _reference_tuple_inner(x, W_qkv, W_z, W_b, W_a, conv_w, dt_bias, A_log, norm_w, W_out):
            B, T, _ = x.shape
            qkv = jnp.einsum('bth,ch->btc', x, W_qkv)
            z = jnp.einsum('bth,vh->btv', x, W_z)
            b_raw = jnp.einsum('bth,nh->btn', x, W_b)
            a_raw = jnp.einsum('bth,nh->btn', x, W_a)
            qkv_t = jnp.swapaxes(qkv, 1, 2)
            padded = jnp.concatenate([jnp.zeros((B, CONV, K - 1), x.dtype), qkv_t], axis=2)
            w = conv_w[:, 0, :]
            conv = sum((w[None, :, j:j + 1] * padded[:, :, j:j + T] for j in range(K)))
            conv = jax.nn.silu(conv)
            new_conv_buf = padded[..., T:]
            qkvc = jnp.swapaxes(conv, 1, 2)
            q = qkvc[..., :KDIM].reshape(B, T, NKH, HD)
            kk = qkvc[..., KDIM:2 * KDIM].reshape(B, T, NKH, HD)
            v = qkvc[..., 2 * KDIM:].reshape(B, T, NVH, HD)
            q = jnp.repeat(q, EXP, axis=2)
            kk = jnp.repeat(kk, EXP, axis=2)
            q = _l2norm(q)
            kk = _l2norm(kk)
            beta = jax.nn.sigmoid(b_raw)
            g = -jnp.exp(A_log) * jax.nn.softplus(a_raw + dt_bias)
            decay = jnp.exp(g)
            state0 = jnp.zeros((B, NVH, HD, HD), x.dtype)
            tm = lambda a: jnp.moveaxis(a, 1, 0)

            def step(state, inp):
                q_t, k_t, v_t, b_t, d_t = inp
                state = state * d_t[..., None, None]
                Sk = jnp.einsum('bhi,bhij->bhj', k_t, state)
                delta = (v_t - Sk) * b_t[..., None]
                state = state + jnp.einsum('bhi,bhj->bhij', k_t, delta)
                o = jnp.einsum('bhi,bhij->bhj', q_t, state)
                return (state, o)
            state, o = jax.lax.scan(step, state0, (tm(q), tm(kk), tm(v), tm(beta), tm(decay)))
            o = jnp.moveaxis(o, 0, 1)
            zz = z.reshape(B, T, NVH, HD)
            y = o * jax.nn.silu(zz)
            y = y * jax.lax.rsqrt(jnp.mean(y * y, axis=-1, keepdims=True) + 1e-06) * norm_w
            out = jnp.einsum('btv,ov->bto', y.reshape(B, T, VDIM), W_out)
            return (out, state, new_conv_buf)
        key = jax.random.key(seed)
        ks = jax.random.split(key, 8)
        s = 0.02
        B, T = (2, 256)
        return {'x': jax.random.normal(ks[0], (B, T, HIDDEN), jnp.float32), 'W_qkv': jax.random.normal(ks[1], (CONV, HIDDEN), jnp.float32) * s, 'W_z': jax.random.normal(ks[2], (VDIM, HIDDEN), jnp.float32) * s, 'W_b': jax.random.normal(ks[3], (NVH, HIDDEN), jnp.float32) * s, 'W_a': jax.random.normal(ks[4], (NVH, HIDDEN), jnp.float32) * s, 'conv_w': jax.random.normal(ks[5], (CONV, 1, K), jnp.float32) * 0.1, 'dt_bias': jnp.ones((NVH,), jnp.float32), 'A_log': jnp.zeros((NVH,), jnp.float32), 'norm_w': jnp.ones((HD,), jnp.float32), 'W_out': jax.random.normal(ks[6], (HIDDEN, VDIM), jnp.float32) * s}
    _L0_attn_in = _L0_attn_setup()

    def _L0_ffn_setup():
        import jax, jax.numpy as jnp
        import numpy as np
        TOP_K = 2

        def _gelu(v):
            return jax.nn.gelu(v, approximate=False)
        key = jax.random.key(seed)
        ks = jax.random.split(key, 7)
        B, T, D, I, E = (2, 256, 256, 1024, 8)
        s = 0.02
        return {'x': jax.random.normal(ks[0], (B, T, D), jnp.float32), 'rw1': jax.random.normal(ks[1], (D, D // 2), jnp.float32) * s, 'rw2': jax.random.normal(ks[2], (D // 2, E), jnp.float32) * s, 'w1': jax.random.normal(ks[3], (E, D, I), jnp.float32) * s, 'b1': jax.random.normal(ks[4], (E, I), jnp.float32) * s, 'w2': jax.random.normal(ks[5], (E, I, D), jnp.float32) * s, 'b2': jax.random.normal(ks[6], (E, D), jnp.float32) * s}
    _L0_ffn_in = _L0_ffn_setup()
    _d = {'L0_attn_x': _L0_attn_in['x'], 'L0_attn_W_qkv': _L0_attn_in['W_qkv'], 'L0_attn_W_z': _L0_attn_in['W_z'], 'L0_attn_W_b': _L0_attn_in['W_b'], 'L0_attn_W_a': _L0_attn_in['W_a'], 'L0_attn_conv_w': _L0_attn_in['conv_w'], 'L0_attn_dt_bias': _L0_attn_in['dt_bias'], 'L0_attn_A_log': _L0_attn_in['A_log'], 'L0_attn_norm_w': _L0_attn_in['norm_w'], 'L0_attn_W_out': _L0_attn_in['W_out'], 'L0_ffn_rw1': _L0_ffn_in['rw1'], 'L0_ffn_rw2': _L0_ffn_in['rw2'], 'L0_ffn_w1': _L0_ffn_in['w1'], 'L0_ffn_b1': _L0_ffn_in['b1'], 'L0_ffn_w2': _L0_ffn_in['w2'], 'L0_ffn_b2': _L0_ffn_in['b2']}
    _x0 = _d['L0_attn_x']
    _d['L0_attn_x'] = jax.random.normal(jax.random.fold_in(jax.random.key(seed), 1), (8, 256, 256), dtype=_x0.dtype)
    del _x0
    return _d

def reference(L0_attn_x, L0_attn_W_qkv, L0_attn_W_z, L0_attn_W_b, L0_attn_W_a, L0_attn_conv_w, L0_attn_dt_bias, L0_attn_A_log, L0_attn_norm_w, L0_attn_W_out, L0_ffn_rw1, L0_ffn_rw2, L0_ffn_w1, L0_ffn_b1, L0_ffn_w2, L0_ffn_b2):

    def _L0_attn_ref(x, W_qkv, W_z, W_b, W_a, conv_w, dt_bias, A_log, norm_w, W_out):
        import jax, jax.numpy as jnp
        import numpy as np
        HIDDEN = 256
        NKH, NVH, HD, K = (16, 32, 128, 4)
        KDIM = NKH * HD
        VDIM = NVH * HD
        CONV = 2 * KDIM + VDIM
        EXP = NVH // NKH

        def _l2norm(a):
            n = jnp.sqrt(jnp.sum(a * a, axis=-1, keepdims=True))
            return a / jnp.maximum(n, 1e-12)

        def _reference_tuple_inner(x, W_qkv, W_z, W_b, W_a, conv_w, dt_bias, A_log, norm_w, W_out):
            B, T, _ = x.shape
            qkv = jnp.einsum('bth,ch->btc', x, W_qkv)
            z = jnp.einsum('bth,vh->btv', x, W_z)
            b_raw = jnp.einsum('bth,nh->btn', x, W_b)
            a_raw = jnp.einsum('bth,nh->btn', x, W_a)
            qkv_t = jnp.swapaxes(qkv, 1, 2)
            padded = jnp.concatenate([jnp.zeros((B, CONV, K - 1), x.dtype), qkv_t], axis=2)
            w = conv_w[:, 0, :]
            conv = sum((w[None, :, j:j + 1] * padded[:, :, j:j + T] for j in range(K)))
            conv = jax.nn.silu(conv)
            new_conv_buf = padded[..., T:]
            qkvc = jnp.swapaxes(conv, 1, 2)
            q = qkvc[..., :KDIM].reshape(B, T, NKH, HD)
            kk = qkvc[..., KDIM:2 * KDIM].reshape(B, T, NKH, HD)
            v = qkvc[..., 2 * KDIM:].reshape(B, T, NVH, HD)
            q = jnp.repeat(q, EXP, axis=2)
            kk = jnp.repeat(kk, EXP, axis=2)
            q = _l2norm(q)
            kk = _l2norm(kk)
            beta = jax.nn.sigmoid(b_raw)
            g = -jnp.exp(A_log) * jax.nn.softplus(a_raw + dt_bias)
            decay = jnp.exp(g)
            state0 = jnp.zeros((B, NVH, HD, HD), x.dtype)
            tm = lambda a: jnp.moveaxis(a, 1, 0)

            def step(state, inp):
                q_t, k_t, v_t, b_t, d_t = inp
                state = state * d_t[..., None, None]
                Sk = jnp.einsum('bhi,bhij->bhj', k_t, state)
                delta = (v_t - Sk) * b_t[..., None]
                state = state + jnp.einsum('bhi,bhj->bhij', k_t, delta)
                o = jnp.einsum('bhi,bhij->bhj', q_t, state)
                return (state, o)
            state, o = jax.lax.scan(step, state0, (tm(q), tm(kk), tm(v), tm(beta), tm(decay)))
            o = jnp.moveaxis(o, 0, 1)
            zz = z.reshape(B, T, NVH, HD)
            y = o * jax.nn.silu(zz)
            y = y * jax.lax.rsqrt(jnp.mean(y * y, axis=-1, keepdims=True) + 1e-06) * norm_w
            out = jnp.einsum('btv,ov->bto', y.reshape(B, T, VDIM), W_out)
            return (out, state, new_conv_buf)
        return _reference_tuple_inner(x, W_qkv, W_z, W_b, W_a, conv_w, dt_bias, A_log, norm_w, W_out)[0]

    def _L0_ffn_ref(x, rw1, rw2, w1, b1, w2, b2):
        import jax, jax.numpy as jnp
        import numpy as np
        TOP_K = 2

        def _gelu(v):
            return jax.nn.gelu(v, approximate=False)
        logits = _gelu(x @ rw1) @ rw2
        probs = jax.nn.softmax(logits, axis=-1)
        wgt, idx = jax.lax.top_k(probs, TOP_K)
        E = w1.shape[0]
        out = jnp.zeros_like(x)
        for e in range(E):
            Ye = _gelu(x @ w1[e] + b1[e]) @ w2[e] + b2[e]
            Ce = _gelu(b1[e]) @ w2[e] + b2[e]
            for k in range(TOP_K):
                mask = idx[..., k] == e
                active = jnp.any(mask).astype(x.dtype)
                term = jnp.where(mask[..., None], Ye, Ce)
                out = out + active * wgt[..., k:k + 1] * term
        return out
    x = L0_attn_x
    xn = _layernorm(x, axis=-1)
    s = _L0_attn_ref(xn, L0_attn_W_qkv, L0_attn_W_z, L0_attn_W_b, L0_attn_W_a, L0_attn_conv_w, L0_attn_dt_bias, L0_attn_A_log, L0_attn_norm_w, L0_attn_W_out)
    g = _silu(_L0_ffn_ref(xn, L0_ffn_rw1, L0_ffn_rw2, L0_ffn_w1, L0_ffn_b1, L0_ffn_w2, L0_ffn_b2))
    x = x + s * g
    return x

_drawn_inputs = setup_inputs


def setup_inputs(seed=0):
    import zlib

    import numpy as np

    out = dict(_drawn_inputs(seed))
    spreads = {'L0_attn_dt_bias': (1.0, 0.6), 'L0_attn_A_log': (0.0, 0.8), 'L0_attn_norm_w': (1.0, 0.6)}
    factors = {'L0_attn_W_qkv': 8.0,
     'L0_attn_W_z': 8.0,
     'L0_attn_W_b': 8.0,
     'L0_attn_W_a': 8.0,
     'L0_attn_conv_w': 8.0,
     'L0_attn_W_out': 8.0,
     'L0_ffn_rw1': 8.0,
     'L0_ffn_rw2': 8.0,
     'L0_ffn_w1': 8.0,
     'L0_ffn_b1': 8.0,
     'L0_ffn_w2': 8.0,
     'L0_ffn_b2': 8.0}
    for name, (base, spread) in spreads.items():
        noise = np.random.default_rng([zlib.crc32(name.encode()), seed]).standard_normal(out[name].shape)
        drawn = base * np.exp(spread * noise) if base else spread * noise
        out[name] = jnp.asarray(drawn.astype(out[name].dtype))
    for name, factor in factors.items():
        out[name] = (out[name] * factor).astype(out[name].dtype)
    return out
```

```python
from contextlib import ExitStack

import numpy as np

import concourse.bass as bass
from concourse import mybir

F32 = mybir.dt.float32
F16 = mybir.dt.float16
ALU = mybir.AluOpType
ACT = mybir.ActivationFunctionType
AX_X = mybir.AxisListType.X
ds = bass.ds

P = 128
H = 256
KH = H // P
T = 256
NE = 8
I = 1024
IC = I // P
G = 512
NLEV = 7
FW = KH * 768
OW = 2 * H
FCH = FW // 8
OCH = OW // 8
LAG = 0


def setup_phase(nc, ctx, A, S, NB, NHK):
    NT = NB * 2
    N = NB * T
    NG = N // G
    NV = 2 * NHK
    W2 = 64

    with ExitStack() as c:
        def sb(name, shape, dt=F32):
            return c.enter_context(nc.sbuf_tensor(name, shape, dt))

        def sem(name):
            return c.enter_context(nc.semaphore(name))

        stats = sb("ln_stats", [P, NT, 6])
        mv = sb("ln_mean_var", [P, NT, 2])
        rstd = sb("ln_rstd", [P, NT])
        std = sb("ln_std", [P, NT])
        xn = sb("xn", [P, NT, H])
        wab = sb("wab", [P, KH, W2])
        wabh = sb("wabh", [P, KH, W2], F16)
        wabl = sb("wabl", [P, KH, W2], F16)
        rw1 = sb("rw1", [P, KH, P])
        rw1h = sb("rw1h", [P, KH, P], F16)
        rw1l = sb("rw1l", [P, KH, P], F16)
        rw2 = sb("rw2", [P, NE])
        dtb = sb("dtb", [32, 1])
        alog = sb("alog", [32, 1])
        expa = sb("expa", [32, 1])
        nega = sb("nega", [32, 1])
        eps = sb("eps", [P, 1])
        ab = sb("ab", [W2, N])
        zrow = sb("zrow", [32, N])
        erow = sb("erow", [W2, N])
        drow = sb("drow", [32, N])
        dcut = sb("dcut", [32, N])
        gb = sb("gin_beta", [W2, N])
        h1 = sb("h1", [P, N])
        lg = sb("lg", [P, NT, NE])
        pr = sb("pr", [P, NT, NE])
        t0 = sb("t0", [P, NT, NE])
        m0 = sb("m0", [P, NT, NE])
        m1 = sb("m1", [P, NT, NE])
        red = sb("red", [P, NT])
        w0 = sb("w0", [P, NT])
        w1 = sb("w1", [P, NT])
        cnt = sb("cnt", [P, 2 * NE])
        actv = sb("actv", [P, 2 * NE])
        ones = sb("ones", [P, P])
        rank = sb("rank", [P, NE])

        s_x = sem("x_loaded")
        s_c = sem("small_inputs_loaded")
        s_v = sem("vector_step")
        s_a = sem("scalar_step")
        s_p = sem("pool_step")
        s_tr = sem("xn_transposed")
        s_xh = sem("xn_hi_written")
        s_xl = sem("xn_lo_written")
        s_xn = sem("xn_ready")
        s_ab = sem("ab_ready")
        s_abc = sem("ab_copied")
        s_h1 = sem("h1_ready")
        s_h1c = sem("h1_copied")
        s_lg = sem("logits_ready")
        s_gt = sem("gin_beta_transposed")
        s_cnt = sem("counts_summed")
        s_ct = sem("gates_transposed")
        s_st = sem("decay_stored")

        pt = [c.enter_context(nc.psum_tensor(f"tr{i}", [P, 2, KH, P], F32)) for i in range(2)]
        pab = [c.enter_context(nc.psum_tensor(f"ab_ps{i}", [P, G], F32)) for i in range(2)]
        plg = c.enter_context(nc.psum_tensor("lg_ps", [P, NT, NE], F32))
        pgt = c.enter_context(nc.psum_tensor("gt_ps", [P, 2, 8, W2], F32))
        pct = c.enter_context(nc.psum_tensor("ct_ps", [P, 512], F32))

        xs, xh, xl, ident, ident4 = S["xs"], S["xh"], S["xl"], S["ident"], S["ident4"]
        NSMALL = 13
        block = c.enter_context(nc.Block())

        @block.sync
        def _(sp):
            for t in range(0, NT, 4):
                k = min(4, NT - t)
                sp.dma_start(xs[:, t:t + k, :], A["x"].rearrange("(n p) h -> p n h", p=P)[:, t:t + k, :]).then_inc(s_x, 16)
            for dst, src in ((wab, "wab"), (rw1, "rw1"), (rw2, "rw2"), (dtb, "dtb"), (alog, "alog"),
                             (ident, "ident"), (ident4, "ident4"), (S["inj"], "inj"), (S["nmask32"], "nmask"),
                             (S["cw"], "cw"), (S["nw"], "nw"), (S["b1"], "b1"), (rank, "rank")):
                sp.dma_start(dst[:], A[src]).then_inc(s_c, 16)
            sp.wait_ge(s_v, 16)
            sp.dma_start(A["dscr"], dcut[0:NV, :]).then_inc(s_st, 16)
            sp.wait_ge(s_st, 16)

        @block.gpsimd
        def _(pool):
            nc.gpsimd.memset(ones[:], 1.0).then_inc(s_p, 1)
            nc.gpsimd.memset(S["half"][:], -0.5).then_inc(s_p, 1)
            nc.gpsimd.memset(S["tiny"][:], 1e-24).then_inc(s_p, 1)
            nc.gpsimd.memset(eps[:], 1e-5).then_inc(s_p, 1)

        @block.scalar
        def _(act):
            act.wait_ge(s_v, 1)
            act.wait_ge(s_p, 4)
            nc.scalar.activation(std[:], mv[:, :, 1], ACT.Sqrt, bias=eps[:, 0:1]).then_inc(s_a, 1)
            for i in range(NT // 2):
                act.wait_ge(s_tr, i + 1)
                nc.scalar.copy(xh[:, :, 2 * i * P:(2 * i + 2) * P].rearrange("p k (t c) -> p t k c", t=2),
                               pt[i % 2][:]).then_inc(s_xh, 1)
            for i in range(NG):
                act.wait_ge(s_ab, i + 1)
                nc.scalar.copy(ab[:, i * G:(i + 1) * G], pab[i % 2][0:W2, :]).then_inc(s_abc, 1)
            act.wait_ge(s_c, 16 * NSMALL)
            nc.scalar.activation(expa[:], alog[:], ACT.Exp).then_inc(s_a, 1)
            act.wait_ge(s_v, 5)
            nc.scalar.activation(erow[0:32, :], zrow[:], ACT.Abs).then_inc(s_a, 1)
            act.wait_ge(s_a, 3)
            nc.scalar.activation(erow[0:32, :], erow[0:32, :], ACT.Exp, scale=-1.0).then_inc(s_a, 1)
            act.wait_ge(s_abc, NG)
            nc.scalar.activation(erow[32:64, :], ab[32:64, :], ACT.Exp, scale=-1.0).then_inc(s_a, 1)
            act.wait_ge(s_a, 4)
            nc.scalar.activation(drow[:], erow[0:32, :], ACT.Ln, bias=1.0).then_inc(s_a, 1)
            act.wait_ge(s_v, 9)
            nc.scalar.activation(drow[:], drow[:], ACT.Exp, scale=nega[:, 0:1]).then_inc(s_a, 1)
            for i in range(NG):
                act.wait_ge(s_h1, i + 1)
                nc.scalar.activation(h1[:, i * G:(i + 1) * G], pab[i % 2][:], ACT.Gelu).then_inc(s_h1c, 1)
            act.wait_ge(s_v, 21)
            nc.scalar.activation(t0[:], t0[:], ACT.Exp).then_inc(s_a, 1)

        @block.vector
        def _(dve):
            n = [0]

            def step(ins):
                n[0] += 1
                ins.then_inc(s_v, 1)
                dve.wait_ge(s_v, n[0])

            v = nc.vector
            dve.wait_ge(s_x, 16 * ((NT + 3) // 4))
            for t in range(NT):
                last = v.bn_stats(stats[:, t, :], xs[:, t, :])
            last.then_inc(s_xn, 1)
            dve.wait_ge(s_xn, 1)
            for t in range(NT):
                last = v.bn_aggr(mv[:, t, :], stats[:, t, :])
            step(last)
            dve.wait_ge(s_a, 1)
            step(v.reciprocal(rstd[:], std[:]))
            for t in range(NT):
                v.tensor_scalar(xn[:, t, :], xs[:, t, :], mv[:, t, 0:1], rstd[:, t:t + 1],
                                ALU.subtract, ALU.mult).then_inc(s_xn, 1)
            dve.wait_ge(s_c, 16 * NSMALL)
            v.tensor_copy(wabh[:], wab[:])
            v.tensor_copy(rw1h[:], rw1[:])
            v.tensor_copy(S["id16"][:], ident4[:])
            step(v.tensor_copy(S["nmask"][:], S["nmask32"][:]))
            v.tensor_tensor(wabl[:], wab[:], wabh[:], ALU.subtract)
            step(v.tensor_tensor(rw1l[:], rw1[:], rw1h[:], ALU.subtract))
            for i in range(NT // 2):
                dve.wait_ge(s_xh, i + 1)
                v.tensor_tensor(xl[:, :, 2 * i * P:(2 * i + 2) * P].rearrange("p k (t c) -> p t k c", t=2),
                                pt[i % 2][:],
                                xh[:, :, 2 * i * P:(2 * i + 2) * P].rearrange("p k (t c) -> p t k c", t=2),
                                ALU.subtract).then_inc(s_xl, 1)
            dve.wait_ge(s_abc, NG)
            step(v.tensor_scalar(zrow[:], ab[0:32, :], dtb[:, 0:1], None, ALU.add))
            dve.wait_ge(s_a, 6)
            step(v.tensor_scalar(erow[32:64, :], erow[32:64, :], 1.0, None, ALU.add))
            step(v.reciprocal(gb[32:64, :], erow[32:64, :]))
            step(v.tensor_scalar(nega[:], expa[:], -1.0, None, ALU.mult))
            step(v.scalar_tensor_tensor(drow[:], zrow[:], 0.0, drow[:], ALU.max, ALU.add))
            dve.wait_ge(s_a, 7)
            first = lambda a: a[:].rearrange("p (n t) -> p n t", t=P)[:, :, 0:1]
            step(v.tensor_copy(dcut[:], drow[:]))
            step(v.memset(zrow[:], 0.0))
            step(v.tensor_copy(first(zrow), first(drow)))
            step(v.memset(first(dcut), 0.0))
            step(v.tensor_tensor_scan(gb[0:32, :], dcut[:], zrow[:], 0.0, ALU.mult, ALU.add))
            step(v.memset(cnt[:], 0.0))
            step(v.memset(S["accf"][:], 0.0))
            for q in range((NT + 7) // 8):
                k = min(8, NT - 8 * q)
                dve.wait_ge(s_gt, q + 1)
                v.tensor_copy(S["col"][:, 8 * q:8 * q + k, :], pgt[:, q, 0:k, :])
            step(v.memset(S["acca"][:], 0.0))
            step(v.tensor_scalar(S["ngin"][:], S["col"][:, :, 0:32], -1.0, None, ALU.mult))
            dve.wait_ge(s_lg, 1)
            bc = lambda a: a[:].unsqueeze(2).to_broadcast([P, NT, NE])
            rk = rank[:].unsqueeze(1).to_broadcast([P, NT, NE])
            step(v.tensor_copy(lg[:], plg[:]))
            step(v.tensor_reduce(red[:], lg[:], AX_X, ALU.max))
            step(v.tensor_tensor(t0[:], lg[:], bc(red), ALU.subtract))
            dve.wait_ge(s_a, 8)
            step(v.tensor_reduce(red[:], t0[:], AX_X, ALU.add))
            step(v.reciprocal(red[:], red[:]))
            step(v.tensor_tensor(pr[:], t0[:], bc(red), ALU.mult))
            for m, w in ((m0, w0), (m1, w1)):
                step(v.tensor_reduce(w[:], pr[:], AX_X, ALU.max))
                step(v.tensor_tensor(m[:], pr[:], bc(w), ALU.is_equal))
                step(v.tensor_tensor(m[:], m[:], rk, ALU.mult))
                step(v.tensor_reduce(red[:], m[:], AX_X, ALU.max))
                step(v.tensor_tensor(m[:], m[:], bc(red), ALU.is_equal))
                if m is m0:
                    step(v.scalar_tensor_tensor(pr[:], m[:], -4.0, pr[:], ALU.mult, ALU.add))
            step(v.tensor_reduce(cnt[:, 0:NE], m0[:].rearrange("p n e -> p e n"), AX_X, ALU.add))
            step(v.tensor_reduce(cnt[:, NE:2 * NE], m1[:].rearrange("p n e -> p e n"), AX_X, ALU.add))
            step(v.tensor_tensor(m0[:], m0[:], bc(w0), ALU.mult))
            step(v.tensor_tensor(m1[:], m1[:], bc(w1), ALU.mult))
            step(v.tensor_tensor(S["gate"][:], m0[:], m1[:], ALU.add))
            dve.wait_ge(s_cnt, 1)
            step(v.tensor_scalar(actv[:], pct[:, 0:2 * NE], 0.0, None, ALU.is_gt))
            act0 = actv[:, 0:NE].unsqueeze(1).to_broadcast([P, NT, NE])
            act1 = actv[:, NE:2 * NE].unsqueeze(1).to_broadcast([P, NT, NE])
            step(v.tensor_tensor(m0[:], act0, bc(w0), ALU.mult))
            step(v.tensor_tensor(m1[:], act1, bc(w1), ALU.mult))
            step(v.tensor_tensor(S["gc"][:, :, 0:NE], m0[:], m1[:], ALU.add))
            v.tensor_tensor(S["gc"][:, :, NE:2 * NE], S["gc"][:, :, 0:NE], S["gate"][:], ALU.subtract).then_inc(s_ct, 1)

        @block.tensor
        def _(pe):
            pe.wait_ge(s_c, 16 * NSMALL)
            for i in range(NT // 2):
                pe.wait_ge(s_xn, 1 + 2 * i + 2)
                if i >= 2:
                    pe.wait_ge(s_xl, i - 1)
                for t in range(2):
                    for k in range(KH):
                        last = nc.tensor.transpose(pt[i % 2][:, t, k, :], xn[:, 2 * i + t, k * P:(k + 1) * P], ident[:])
                last.then_inc(s_tr, 1)
            pe.wait_ge(s_xl, NT // 2)
            pe.wait_ge(s_v, 4)

            def project(out, wh, wl, i):
                for n, (w, x) in enumerate(((wh, xh), (wl, xh), (wh, xl))):
                    for k in range(KH):
                        last = nc.tensor.matmul(out, w[:, k, :], x[:, k, i * G:(i + 1) * G],
                                                start=(n == 0 and k == 0), stop=(n == 2 and k == KH - 1))
                return last

            for i in range(NG):
                if i >= 2:
                    pe.wait_ge(s_abc, i - 1)
                project(pab[i % 2][0:W2, :], wabh, wabl, i).then_inc(s_ab, 1)
            pe.wait_ge(s_abc, NG)
            for i in range(NG):
                if i >= 2:
                    pe.wait_ge(s_h1c, i - 1)
                project(pab[i % 2][:], rw1h, rw1l, i).then_inc(s_h1, 1)
            pe.wait_ge(s_h1c, NG)
            for t in range(NT):
                last = nc.tensor.matmul(plg[:, t, :], h1[:, t * P:(t + 1) * P], rw2[:], start=True, stop=True)
            last.then_inc(s_lg, 1)
            pe.wait_ge(s_v, 14)
            for t in range(NT):
                last = nc.tensor.transpose(pgt[:, t // 8, t % 8, :], gb[:, t * P:(t + 1) * P], ident[0:W2, 0:W2])
                if t % 8 == 7 or t == NT - 1:
                    last.then_inc(s_gt, 1)
            pe.wait_ge(s_v, 37)
            pe.wait_ge(s_p, 4)
            nc.tensor.matmul(pct[:, 0:2 * NE], ones[:], cnt[:], start=True, stop=True).then_inc(s_cnt, 1)
            pe.wait_ge(s_ct, 1)


def ffn_phase(nc, A, S, NB, NHK):
    NT, N = NB * 2, NB * T
    NG = N // G
    TG = G // P
    W1 = KH * I
    WX = W1 + IC * H
    NJ = NE * NG
    xh, xl, accf = S["xh"], S["xl"], S["accf"]
    gate = S["gate"][:].rearrange("p n e -> p (n e)")

    with ExitStack() as c:
        def sb(name, shape, dt=F32):
            return c.enter_context(nc.sbuf_tensor(name, shape, dt))

        def sem(name):
            return c.enter_context(nc.semaphore(name))

        raw = sb("ffn_raw", [P, WX])
        wh = sb("ffn_wh", [P, 2 * WX], F16)
        wl = sb("ffn_wl", [P, 2 * WX], F16)
        g32 = [sb(f"hid{i}", [P, G]) for i in range(2)]
        gh = sb("hid_hi", [P, 2 * IC * G], F16)
        gl = sb("hid_lo", [P, 2 * IC * G], F16)
        gb1 = sb("gelu_b1", [P, NE * IC])
        gb1h = sb("gelu_b1_hi", [P, NE * IC], F16)
        gb1l = sb("gelu_b1_lo", [P, NE * IC], F16)
        tail_r = sb("tail_rhs", [2 * NE, H])
        tail_l = sb("tail_lhs", [2 * NE, N])
        cg = sb("cg", [1, NE * H])

        hid_ps = [c.enter_context(nc.psum_tensor(f"hid_ps{i}", [P, G], F32)) for i in range(2)]
        out_ps = c.enter_context(nc.psum_tensor("ffn_ps", [P, 2 * TG * H], F32))
        cg_ps = c.enter_context(nc.psum_tensor("cg_ps", [P, 512], F32))
        tail_ps = c.enter_context(nc.psum_tensor("tail_ps", [P, 512], F32))

        s_raw = sem("expert_loaded")
        s_split = sem("expert_split")
        s_gb = sem("gelu_b1_done")
        s_gbl = sem("gelu_b1_lo_written")
        s_hid = sem("hidden_in_psum")
        s_g32 = sem("hidden_gelu")
        s_gh = sem("hidden_hi")
        s_gl = sem("hidden_lo")
        s_out = sem("expert_out_in_psum")
        s_acc = sem("expert_out_added")
        s_cg = sem("bias_only_out_in_psum")
        s_cgc = sem("bias_only_out_copied")
        s_cgd = sem("bias_only_out_placed")
        s_tl = sem("tail_lhs_in_psum")
        s_tlc = sem("tail_lhs_copied")
        s_to = sem("tail_in_psum")
        s_toa = sem("tail_added")
        s_b2 = sem("b2_loaded")
        s_sg = sem("gate_silu")
        block = c.enter_context(nc.Block())
        NTL = NT // 4

        @block.sync
        def _(sp):
            sp.dma_start(tail_r[0:NE, :], A["b2"]).then_inc(s_b2, 16)
            sp.dma_start(raw[:], A["wffn"][0]).then_inc(s_raw, 16)
            with sp.Fori(1, NE) as e:
                sp.wait_ge(s_split, e * 2)
                sp.wait_ge(s_raw, 16)
                sp.dma_start(raw[:], A["wffn"][ds(e, 1)].rearrange("e p n -> (e p) n")).then_inc(s_raw, 16)
            with sp.Fori(0, NE) as e:
                sp.wait_ge(s_cgc, e + 2)
                sp.wait_ge(s_raw, 16)
                sp.dma_start(A["cgscr"][ds(e, 1), :], cg[:, ds(e * H, H)]).then_inc(s_cgd, 16)
            sp.wait_ge(s_cgd, 16 * NE)
            sp.dma_start(tail_r[NE:2 * NE, :], A["cgscr"]).then_inc(s_b2, 16)
            sp.wait_ge(s_b2, 32)

        @block.gpsimd
        def _(pool):
            def split(e):
                pool.wait_ge(s_raw, e * 16 + 16)
                pool.wait_ge(s_raw, 16)
                nc.gpsimd.tensor_copy(wh[:, ds((e % 2) * WX, WX)], raw[:]).then_inc(s_split, 1)
                pool.wait_ge(s_split, e * 2 + 1)
                nc.gpsimd.tensor_tensor(wl[:, ds((e % 2) * WX, WX)], raw[:], wh[:, ds((e % 2) * WX, WX)],
                                        ALU.subtract).then_inc(s_split, 1)

            split(0)
            split(1)
            with pool.Fori(2, NE) as e:
                pool.wait_ge(s_cg, e - 1)
                split(e)

        @block.scalar
        def _(act):
            act.sem_inc(s_g32, 2)
            nc.scalar.activation(gb1[:], S["b1"][:], ACT.Gelu).then_inc(s_gb, 1)
            act.wait_ge(s_gb, 1)
            nc.scalar.copy(gb1h[:], gb1[:]).then_inc(s_gb, 1)
            with act.Fori(0, NE) as e:
                with act.Fori(0, NG) as g:
                    for k in range(IC):
                        n = e * (NG * IC) + g * IC + k
                        act.wait_ge(s_hid, n + 1)
                        act.wait_ge(s_gl, n + 1)
                        nc.scalar.activation(g32[k % 2][:], hid_ps[k % 2][:], ACT.Gelu,
                                             bias=S["b1"][:, ds(e * IC + k, 1)]).then_inc(s_g32, 1)
                        if k == 0:
                            act.wait_ge(s_out, e * NG + g + 1)
                        act.wait_ge(s_g32, n + 3)
                        nc.scalar.copy(gh[:, ds(g % 2 * (IC * G) + k * G, G)], g32[k % 2][:]).then_inc(s_gh, 1)
            for i in range(NT // 2):
                act.wait_ge(s_toa, i + 1)
                nc.scalar.activation(accf[:, 2 * i:2 * i + 2, :], accf[:, 2 * i:2 * i + 2, :], ACT.Silu).then_inc(s_sg, 1)

        @block.vector
        def _(dve):
            dve.sem_inc(s_gl, 2)
            dve.sem_inc(s_acc, 2)
            dve.sem_inc(s_cgc, 1)
            dve.wait_ge(s_gb, 2)
            nc.vector.tensor_tensor(gb1l[:], gb1[:], gb1h[:], ALU.subtract).then_inc(s_gbl, 1)

            def add(e, g):
                dve.wait_ge(s_out, e * NG + g + 3)
                dve.wait_ge(s_acc, e * NG + g + 2)
                for t in range(TG):
                    dst = accf[:].rearrange("p n h -> p (n h)")[:, ds(g * (TG * H) + t * H, H)]
                    last = nc.vector.scalar_tensor_tensor(
                        dst, out_ps[:, ds(g % 2 * (TG * H) + t * H, H)], gate[:, ds(e + g * (TG * NE) + t * NE, 1)],
                        dst, ALU.mult, ALU.add)
                last.then_inc(s_acc, 1)

            def low(e, g, k):
                dve.wait_ge(s_gh, e * (NG * IC) + g * IC + (k + 1))
                part = ds(g % 2 * (IC * G) + k * G, G)
                nc.vector.tensor_tensor(gl[:, part], g32[k % 2][:], gh[:, part], ALU.subtract).then_inc(s_gl, 1)

            with dve.Fori(0, NE) as e:
                for k in range(IC):
                    low(e, 0, k)
                with dve.Fori(1, NG) as g:
                    for k in range(IC):
                        low(e, g, k)
                    add(e, g - 1)
                add(e, NG - 1)
                dve.wait_ge(s_cg, e + 1)
                nc.vector.tensor_copy(cg[:, ds(e * H, H)], cg_ps[0:1, 0:H]).then_inc(s_cgc, 1)
            for q in range(NTL):
                dve.wait_ge(s_tl, q + 1)
                nc.vector.tensor_copy(tail_l[:, q * 512:(q + 1) * 512], tail_ps[0:2 * NE, :]).then_inc(s_tlc, 1)
            dve.wait_ge(s_acc, NE * NG + 2)
            for i in range(NT // 2):
                dve.wait_ge(s_to, i + 1)
                nc.vector.tensor_tensor(accf[:, 2 * i:2 * i + 2, :].rearrange("p t h -> p (t h)"),
                                        accf[:, 2 * i:2 * i + 2, :].rearrange("p t h -> p (t h)"),
                                        hid_ps[i % 2][:], ALU.add).then_inc(s_toa, 1)
            dve.wait_ge(s_sg, NT // 2)

        @block.tensor
        def _(pe):
            pe.sem_inc(s_out, 2)

            def hidden(e, g, k):
                pe.wait_ge(s_g32, e * (NG * IC) + g * IC + (k + 1))
                for m, (w, x) in enumerate(((wh, xh), (wl, xh), (wh, xl))):
                    for kk in range(KH):
                        last = nc.tensor.matmul(hid_ps[k % 2][:], w[:, ds((e % 2) * WX + kk * I + k * P, P)],
                                                x[:, kk, ds(g * G, G)],
                                                start=(m == 0 and kk == 0), stop=(m == 2 and kk == KH - 1))
                last.then_inc(s_hid, 1)

            def product(e, g, k):
                pe.wait_ge(s_gl, e * (NG * IC) + g * IC + (k + 3))
                if k == 0:
                    pe.wait_ge(s_acc, e * NG + g + 1)
                for t in range(TG):
                    for m, (x, w) in enumerate(((gh, wh), (gh, wl), (gl, wh))):
                        last = nc.tensor.matmul(out_ps[:, ds(g % 2 * (TG * H) + t * H, H)],
                                                x[:, ds(g % 2 * (IC * G) + (k * G + t * P), P)],
                                                w[:, ds((e % 2) * WX + W1 + k * H, H)],
                                                start=(k == 0 and m == 0 and t % 2 == 0), stop=(k == IC - 1 and m == 2),
                                                skip_group_check=True)
                if k == IC - 1:
                    last.then_inc(s_out, 1)

            with pe.Fori(0, NE) as e:
                pe.wait_ge(s_split, e * 2 + 2)
                for k in range(IC):
                    hidden(e, 0, k)
                with pe.Fori(1, NG) as g:
                    for k in range(IC):
                        hidden(e, g, k)
                        product(e, g - 1, k)
                for k in range(IC):
                    product(e, NG - 1, k)
                pe.wait_ge(s_gbl, 1)
                pe.wait_ge(s_cgc, e + 1)
                for k in range(IC):
                    for m, (x, w) in enumerate(((gb1h, wh), (gb1h, wl), (gb1l, wh))):
                        last = nc.tensor.matmul(cg_ps[0:1, 0:H], x[:, ds(e * IC + k, 1)],
                                                w[:, ds((e % 2) * WX + W1 + k * H, H)],
                                                start=(k == 0 and m == 0), stop=(k == IC - 1 and m == 2))
                last.then_inc(s_cg, 1)
            for q in range(NTL):
                if q:
                    pe.wait_ge(s_tlc, q)
                for t in range(4 * q, 4 * q + 4):
                    last = nc.tensor.transpose(tail_ps[0:2 * NE, (t % 4) * P:(t % 4 + 1) * P], S["gc"][:, t, :], S["ident"][:])
                last.then_inc(s_tl, 1)
            pe.wait_ge(s_b2, 32)
            pe.wait_ge(s_tlc, NTL)
            for t in range(NT):
                if t % 2 == 0 and t >= 4:
                    pe.wait_ge(s_toa, t // 2 - 1)
                last = nc.tensor.matmul(hid_ps[t // 2 % 2][:, (t % 2) * H:(t % 2 + 1) * H],
                                        tail_l[:, t * P:(t + 1) * P], tail_r[:], start=True, stop=True)
                if t % 2:
                    last.then_inc(s_to, 1)


def attention_phase(nc, A, S, NB, NHK):
    NT = NB * 2
    NJ = NB * NHK
    C0 = 4
    ident, id16 = S["ident"], S["id16"]
    xh, xl, acca, accf, xs = S["xh"], S["xl"], S["acca"], S["accf"], S["xs"]

    with ExitStack() as c:
        def sb(name, shape, dt=F32):
            return c.enter_context(nc.sbuf_tensor(name, shape, dt))

        def ring(name, shape, dt=F32):
            return [sb(f"{name}{i}", shape, dt) for i in range(2)]

        owners = {"pe": [], "dve": [], "act": [], "pool": []}

        def sem(name, owner):
            s = c.enter_context(nc.semaphore(name))
            owners[owner].append(s)
            return s

        wraw = sb("w_raw", [P, 8 * (FCH + OCH)])
        wscl = sb("w_scaled", [P, OCH])
        wfh = sb("wf_hi", [P, 2 * FW], F16)
        wfl = sb("wf_lo", [P, 2 * FW], F16)
        woh = sb("wo_hi", [P, 2 * OW], F16)
        wol = sb("wo_lo", [P, 2 * OW], F16)
        pad = sb("qkv_padded", [P, 4, T + 3])
        cv = sb("conv", [P, 4, T])
        act4 = sb("conv_silu", [P, 4, T])
        sq = sb("squares", [P, 4, P])
        ssq = sb("ssq", [P, 4])
        rn = sb("rnorm", [P, 4])
        qkn = sb("qk_unit", [P, 4, P])
        qkh = sb("qk_unit_hi", [P, 4, P], F16)
        qkl = sb("qk_unit_lo", [P, 4, P], F16)
        qkT = ring("qkT", [P, 2, 2, 2, P], F16)
        vtok = ring("v_tok", [P, 2, 2, P])
        sz = ring("silu_z", [P, 2, 2, P])
        beta = sb("beta4", [P, 2, 2])
        gin = ring("gin2", [P, 2])
        ngin = ring("ngin2", [P, 2])
        dbc = ring("decay_rows", [P, 2, T])
        Es = sb("E_strict", [P, 4, P])
        E1 = sb("E_incl", [P, 4, P])
        Eb = sb("E_strict_beta", [P, 4, P])
        E1b = sb("E_incl_beta", [P, 4, P])
        kw = sb("k_weighted", [P, 2, P])
        kwh = ring("k_weighted_hi", [P, 2, P], F16)
        kwl = ring("k_weighted_lo", [P, 2, P], F16)
        A32 = sb("A32", [P, 4, P])
        M32 = sb("M32", [P, 4, P])
        Ah = ring("A_hi", [P, 4, P], F16)
        Al = ring("A_lo", [P, 4, P], F16)
        Mh = ring("M_hi", [P, 4, P], F16)
        Ml = ring("M_lo", [P, 4, P], F16)
        XX = ring("X_XT", [P, 4, 2, P], F16)
        nP = sb("neg_P", [P, 4, P], F16)
        XF = ring("XT_final", [P, 4, P], F16)
        Rh = sb("R_hi", [P, 2, P], F16)
        R1 = sb("R1", [P, 2, P])
        Dh = ring("D_hi", [P, 2, P], F16)
        rh = sb("residual", [P, 2, P], F16)
        Dl = ring("D_lo", [P, 2, P], F16)
        Sh = sb("S_hi", [P, 2, P], F16)
        Sl = sb("S_lo", [P, 2, P], F16)
        QS = sb("q_state", [P, 2, P])
        o1 = sb("o_chunk1", [P, 2, P])
        y = sb("y", [P, 2, 2, P])
        ysq = sb("y_sq", [P, 4, P])
        yss = sb("y_ss", [P, 4])
        yr = sb("y_rms", [P, 4])
        yn = sb("y_unit", [P, 4, P])
        yh = sb("y_hi", [P, 4, P], F16)
        yl = sb("y_lo", [P, 4, P], F16)
        yT = sb("yT", [P, 2, 4, P], F16)

        def bank(name, shape, dt=F32):
            return c.enter_context(nc.psum_tensor(name, shape, dt))

        b_qk = bank("b_qk", [P, 512])
        b_v = bank("b_v", [P, 512])
        b_z = bank("b_z", [P, 512])
        b_P = bank("b_P", [P, 512])
        b_X = bank("b_X", [P, 4, 2, P])
        b_s = bank("b_s", [P, 512])
        b_o = bank("b_o", [P, 512])
        b_qk4 = b_qk[:].rearrange("p (u t) -> p u t", u=4)
        b_v4 = b_v[:].rearrange("p (u t) -> p u t", u=4)
        b_qk16 = b_qk[:].bitcast(F16).rearrange("p (n t) -> p n t", t=P)
        b_s16 = b_s[:].bitcast(F16).rearrange("p (n t) -> p n t", t=P)
        b_s4 = b_s[:].rearrange("p (u t) -> p u t", u=4)
        b_o4 = b_o[:].rearrange("p (c v t) -> p c v t", c=2, v=2)
        b_P4 = b_P[:].rearrange("p (u t) -> p u t", u=4)

        s_wld0 = c.enter_context(nc.semaphore("first_weights_loaded"))
        s_wld = [c.enter_context(nc.semaphore(f"weight_chunk_loaded{i}")) for i in range(2)]
        s_dbc = [c.enter_context(nc.semaphore(f"decay_rows_loaded{i}")) for i in range(2)]
        s_done = c.enter_context(nc.semaphore("output_stored"))
        s_settled = c.enter_context(nc.semaphore("waits_settled"))
        s_pz = c.enter_context(nc.semaphore("padding_zeroed"))
        s_ssum = c.enter_context(nc.semaphore("ssq_summed"))
        s_ysum = c.enter_context(nc.semaphore("y_ss_summed"))
        s_mul = c.enter_context(nc.semaphore("branches_multiplied"))
        s_wf = sem("front_weights_split", "pool")
        s_wo = sem("out_weights_split", "pool")
        s_wt = sem("weight_step", "pool")
        s_rn = sem("rnorm_ready", "pool")
        s_E1 = sem("E_incl_ready", "pool")
        s_Eb = sem("E_strict_beta_ready", "pool")
        s_E1b = sem("E_incl_beta_ready", "pool")
        s_kws = sem("k_weighted_step", "pool")
        s_kw = sem("k_weighted_ready", "pool")
        s_Al = sem("A_lo_ready", "pool")
        s_Ml = sem("M_lo_ready", "pool")
        s_yr = sem("y_rms_ready", "pool")
        s_rqk = sem("qk_raw_in_psum", "pe")
        s_rv = sem("v_raw_in_psum", "pe")
        s_z = sem("z_in_psum", "pe")
        s_tqk = sem("qk_tok_in_psum", "pe")
        s_tv = sem("v_tok_in_psum", "pe")
        s_T = sem("qkT_in_psum", "pe")
        s_kk = sem("kk_qk_in_psum", "pe")
        s_P = sem("inv_P_in_psum", "pe")
        s_Z = sem("inv_X_in_psum", "pe")
        s_d0 = sem("first_solve_in_psum", "pe")
        s_rs = sem("residual_in_psum", "pe")
        s_dd = sem("correction_in_psum", "pe")
        s_o = sem("o_in_psum", "pe")
        s_S = sem("state_in_psum", "pe")
        s_KQ = sem("k_q_state_in_psum", "pe")
        s_yT = sem("yT_in_psum", "pe")
        s_out = sem("out_in_psum", "pe")
        s_pqk = sem("qk_padded", "act")
        s_pv = sem("v_padded", "act")
        s_sqk = sem("qk_silu", "act")
        s_sv = sem("v_silu", "act")
        s_sz = sem("z_silu", "act")
        s_sq = sem("qk_squared", "act")
        s_vt = sem("v_tok_copied", "act")
        s_qkh = sem("qk_hi_ready", "act")
        s_Ah = sem("A_hi_ready", "act")
        s_Mh = sem("M_hi_ready", "act")
        s_X = sem("inv_X_copied", "act")
        s_Rh = sem("R_hi_ready", "act")
        s_Dh = sem("D_hi_ready", "act")
        s_Dl = sem("D_lo_ready", "act")
        s_Sh = sem("S_hi_ready", "act")
        s_QS = sem("q_state_ready", "act")
        s_ysq = sem("y_squared", "act")
        s_yh = sem("y_hi_ready", "act")
        s_tap = sem("conv_tap", "dve")
        s_cqk = sem("conv_qk_ready", "dve")
        s_cv = sem("conv_v_ready", "dve")
        s_ssq = sem("ssq_ready", "dve")
        s_qkn = sem("qk_unit_ready", "dve")
        s_qkl = sem("qk_lo_ready", "dve")
        s_qkT = sem("qkT_ready", "dve")
        s_g = sem("gates_ready", "dve")
        s_Es = sem("E_strict_ready", "dve")
        s_A = sem("A_ready", "dve")
        s_M = sem("M_ready", "dve")
        s_nP = sem("neg_P_ready", "dve")
        s_r = sem("residual_ready", "dve")
        s_Sl = sem("S_lo_ready", "dve")
        s_R1 = sem("R1_ready", "dve")
        s_o1 = sem("o_chunk1_ready", "dve")
        s_y = sem("y_ready", "dve")
        s_yss = sem("y_ss_ready", "dve")
        s_yn = sem("y_unit_ready", "dve")
        s_yl = sem("y_lo_ready", "dve")
        s_yTc = sem("yT_ready", "dve")
        s_acc = sem("out_added", "dve")
        s_fin = sem("final_step", "dve")

        def ready(eng, s, n):
            eng.wait_ge(s, n + (1 + C0))

        def spare(eng, s, n, slots=1):
            eng.wait_ge(s, n + (1 + C0 - slots))

        def settle(eng):
            eng.sem_inc(s_settled, 1)

        def start(eng, owner):
            for s in owners[owner]:
                eng.sem_inc(s, C0)

        block = c.enter_context(nc.Block())

        @block.sync
        def _(sp):
            CH = FCH + OCH
            sp.dma_start(wraw[:].rearrange("p (b n) -> p b n", b=8),
                         A["wattn"][0:8].rearrange("b p n -> p b n")).then_inc(s_wld0, 16)
            with sp.Fori(0, NJ // 2) as i:
                for u in range(2):
                    j, hk, b = 2 * i + u, i // 4, i % 4 * 2 + u
                    spare(sp, s_Es, j, 2)
                    settle(sp)
                    sp.dma_start(dbc[u][:], A["dscr"][ds(hk * 2, 2), ds(b * T, T)]
                                 .partition_broadcast(P)).then_inc(s_dbc[u], 16)
                    spare(sp, s_wf, j + 8, 2)
                    settle(sp)
                    spare(sp, s_wo, j + 8, 8)
                    settle(sp)
                    sp.dma_start(wraw[:, ds(b * CH, CH)],
                                 A["wattn"][ds(j + 8, 1)].rearrange("b p n -> (b p) n")).then_inc(s_wld[u], 16)
            for t in range(0, NT, 4):
                sp.wait_ge(s_fin, C0 + t // 4 + 1)
                sp.dma_start(A["out"].rearrange("(n p) h -> p n h", p=P)[:, t:t + 4, :], xs[:, t:t + 4, :]).then_inc(s_done, 16)
            sp.wait_ge(s_done, 16 * (NT // 4))

        @block.gpsimd
        def _(pool):
            start(pool, "pool")
            CH = FCH + OCH
            g = nc.gpsimd

            def split_front(q, head, part):
                src = wraw[:, ds(part * CH, FCH)]
                dst = ds(head % 2 * FW + part * FCH, FCH)
                settle(pool)
                g.tensor_copy(wfh[:, dst], src).then_inc(s_wt, 1)
                ready(pool, s_wt, q * 3)
                g.tensor_tensor(wfl[:, dst], src, wfh[:, dst], ALU.subtract).then_inc(s_wf, 1)

            def split_out(q, head, part):
                dst = ds(head % 2 * OW + part * OCH, OCH)
                g.tensor_tensor(wscl[:], wraw[:, ds(part * CH + FCH, OCH)], S["nw"][:, 0:1].to_broadcast([P, OCH]),
                                ALU.mult).then_inc(s_wt, 1)
                ready(pool, s_wt, q * 3 + 1)
                settle(pool)
                g.tensor_copy(woh[:, dst], wscl[:]).then_inc(s_wt, 1)
                ready(pool, s_wt, q * 3 + 2)
                g.tensor_tensor(wol[:, dst], wscl[:], woh[:, dst], ALU.subtract).then_inc(s_wo, 1)

            pool.wait_ge(s_wld0, 16)
            for q in range(8):
                split_front(q, 0, q)
                if q:
                    ready(pool, s_wo, q - 1)
                split_out(q, 0, q)

            def decays(j, p):
                ready(pool, s_Es, j)
                ready(pool, s_g, j)
                spare(pool, s_M, j)
                spare(pool, s_kws, j * 2, 2)
                g.tensor_tensor(E1[:], Es[:], S["ident4"][:].rearrange("p (u t) -> p u t", u=4), ALU.add).then_inc(s_E1, 1)
                b = beta[:].rearrange("p v c -> p (v c)").unsqueeze(2).to_broadcast([P, 4, P])
                spare(pool, s_A, j)
                g.tensor_tensor(Eb[:], Es[:], b, ALU.mult).then_inc(s_Eb, 1)
                ready(pool, s_E1, j)
                g.tensor_tensor(E1b[:], E1[:], b, ALU.mult).then_inc(s_E1b, 1)

            def unit(j):
                ready(pool, s_ssq, j)
                spare(pool, s_qkn, j)
                g.tensor_tensor(rn[:], ssq[:], S["half"][:], ALU.pow).then_inc(s_rn, 1)

            def weigh_k(j, p):
                ready(pool, s_qkn, j)
                ready(pool, s_E1b, j)
                spare(pool, s_kw, j)
                wend = E1b[:].rearrange("p (v c) t -> p v c t", v=2)[:, :, 0, P - 1:P].to_broadcast([P, 2, P])
                g.tensor_tensor(kw[:], qkn[:, 0:1, :].to_broadcast([P, 2, P]), wend, ALU.mult).then_inc(s_kws, 1)
                ready(pool, s_kws, j * 2)
                spare(pool, s_S, j, 2)
                settle(pool)
                g.tensor_copy(kwh[p][:], kw[:]).then_inc(s_kws, 1)
                ready(pool, s_kws, j * 2 + 1)
                g.tensor_tensor(kwl[p][:], kw[:], kwh[p][:], ALU.subtract).then_inc(s_kw, 1)

            def low_parts(j, p):
                ready(pool, s_Ah, j)
                g.tensor_tensor(Al[p][:], A32[:], Ah[p][:], ALU.subtract).then_inc(s_Al, 1)
                ready(pool, s_Mh, j)
                g.tensor_tensor(Ml[p][:], M32[:], Mh[p][:], ALU.subtract).then_inc(s_Ml, 1)

            def rms(j):
                ready(pool, s_yss, j)
                spare(pool, s_yn, j)
                g.tensor_tensor(yr[:], yss[:], S["half"][:], ALU.pow).then_inc(s_yr, 1)

            with pool.Fori(0, NJ // 2) as i:
                for u in range(2):
                    j, hk, b = 2 * i + u, i // 4, i % 4 * 2 + u
                    decays(j, u)
                    unit(j)
                    weigh_k(j, u)
                    low_parts(j, u)
                    rms(j)
                    pool.wait_ge(s_wld[u], i * 16 + 16)
                    spare(pool, s_z, hk * 8 + 7, 8)
                    split_front(j + 8, hk + 1, b)
                    spare(pool, s_out, hk * 8 + 7, 8)
                    ready(pool, s_wo, j + 7)
                    split_out(j + 8, hk + 1, b)

        @block.scalar
        def _(act):
            start(act, "act")
            a = nc.scalar

            def pads(j):
                ready(act, s_rqk, j)
                spare(act, s_cqk, j)
                a.copy(pad[:, 0:2, 3:T + 3], b_qk[:].rearrange("p (m t) -> p m t", m=2)).then_inc(s_pqk, 1)
                ready(act, s_rv, j)
                spare(act, s_cv, j)
                a.copy(pad[:, 2:4, 3:T + 3], b_v[:].rearrange("p (m t) -> p m t", m=2)).then_inc(s_pv, 1)

            def silus(j, p):
                ready(act, s_z, j)
                spare(act, s_y, j * 2 + 1, 4)
                a.activation(sz[p][:], b_z[:].rearrange("p (c v t) -> p c v t", c=2, v=2), ACT.Silu).then_inc(s_sz, 1)
                ready(act, s_cqk, j)
                spare(act, s_tqk, j)
                a.activation(act4[:, 0:2, :], cv[:, 0:2, :], ACT.Silu).then_inc(s_sqk, 1)
                ready(act, s_cv, j)
                spare(act, s_tv, j)
                a.activation(act4[:, 2:4, :], cv[:, 2:4, :], ACT.Silu).then_inc(s_sv, 1)

            def squares(j, p):
                ready(act, s_tqk, j)
                spare(act, s_ssq, j)
                a.activation(sq[:], b_qk4, ACT.Square).then_inc(s_sq, 1)
                ready(act, s_tv, j)
                spare(act, s_R1, j, 2)
                spare(act, s_r, j * 2, 4)
                a.copy(vtok[p][:].rearrange("p v c t -> p (v c) t"), b_v4).then_inc(s_vt, 1)

            def qk_hi(j):
                ready(act, s_qkn, j)
                spare(act, s_T, j)
                spare(act, s_qkl, j)
                a.copy(qkh[:], qkn[:]).then_inc(s_qkh, 1)

            def high_parts(j, p):
                ready(act, s_A, j)
                spare(act, s_rs, j * 2 + 1, 4)
                a.copy(Ah[p][:], A32[:]).then_inc(s_Ah, 1)
                ready(act, s_M, j)
                spare(act, s_o, j * 2 + 1, 4)
                a.copy(Mh[p][:], M32[:]).then_inc(s_Mh, 1)

            def grow(j, p, k):
                n = j * NLEV + k
                ready(act, s_Z, n)
                if k < NLEV - 1:
                    a.copy(XX[(k + 1) % 2][:], b_X[:]).then_inc(s_X, 1)
                else:
                    spare(act, s_dd, j * 2 + 1, 4)
                    a.copy(XF[p][:], b_X[:, :, 1, :]).then_inc(s_X, 1)

            def right_side(j, p, ch):
                n = j * 2 + ch
                spare(act, s_d0, n)
                if ch == 0:
                    ready(act, s_vt, j)
                    a.copy(Rh[:], vtok[p][:, :, 0, :]).then_inc(s_Rh, 1)
                else:
                    ready(act, s_R1, j)
                    a.copy(Rh[:], R1[:]).then_inc(s_Rh, 1)

            def delta(j, ch):
                n = j * 2 + ch
                ready(act, s_d0, n)
                spare(act, s_o, n, 2)
                if ch == 0:
                    spare(act, s_S, j)
                a.copy(Dh[ch][:], b_s4[:, 0:2, :]).then_inc(s_Dh, 1)
                ready(act, s_dd, n)
                a.copy(Dl[ch][:], b_s4[:, 0:2, :]).then_inc(s_Dl, 1)

            def state(j, p):
                ready(act, s_S, j)
                spare(act, s_KQ, j)
                a.copy(Sh[:], b_s4[:, 0:2, :]).then_inc(s_Sh, 1)
                ready(act, s_KQ, j)
                ready(act, s_R1, j)
                spare(act, s_o1, j)
                a.activation(QS[:, 0, :], b_s4[:, 2, :], ACT.Copy, scale=gin[p][:, 0:1])
                a.activation(QS[:, 1, :], b_s4[:, 3, :], ACT.Copy, scale=gin[p][:, 1:2]).then_inc(s_QS, 1)

            def y_square(j):
                ready(act, s_y, j * 2 + 1)
                spare(act, s_yss, j)
                a.activation(ysq[:], y[:].rearrange("p c v t -> p (c v) t"), ACT.Square).then_inc(s_ysq, 1)

            def y_hi(j):
                ready(act, s_yn, j)
                spare(act, s_yT, j)
                spare(act, s_yl, j)
                a.copy(yh[:], yn[:]).then_inc(s_yh, 1)

            with act.Fori(0, NJ // 2) as i:
                for u in range(2):
                    j, hk, b = 2 * i + u, i // 4, i % 4 * 2 + u
                    pads(j)
                    silus(j, u)
                    squares(j, u)
                    qk_hi(j)
                    high_parts(j, u)
                    for k in range(NLEV):
                        grow(j, u, k)
                    right_side(j, u, 0)
                    delta(j, 0)
                    state(j, u)
                    right_side(j, u, 1)
                    delta(j, 1)
                    y_square(j)
                    y_hi(j)

        @block.vector
        def _(dve):
            start(dve, "dve")
            v = nc.vector
            v.memset(pad[:, :, 0:3], 0.0).then_inc(s_pz, 1)
            dve.wait_ge(s_pz, 1)

            def conv(j, hk, half, src, out):
                ready(dve, src, j)
                spare(dve, (s_sqk, s_sv)[half], j)
                for tap in range(3, -1, -1):
                    for m in range(2 * half, 2 * half + 2):
                        n = (3 - tap) * 2 + m % 2 + 7 * half
                        w = S["cw"][:, ds(hk * 16 + (m * 4 + tap), 1)]
                        if tap == 3:
                            ins = v.tensor_scalar(cv[:, m, :], pad[:, m, 3:T + 3], w, None, ALU.mult)
                        else:
                            ready(dve, s_tap, j * 14 + (n - 2))
                            ins = v.scalar_tensor_tensor(cv[:, m, :], pad[:, m, tap:tap + T], w, cv[:, m, :],
                                                         ALU.mult, ALU.add)
                        ins.then_inc(s_tap if (tap, m % 2) != (0, 1) else out, 1)

            def norms(j):
                ready(dve, s_sq, j)
                spare(dve, s_rn, j)
                v.tensor_reduce(ssq[:], sq[:], AX_X, ALU.add).then_inc(s_ssum, 1)
                dve.wait_ge(s_ssum, j + 1)
                v.tensor_scalar(ssq[:], ssq[:], 1e-24, None, ALU.max).then_inc(s_ssq, 1)

            def unit(j):
                ready(dve, s_rn, j)
                spare(dve, s_qkh, j)
                spare(dve, s_kws, j * 2, 2)
                v.tensor_tensor(qkn[:], b_qk4, rn[:].unsqueeze(2).to_broadcast([P, 4, P]), ALU.mult).then_inc(s_qkn, 1)
                ready(dve, s_qkh, j)
                spare(dve, s_T, j)
                v.tensor_tensor(qkl[:], qkn[:], qkh[:], ALU.subtract).then_inc(s_qkl, 1)

            def qk_T(j, p):
                ready(dve, s_T, j)
                spare(dve, s_KQ, j, 2)
                v.tensor_copy(qkT[p][:].rearrange("p a c x t -> p (a c x) t"), b_qk16).then_inc(s_qkT, 1)

            def gates(i, j, hk, b, p):
                spare(dve, s_Eb, j)
                spare(dve, s_E1b, j)
                spare(dve, s_QS, j, 2)
                spare(dve, s_R1, j, 2)
                col = S["col"][:].rearrange("p n w -> p (n w)")
                hk2, tile = hk * 2, b * 2
                for ch in range(2):
                    v.tensor_copy(beta[:, :, ch], col[:, ds((tile + ch) * 64 + (hk2 + 32), 2)])
                v.tensor_copy(gin[p][:], col[:, ds((tile + 1) * 64 + hk2, 2)])
                v.tensor_copy(ngin[p][:], S["ngin"][:].rearrange("p n w -> p (n w)")[:, ds((tile + 1) * 32 + hk2, 2)]).then_inc(s_g, 1)
                dve.wait_ge(s_dbc[p], i * 16 + 16)
                spare(dve, s_E1, j)
                v.tensor_tensor_scan(Es[:].rearrange("p u t -> p (u t)"), S["inj"][:],
                                     dbc[p][:].rearrange("p v t -> p (v t)"), 0.0, ALU.add, ALU.mult).then_inc(s_Es, 1)

            def matrices(j):
                kk = b_v[:].rearrange("p (c x t) -> p c x t", c=2, x=2)
                four = lambda m: m[:].rearrange("p (v c) t -> p v c t", v=2)
                ready(dve, s_kk, j)
                ready(dve, s_Eb, j)
                spare(dve, s_Al, j)
                for w in range(2):
                    ins = v.tensor_tensor(four(A32)[:, w], kk[:, :, 0, :], four(Eb)[:, w], ALU.mult)
                ins.then_inc(s_A, 1)
                ready(dve, s_E1b, j)
                spare(dve, s_Ml, j)
                for w in range(2):
                    ins = v.tensor_tensor(four(M32)[:, w], kk[:, :, 1, :], four(E1b)[:, w], ALU.mult)
                ins.then_inc(s_M, 1)

            def mask(j, k):
                n = j * NLEV + k
                ready(dve, s_P, n)
                spare(dve, s_Z, n)
                v.tensor_tensor(nP[:], b_P4, S["nmask"][:, k, :].unsqueeze(1).to_broadcast([P, 4, P]),
                                ALU.mult).then_inc(s_nP, 1)

            def residual(j, p, ch):
                n = j * 2 + ch
                ready(dve, s_rs, n)
                spare(dve, s_dd, n)
                v.tensor_tensor(rh[:], vtok[p][:, :, 0, :] if ch == 0 else R1[:], b_s4[:, 0:2, :],
                                ALU.subtract).then_inc(s_r, 1)

            def state(j, p):
                ready(dve, s_Sh, j)
                spare(dve, s_KQ, j)
                v.tensor_tensor(Sl[:], b_s4[:, 0:2, :], Sh[:], ALU.subtract).then_inc(s_Sl, 1)
                ready(dve, s_KQ, j)
                spare(dve, s_r, j * 2 + 1, 2)
                spare(dve, s_Rh, j * 2 + 1, 2)
                for w in range(2):
                    ins = v.scalar_tensor_tensor(R1[:, w, :], b_s4[:, w, :], ngin[p][:, w:w + 1], vtok[p][:, w, 1, :],
                                                 ALU.mult, ALU.add)
                ins.then_inc(s_R1, 1)

            def gated(j, p, ch):
                ready(dve, s_o, j * 2 + ch)
                ready(dve, s_sz, j)
                spare(dve, s_yn, j)
                spare(dve, s_ysq, j)
                o = b_o4[:, ch]
                if ch:
                    ready(dve, s_QS, j)
                    v.tensor_tensor(o1[:], o, QS[:], ALU.add).then_inc(s_o1, 1)
                    ready(dve, s_o1, j)
                    o = o1[:]
                v.tensor_tensor(y[:, ch], o, sz[p][:, ch], ALU.mult).then_inc(s_y, 1)

            def rms(j):
                ready(dve, s_ysq, j)
                spare(dve, s_yr, j)
                v.tensor_reduce(yss[:], ysq[:], AX_X, ALU.add).then_inc(s_ysum, 1)
                dve.wait_ge(s_ysum, j + 1)
                v.tensor_scalar(yss[:], yss[:], 1.0 / P, 1e-6, ALU.mult, ALU.add).then_inc(s_yss, 1)
                ready(dve, s_yr, j)
                spare(dve, s_yh, j)
                v.tensor_tensor(yn[:], y[:].rearrange("p c v t -> p (c v) t"),
                                yr[:].unsqueeze(2).to_broadcast([P, 4, P]), ALU.mult).then_inc(s_yn, 1)
                ready(dve, s_yh, j)
                spare(dve, s_yT, j)
                v.tensor_tensor(yl[:], yn[:], yh[:], ALU.subtract).then_inc(s_yl, 1)

            def y_T(j):
                ready(dve, s_yT, j)
                spare(dve, s_out, j)
                v.tensor_copy(yT[:].rearrange("p a u t -> p (a u) t"), b_s16).then_inc(s_yTc, 1)

            def add(j, b):
                ready(dve, s_out, j)
                spare(dve, s_acc, j)
                dst = acca[:].rearrange("p n h -> p (n h)")[:, ds(b * 2 * H, 2 * H)]
                v.tensor_tensor(dst, dst, b_o[:], ALU.add).then_inc(s_acc, 1)

            with dve.Fori(0, NJ // 2) as i:
                for u in range(2):
                    j, hk, b = 2 * i + u, i // 4, i % 4 * 2 + u
                    conv(j, hk, 0, s_pqk, s_cqk)
                    conv(j, hk, 1, s_pv, s_cv)
                    gates(i, j, hk, b, u)
                    norms(j)
                    unit(j)
                    qk_T(j, u)
                    matrices(j)
                    for k in range(NLEV):
                        mask(j, k)
                    residual(j, u, 0)
                    gated(j, u, 0)
                    state(j, u)
                    residual(j, u, 1)
                    gated(j, u, 1)
                    rms(j)
                    y_T(j)
                    add(j, b)
            ready(dve, s_acc, NJ - 1)
            for t in range(0, NT, 4):
                v.tensor_tensor(acca[:, t:t + 4, :], acca[:, t:t + 4, :], accf[:, t:t + 4, :], ALU.mult).then_inc(s_mul, 1)
                dve.wait_ge(s_mul, t // 4 + 1)
                v.tensor_tensor(xs[:, t:t + 4, :], xs[:, t:t + 4, :], acca[:, t:t + 4, :], ALU.add).then_inc(s_fin, 1)

        @block.tensor
        def _(pe):
            start(pe, "pe")
            mm = nc.tensor.matmul

            def project(j, hk, b):
                pe.wait_ge(s_wf, hk * 8 + (8 + C0))
                base, tok = hk % 2 * FW, b * T

                def block_of(out, m):
                    for n, (w, x) in enumerate(((wfh, xh), (wfl, xh), (wfh, xl))):
                        for k in range(KH):
                            last = mm(out, w[:, ds(base + k * 768 + m * P, P)], x[:, k, ds(tok, T)],
                                      start=(n == 0 and k == 0), stop=(n == 2 and k == KH - 1))
                    return last

                spare(pe, s_qkT, j)
                block_of(b_qk[:, 0:T], 0)
                block_of(b_qk[:, T:2 * T], 1).then_inc(s_rqk, 1)
                spare(pe, s_A, j)
                spare(pe, s_M, j)
                block_of(b_v[:, 0:T], 2)
                block_of(b_v[:, T:2 * T], 3).then_inc(s_rv, 1)
                spare(pe, s_sz, j)
                for t in range(2):
                    for n, (w, x) in enumerate(((wfh, xh), (wfl, xh), (wfh, xl))):
                        for k in range(KH):
                            last = mm(b_z[:, t * H:(t + 1) * H], x[:, k, ds(tok + t * P, P)], w[:, ds(base + k * 768 + 512, H)],
                                      start=(n == 0 and k == 0), stop=(n == 2 and k == KH - 1))
                last.then_inc(s_z, 1)

            def to_tokens(j):
                ready(pe, s_sqk, j)
                ready(pe, s_pqk, j)
                for n, (m, ch) in enumerate(((1, 0), (1, 1), (0, 0), (0, 1))):
                    last = nc.tensor.transpose(b_qk4[:, n, :], act4[:, m, ch * P:(ch + 1) * P], ident[:])
                last.then_inc(s_tqk, 1)
                ready(pe, s_sv, j)
                ready(pe, s_pv, j)
                for w in range(2):
                    for ch in range(2):
                        last = nc.tensor.transpose(b_v4[:, 2 * w + ch, :], act4[:, 2 + w, ch * P:(ch + 1) * P], ident[:])
                last.then_inc(s_tv, 1)

            def to_channels(j):
                ready(pe, s_qkl, j)
                for a, src in enumerate((qkh, qkl)):
                    for ch in range(2):
                        for x in range(2):
                            last = nc.tensor.transpose(b_qk16[:, a * 4 + ch * 2 + x, :], src[:, 2 * x + ch, :], id16[:, 0:P])
                last.then_inc(s_T, 1)

            def similarities(j, p):
                ready(pe, s_qkT, j)
                ready(pe, s_vt, j)
                for ch in range(2):
                    for n, (a, b) in enumerate(((0, 0), (0, 1), (1, 0))):
                        last = mm(b_v[:, ch * 2 * P:(ch + 1) * 2 * P], qkT[p][:, a, ch, 0, :],
                                  qkT[p][:, b, ch].rearrange("p x t -> p (x t)"), start=(n == 0), stop=(n == 2))
                last.then_inc(s_kk, 1)

            def level(j, p, k):
                n = j * NLEV + k
                if k == 0:
                    ready(pe, s_Ah, j)
                else:
                    ready(pe, s_X, n - 1)
                spare(pe, s_nP, n)
                X = XX[k % 2]
                for w in range(4):
                    last = mm(b_P4[:, w, :], Ah[p][:, w, :], X[:, w, 0, :] if k else id16[:, 0:P], start=True, stop=True)
                last.then_inc(s_P, 1)
                ready(pe, s_nP, n)
                spare(pe, s_X, n)
                for w in range(4):
                    xt = X[:, w, 1, :] if k else id16[:, 0:P]
                    both = X[:, w].rearrange("p a t -> p (a t)") if k else id16[:, 0:2 * P]
                    if k < NLEV - 1:
                        mm(b_X[:, w].rearrange("p a t -> p (a t)"), id16[:, 0:P], both, start=True, stop=False,
                           skip_group_check=True)
                        mm(b_X[:, w, 0, :], xt, nP[:, w, :], start=False, stop=False, skip_group_check=True)
                    else:
                        mm(b_X[:, w, 1, :], id16[:, 0:P], xt, start=True, stop=False, skip_group_check=True)
                    last = mm(b_X[:, w, 1, :], nP[:, w, :], xt, start=False, stop=True, skip_group_check=True)
                last.then_inc(s_Z, 1)

            def unit(ch, w):
                return 2 * w + ch

            def solve(j, p, ch):
                n = j * 2 + ch
                ready(pe, s_Rh, n)
                if ch == 0:
                    ready(pe, s_X, j * NLEV + NLEV - 1)
                    spare(pe, s_yTc, j)
                else:
                    ready(pe, s_QS, j)
                for w in range(2):
                    last = mm(b_s4[:, w, :], XF[p][:, unit(ch, w), :], Rh[:, w, :], start=True, stop=True)
                last.then_inc(s_d0, 1)
                ready(pe, s_Dh, n)
                ready(pe, s_Al, j)
                for w in range(2):
                    for m, lhs in enumerate((id16[:, 0:P], Ah[p][:, unit(ch, w), :], Al[p][:, unit(ch, w), :])):
                        last = mm(b_s4[:, w, :], lhs, Dh[ch][:, w, :], start=(m == 0), stop=(m == 2))
                last.then_inc(s_rs, 1)
                ready(pe, s_r, n)
                for w in range(2):
                    last = mm(b_s4[:, w, :], XF[p][:, unit(ch, w), :], rh[:, w, :], start=True, stop=True)
                last.then_inc(s_dd, 1)

            def outputs(j, p, ch):
                n = j * 2 + ch
                ready(pe, s_Dl, n)
                ready(pe, s_Ml, j)
                if ch == 0:
                    spare(pe, s_acc, j)
                else:
                    ready(pe, s_y, n - 1)
                for w in range(2):
                    for m, (a, d) in enumerate(((Mh, Dh), (Ml, Dh), (Mh, Dl))):
                        last = mm(b_o4[:, ch, w, :], a[p][:, unit(ch, w), :], d[ch][:, w, :], start=(m == 0), stop=(m == 2))
                last.then_inc(s_o, 1)

            def state(j, p):
                ready(pe, s_kw, j)
                for w in range(2):
                    for m, (a, d) in enumerate(((kwh, Dh), (kwl, Dh), (kwh, Dl))):
                        last = mm(b_s4[:, w, :], a[p][:, w, :], d[0][:, w, :], start=(m == 0), stop=(m == 2))
                last.then_inc(s_S, 1)
                ready(pe, s_Sl, j)
                for x in range(2):
                    for m, (a, d) in enumerate(((0, Sh), (0, Sl), (1, Sh))):
                        last = mm(b_s[:, x * 2 * P:(x + 1) * 2 * P], qkT[p][:, a, 1, x, :],
                                  d[:].rearrange("p v t -> p (v t)"), start=(m == 0), stop=(m == 2))
                last.then_inc(s_KQ, 1)

            def y_T(j):
                ready(pe, s_yl, j)
                for a, src in enumerate((yh, yl)):
                    for w in range(4):
                        last = nc.tensor.transpose(b_s16[:, a * 4 + w, :], src[:, w, :], id16[:, 0:P])
                last.then_inc(s_yT, 1)

            def out(j, hk):
                ready(pe, s_yTc, j)
                pe.wait_ge(s_wo, hk * 8 + (8 + C0))
                base = hk % 2 * OW
                for ch in range(2):
                    for w in range(2):
                        for m, (a, wt) in enumerate(((0, woh), (0, wol), (1, woh))):
                            last = mm(b_o[:, ch * H:(ch + 1) * H], yT[:, a, 2 * ch + w, :], wt[:, ds(base + w * H, H)],
                                      start=(w == 0 and m == 0), stop=(w == 1 and m == 2))
                last.then_inc(s_out, 1)

            with pe.Fori(0, NJ // 2) as i:
                for u in range(2):
                    j, hk, b = 2 * i + u, i // 4, i % 4 * 2 + u
                    project(j, hk, b)
                    to_tokens(j)
                    to_channels(j)
                    similarities(j, u)
                    for k in range(NLEV):
                        level(j, u, k)
                    solve(j, u, 0)
                    outputs(j, u, 0)
                    state(j, u)
                    solve(j, u, 1)
                    outputs(j, u, 1)
                    y_T(j)
                    out(j, hk)


def build(nc, A, NB, NHK):
    NT, N = NB * 2, NB * T
    with ExitStack() as c:
        def sb(name, shape, dt=F32):
            return c.enter_context(nc.sbuf_tensor(name, shape, dt))

        S = {
            "xs": sb("x_tok", [P, NT, H]),
            "xh": sb("xT_hi", [P, KH, N], F16),
            "xl": sb("xT_lo", [P, KH, N], F16),
            "accf": sb("ffn_sum", [P, NT, H]),
            "acca": sb("attn_sum", [P, NT, H]),
            "ident": sb("identity", [P, P]),
            "ident4": sb("identity4", [P, 4 * P]),
            "id16": sb("identity4_16", [P, 4 * P], F16),
            "inj": sb("scan_starts", [P, 4 * P]),
            "nmask32": sb("level_masks32", [P, NLEV, P]),
            "nmask": sb("level_masks", [P, NLEV, P], F16),
            "cw": sb("conv_w", [P, NHK * 16]),
            "nw": sb("norm_w", [P, 1]),
            "b1": sb("b1", [P, NE * IC]),
            "half": sb("minus_half", [P, 4]),
            "tiny": sb("tiny", [P, 4]),
            "col": sb("gin_beta_cols", [P, NT, 64]),
            "ngin": sb("neg_gin_cols", [P, NT, 32]),
            "gate": sb("gate", [P, NT, NE]),
            "gc": sb("gate_and_bias_weight", [P, NT, 2 * NE]),
        }
        setup_phase(nc, c, A, S, NB, NHK)
        ffn_phase(nc, A, S, NB, NHK)
        attention_phase(nc, A, S, NB, NHK)


def shape_constants():
    t = np.arange(P)
    ident = np.eye(P, dtype=np.float32)
    ident4 = np.tile(ident, (1, 4))
    starts = np.tile(np.eye(P, k=1, dtype=np.float32), (1, 4))
    masks = np.zeros((P, NLEV, P), np.float32)
    for k in range(NLEV):
        b = t >> k
        masks[:, k, :] = -((b[:, None] % 2 == 1) & (b[None, :] == b[:, None] - 1)).astype(np.float32)
    rank = np.tile(np.arange(NE, 0, -1, dtype=np.float32), (P, 1))
    return {"ident": ident, "ident4": ident4, "inj": starts, "nmask": masks, "rank": rank}


def kernel(L0_attn_x, L0_attn_W_qkv, L0_attn_W_z, L0_attn_W_b, L0_attn_W_a, L0_attn_conv_w, L0_attn_dt_bias,
           L0_attn_A_log, L0_attn_norm_w, L0_attn_W_out, L0_ffn_rw1, L0_ffn_rw2, L0_ffn_w1, L0_ffn_b1, L0_ffn_w2,
           L0_ffn_b2):
    import numpy as np
    import concourse.bacc as bacc
    from concourse.bass_utils import run_bass_kernel_spmd

    g = lambda a: np.asarray(a)
    x = g(L0_attn_x)
    NB = x.shape[0]
    wqkv, wz, wout = g(L0_attn_W_qkv), g(L0_attn_W_z), g(L0_attn_W_out)
    NHK = wz.shape[0] // 256
    K = NHK * P
    q, k, v = wqkv[:K].reshape(NHK, P, H), wqkv[K:2 * K].reshape(NHK, P, H), wqkv[2 * K:].reshape(NHK, 2 * P, H)
    front = np.concatenate([q, k, v, wz.reshape(NHK, 2 * P, H)], axis=1)
    front = front.reshape(NHK, 768, KH, P).transpose(0, 3, 2, 1).reshape(NHK, P, FW)
    outw = wout.T.reshape(NHK, 2, P, H).transpose(0, 2, 1, 3).reshape(NHK, P, OW)
    chunks = np.concatenate([front.reshape(NHK, P, 8, FCH), outw.reshape(NHK, P, 8, OCH)], axis=3)
    chunks = chunks.transpose(0, 2, 1, 3).reshape(NHK * 8, P, FCH + OCH)
    wattn = np.concatenate([chunks, np.zeros((8, P, FCH + OCH), np.float32)], axis=0)
    cw = g(L0_attn_conv_w)[:, 0, :]
    cw = np.stack([cw[:K].reshape(NHK, P, 4), cw[K:2 * K].reshape(NHK, P, 4),
                   cw[2 * K:].reshape(NHK, 2, P, 4)[:, 0], cw[2 * K:].reshape(NHK, 2, P, 4)[:, 1]], axis=1)
    cw = cw.transpose(2, 0, 1, 3).reshape(P, NHK * 16)

    def col32(a):
        out = np.zeros((32, 1), np.float32)
        out[:a.shape[0], 0] = a
        return out

    def rows32(w):
        out = np.zeros((32, H), np.float32)
        out[:w.shape[0]] = w
        return out

    wab = np.concatenate([rows32(g(L0_attn_W_a)), rows32(g(L0_attn_W_b))], axis=0).reshape(64, KH, P).transpose(2, 1, 0)
    w1 = g(L0_ffn_w1).reshape(NE, KH, P, I).transpose(0, 2, 1, 3).reshape(NE, P, KH * I)
    w2 = g(L0_ffn_w2).reshape(NE, IC, P, H).transpose(0, 2, 1, 3).reshape(NE, P, IC * H)
    arrays = {
        "x": x.reshape(NB * T, H),
        "wattn": wattn,
        "wffn": np.concatenate([w1, w2], axis=2),
        "cw": cw,
        "wab": wab,
        "dtb": col32(g(L0_attn_dt_bias)),
        "alog": col32(g(L0_attn_A_log)),
        "nw": g(L0_attn_norm_w).reshape(P, 1),
        "rw1": g(L0_ffn_rw1).reshape(KH, P, P).transpose(1, 0, 2),
        "rw2": g(L0_ffn_rw2),
        "b1": g(L0_ffn_b1).reshape(NE, IC, P).transpose(2, 0, 1).reshape(P, NE * IC),
        "b2": g(L0_ffn_b2),
        **shape_constants(),
    }
    arrays = {f"in_{n}": np.ascontiguousarray(a) for n, a in arrays.items()}
    nc = bacc.Bacc("TRN2", target_bir_lowering=False, num_devices=1)
    A = {n[3:]: nc.dram_tensor(n, a.shape, mybir.dt.from_np(a.dtype), kind="ExternalInput").ap() for n, a in arrays.items()}
    A["dscr"] = nc.dram_tensor("decay_scratch", (2 * NHK, NB * T), F32, kind="Internal").ap()
    A["cgscr"] = nc.dram_tensor("bias_only_scratch", (NE, H), F32, kind="Internal").ap()
    A["out"] = nc.dram_tensor("out", (NB * T, H), F32, kind="ExternalOutput").ap()
    build(nc, A, NB, NHK)
    r = run_bass_kernel_spmd(nc, [arrays], core_ids=[0])
    return r.results[0]["out"].reshape(NB, T, H)
```

```python
from collections import namedtuple
from contextlib import ExitStack

import numpy as np

import concourse.bass as bass
from concourse import mybir

F32 = mybir.dt.float32
F16 = mybir.dt.float16
ALU = mybir.AluOpType
ACT = mybir.ActivationFunctionType
AX_X = mybir.AxisListType.X
ds = bass.ds

P = 128
H = 256
KH = H // P
T = 256
NE = 8
I = 1024
IC = I // P
G = 512
NLEV = 7
FW = KH * 768
OW = 2 * H
FCH = FW // 8
OCH = OW // 8
RING = 3
LAG = 3


Step = namedtuple("Step", "j p q hk b")


def setup_phase(nc, ctx, A, S, NB, NHK):
    NT = NB * 2
    N = NB * T
    NG = N // G
    NV = 2 * NHK
    W2 = 64

    with ExitStack() as c:
        def sb(name, shape, dt=F32):
            return c.enter_context(nc.sbuf_tensor(name, shape, dt))

        def sem(name):
            return c.enter_context(nc.semaphore(name))

        stats = sb("ln_stats", [P, NT, 6])
        mv = sb("ln_mean_var", [P, NT, 2])
        rstd = sb("ln_rstd", [P, NT])
        std = sb("ln_std", [P, NT])
        xn = sb("xn", [P, NT, H])
        wab = sb("wab", [P, KH, W2])
        wabh = sb("wabh", [P, KH, W2], F16)
        wabl = sb("wabl", [P, KH, W2], F16)
        rw1 = sb("rw1", [P, KH, P])
        rw1h = sb("rw1h", [P, KH, P], F16)
        rw1l = sb("rw1l", [P, KH, P], F16)
        rw2 = sb("rw2", [P, NE])
        dtb = sb("dtb", [32, 1])
        alog = sb("alog", [32, 1])
        expa = sb("expa", [32, 1])
        nega = sb("nega", [32, 1])
        eps = sb("eps", [P, 1])
        ab = sb("ab", [W2, N])
        zrow = sb("zrow", [32, N])
        erow = sb("erow", [W2, N])
        drow = sb("drow", [32, N])
        dcut = sb("dcut", [32, N])
        gb = sb("gin_beta", [W2, N])
        h1 = sb("h1", [P, N])
        lg = sb("lg", [P, NT, NE])
        pr = sb("pr", [P, NT, NE])
        t0 = sb("t0", [P, NT, NE])
        m0 = sb("m0", [P, NT, NE])
        m1 = sb("m1", [P, NT, NE])
        red = sb("red", [P, NT])
        w0 = sb("w0", [P, NT])
        w1 = sb("w1", [P, NT])
        cnt = sb("cnt", [P, 2 * NE])
        actv = sb("actv", [P, 2 * NE])
        ones = sb("ones", [P, P])
        rank = sb("rank", [P, NE])

        s_x = sem("x_loaded")
        s_c = sem("small_inputs_loaded")
        s_v = sem("vector_step")
        s_a = sem("scalar_step")
        s_p = sem("pool_step")
        s_tr = sem("xn_transposed")
        s_xh = sem("xn_hi_written")
        s_xl = sem("xn_lo_written")
        s_xn = sem("xn_ready")
        s_ab = sem("ab_ready")
        s_abc = sem("ab_copied")
        s_h1 = sem("h1_ready")
        s_h1c = sem("h1_copied")
        s_lg = sem("logits_ready")
        s_gt = sem("gin_beta_transposed")
        s_cnt = sem("counts_summed")
        s_ct = sem("gates_transposed")
        s_st = sem("decay_stored")

        pt = [c.enter_context(nc.psum_tensor(f"tr{i}", [P, 2, KH, P], F32)) for i in range(2)]
        pab = [c.enter_context(nc.psum_tensor(f"ab_ps{i}", [P, G], F32)) for i in range(2)]
        plg = c.enter_context(nc.psum_tensor("lg_ps", [P, NT, NE], F32))
        pgt = c.enter_context(nc.psum_tensor("gt_ps", [P, 2, 8, W2], F32))
        pct = c.enter_context(nc.psum_tensor("ct_ps", [P, 512], F32))

        xs, xh, xl, ident, ident4 = S["xs"], S["xh"], S["xl"], S["ident"], S["ident4"]
        NSMALL = 13
        block = c.enter_context(nc.Block())

        @block.sync
        def _(sp):
            for t in range(0, NT, 4):
                k = min(4, NT - t)
                sp.dma_start(xs[:, t:t + k, :], A["x"].rearrange("(n p) h -> p n h", p=P)[:, t:t + k, :]).then_inc(s_x, 16)
            for dst, src in ((wab, "wab"), (rw1, "rw1"), (rw2, "rw2"), (dtb, "dtb"), (alog, "alog"),
                             (ident, "ident"), (ident4, "ident4"), (S["inj"], "inj"), (S["nmask32"], "nmask"),
                             (S["cw"], "cw"), (S["nw"], "nw"), (S["b1"], "b1"), (rank, "rank")):
                sp.dma_start(dst[:], A[src]).then_inc(s_c, 16)
            sp.wait_ge(s_v, 16)
            sp.dma_start(A["dscr"], dcut[0:NV, :]).then_inc(s_st, 16)
            sp.wait_ge(s_st, 16)

        @block.gpsimd
        def _(pool):
            nc.gpsimd.memset(ones[:], 1.0).then_inc(s_p, 1)
            nc.gpsimd.memset(S["half"][:], -0.5).then_inc(s_p, 1)
            nc.gpsimd.memset(S["tiny"][:], 1e-24).then_inc(s_p, 1)
            nc.gpsimd.memset(eps[:], 1e-5).then_inc(s_p, 1)

        @block.scalar
        def _(act):
            act.wait_ge(s_v, 1)
            act.wait_ge(s_p, 4)
            nc.scalar.activation(std[:], mv[:, :, 1], ACT.Sqrt, bias=eps[:, 0:1]).then_inc(s_a, 1)
            for i in range(NT // 2):
                act.wait_ge(s_tr, i + 1)
                nc.scalar.copy(xh[:, :, 2 * i * P:(2 * i + 2) * P].rearrange("p k (t c) -> p t k c", t=2),
                               pt[i % 2][:]).then_inc(s_xh, 1)
            for i in range(NG):
                act.wait_ge(s_ab, i + 1)
                nc.scalar.copy(ab[:, i * G:(i + 1) * G], pab[i % 2][0:W2, :]).then_inc(s_abc, 1)
            act.wait_ge(s_c, 16 * NSMALL)
            nc.scalar.activation(expa[:], alog[:], ACT.Exp).then_inc(s_a, 1)
            act.wait_ge(s_v, 5)
            nc.scalar.activation(erow[0:32, :], zrow[:], ACT.Abs).then_inc(s_a, 1)
            act.wait_ge(s_a, 3)
            nc.scalar.activation(erow[0:32, :], erow[0:32, :], ACT.Exp, scale=-1.0).then_inc(s_a, 1)
            act.wait_ge(s_abc, NG)
            nc.scalar.activation(erow[32:64, :], ab[32:64, :], ACT.Exp, scale=-1.0).then_inc(s_a, 1)
            act.wait_ge(s_a, 4)
            nc.scalar.activation(drow[:], erow[0:32, :], ACT.Ln, bias=1.0).then_inc(s_a, 1)
            act.wait_ge(s_v, 9)
            nc.scalar.activation(drow[:], drow[:], ACT.Exp, scale=nega[:, 0:1]).then_inc(s_a, 1)
            for i in range(NG):
                act.wait_ge(s_h1, i + 1)
                nc.scalar.activation(h1[:, i * G:(i + 1) * G], pab[i % 2][:], ACT.Gelu).then_inc(s_h1c, 1)
            act.wait_ge(s_v, 21)
            nc.scalar.activation(t0[:], t0[:], ACT.Exp).then_inc(s_a, 1)

        @block.vector
        def _(dve):
            n = [0]

            def step(ins):
                n[0] += 1
                ins.then_inc(s_v, 1)
                dve.wait_ge(s_v, n[0])

            v = nc.vector
            dve.wait_ge(s_x, 16 * ((NT + 3) // 4))
            for t in range(NT):
                last = v.bn_stats(stats[:, t, :], xs[:, t, :])
            last.then_inc(s_xn, 1)
            dve.wait_ge(s_xn, 1)
            for t in range(NT):
                last = v.bn_aggr(mv[:, t, :], stats[:, t, :])
            step(last)
            dve.wait_ge(s_a, 1)
            step(v.reciprocal(rstd[:], std[:]))
            for t in range(NT):
                v.tensor_scalar(xn[:, t, :], xs[:, t, :], mv[:, t, 0:1], rstd[:, t:t + 1],
                                ALU.subtract, ALU.mult).then_inc(s_xn, 1)
            dve.wait_ge(s_c, 16 * NSMALL)
            v.tensor_copy(wabh[:], wab[:])
            v.tensor_copy(rw1h[:], rw1[:])
            v.tensor_copy(S["id16"][:], ident4[:])
            step(v.tensor_copy(S["nmask"][:], S["nmask32"][:]))
            v.tensor_tensor(wabl[:], wab[:], wabh[:], ALU.subtract)
            step(v.tensor_tensor(rw1l[:], rw1[:], rw1h[:], ALU.subtract))
            for i in range(NT // 2):
                dve.wait_ge(s_xh, i + 1)
                v.tensor_tensor(xl[:, :, 2 * i * P:(2 * i + 2) * P].rearrange("p k (t c) -> p t k c", t=2),
                                pt[i % 2][:],
                                xh[:, :, 2 * i * P:(2 * i + 2) * P].rearrange("p k (t c) -> p t k c", t=2),
                                ALU.subtract).then_inc(s_xl, 1)
            dve.wait_ge(s_abc, NG)
            step(v.tensor_scalar(zrow[:], ab[0:32, :], dtb[:, 0:1], None, ALU.add))
            dve.wait_ge(s_a, 6)
            step(v.tensor_scalar(erow[32:64, :], erow[32:64, :], 1.0, None, ALU.add))
            step(v.reciprocal(gb[32:64, :], erow[32:64, :]))
            step(v.tensor_scalar(nega[:], expa[:], -1.0, None, ALU.mult))
            step(v.scalar_tensor_tensor(drow[:], zrow[:], 0.0, drow[:], ALU.max, ALU.add))
            dve.wait_ge(s_a, 7)
            first = lambda a: a[:].rearrange("p (n t) -> p n t", t=P)[:, :, 0:1]
            step(v.tensor_copy(dcut[:], drow[:]))
            step(v.memset(zrow[:], 0.0))
            step(v.tensor_copy(first(zrow), first(drow)))
            step(v.memset(first(dcut), 0.0))
            step(v.tensor_tensor_scan(gb[0:32, :], dcut[:], zrow[:], 0.0, ALU.mult, ALU.add))
            step(v.memset(cnt[:], 0.0))
            step(v.memset(S["accf"][:], 0.0))
            for q in range((NT + 7) // 8):
                k = min(8, NT - 8 * q)
                dve.wait_ge(s_gt, q + 1)
                v.tensor_copy(S["col"][:, 8 * q:8 * q + k, :], pgt[:, q, 0:k, :])
            step(v.memset(S["acca"][:], 0.0))
            step(v.tensor_scalar(S["ngin"][:], S["col"][:, :, 0:32], -1.0, None, ALU.mult))
            dve.wait_ge(s_lg, 1)
            bc = lambda a: a[:].unsqueeze(2).to_broadcast([P, NT, NE])
            rk = rank[:].unsqueeze(1).to_broadcast([P, NT, NE])
            step(v.tensor_copy(lg[:], plg[:]))
            step(v.tensor_reduce(red[:], lg[:], AX_X, ALU.max))
            step(v.tensor_tensor(t0[:], lg[:], bc(red), ALU.subtract))
            dve.wait_ge(s_a, 8)
            step(v.tensor_reduce(red[:], t0[:], AX_X, ALU.add))
            step(v.reciprocal(red[:], red[:]))
            step(v.tensor_tensor(pr[:], t0[:], bc(red), ALU.mult))
            for m, w in ((m0, w0), (m1, w1)):
                step(v.tensor_reduce(w[:], pr[:], AX_X, ALU.max))
                step(v.tensor_tensor(m[:], pr[:], bc(w), ALU.is_equal))
                step(v.tensor_tensor(m[:], m[:], rk, ALU.mult))
                step(v.tensor_reduce(red[:], m[:], AX_X, ALU.max))
                step(v.tensor_tensor(m[:], m[:], bc(red), ALU.is_equal))
                if m is m0:
                    step(v.scalar_tensor_tensor(pr[:], m[:], -4.0, pr[:], ALU.mult, ALU.add))
            step(v.tensor_reduce(cnt[:, 0:NE], m0[:].rearrange("p n e -> p e n"), AX_X, ALU.add))
            step(v.tensor_reduce(cnt[:, NE:2 * NE], m1[:].rearrange("p n e -> p e n"), AX_X, ALU.add))
            step(v.tensor_tensor(m0[:], m0[:], bc(w0), ALU.mult))
            step(v.tensor_tensor(m1[:], m1[:], bc(w1), ALU.mult))
            step(v.tensor_tensor(S["gate"][:], m0[:], m1[:], ALU.add))
            dve.wait_ge(s_cnt, 1)
            step(v.tensor_scalar(actv[:], pct[:, 0:2 * NE], 0.0, None, ALU.is_gt))
            act0 = actv[:, 0:NE].unsqueeze(1).to_broadcast([P, NT, NE])
            act1 = actv[:, NE:2 * NE].unsqueeze(1).to_broadcast([P, NT, NE])
            step(v.tensor_tensor(m0[:], act0, bc(w0), ALU.mult))
            step(v.tensor_tensor(m1[:], act1, bc(w1), ALU.mult))
            step(v.tensor_tensor(S["gc"][:, :, 0:NE], m0[:], m1[:], ALU.add))
            v.tensor_tensor(S["gc"][:, :, NE:2 * NE], S["gc"][:, :, 0:NE], S["gate"][:], ALU.subtract).then_inc(s_ct, 1)

        @block.tensor
        def _(pe):
            pe.wait_ge(s_c, 16 * NSMALL)
            for i in range(NT // 2):
                pe.wait_ge(s_xn, 1 + 2 * i + 2)
                if i >= 2:
                    pe.wait_ge(s_xl, i - 1)
                for t in range(2):
                    for k in range(KH):
                        last = nc.tensor.transpose(pt[i % 2][:, t, k, :], xn[:, 2 * i + t, k * P:(k + 1) * P], ident[:])
                last.then_inc(s_tr, 1)
            pe.wait_ge(s_xl, NT // 2)
            pe.wait_ge(s_v, 4)

            def project(out, wh, wl, i):
                for n, (w, x) in enumerate(((wh, xh), (wl, xh), (wh, xl))):
                    for k in range(KH):
                        last = nc.tensor.matmul(out, w[:, k, :], x[:, k, i * G:(i + 1) * G],
                                                start=(n == 0 and k == 0), stop=(n == 2 and k == KH - 1))
                return last

            for i in range(NG):
                if i >= 2:
                    pe.wait_ge(s_abc, i - 1)
                project(pab[i % 2][0:W2, :], wabh, wabl, i).then_inc(s_ab, 1)
            pe.wait_ge(s_abc, NG)
            for i in range(NG):
                if i >= 2:
                    pe.wait_ge(s_h1c, i - 1)
                project(pab[i % 2][:], rw1h, rw1l, i).then_inc(s_h1, 1)
            pe.wait_ge(s_h1c, NG)
            for t in range(NT):
                last = nc.tensor.matmul(plg[:, t, :], h1[:, t * P:(t + 1) * P], rw2[:], start=True, stop=True)
            last.then_inc(s_lg, 1)
            pe.wait_ge(s_v, 14)
            for t in range(NT):
                last = nc.tensor.transpose(pgt[:, t // 8, t % 8, :], gb[:, t * P:(t + 1) * P], ident[0:W2, 0:W2])
                if t % 8 == 7 or t == NT - 1:
                    last.then_inc(s_gt, 1)
            pe.wait_ge(s_v, 37)
            pe.wait_ge(s_p, 4)
            nc.tensor.matmul(pct[:, 0:2 * NE], ones[:], cnt[:], start=True, stop=True).then_inc(s_cnt, 1)
            pe.wait_ge(s_ct, 1)


def ffn_phase(nc, A, S, NB, NHK):
    NT, N = NB * 2, NB * T
    NG = N // G
    TG = G // P
    W1 = KH * I
    WX = W1 + IC * H
    NJ = NE * NG
    xh, xl, accf = S["xh"], S["xl"], S["accf"]
    gate = S["gate"][:].rearrange("p n e -> p (n e)")

    with ExitStack() as c:
        def sb(name, shape, dt=F32):
            return c.enter_context(nc.sbuf_tensor(name, shape, dt))

        def sem(name):
            return c.enter_context(nc.semaphore(name))

        raw = sb("ffn_raw", [P, WX])
        wh = sb("ffn_wh", [P, 2 * WX], F16)
        wl = sb("ffn_wl", [P, 2 * WX], F16)
        g32 = [sb(f"hid{i}", [P, G]) for i in range(2)]
        gh = sb("hid_hi", [P, 2 * IC * G], F16)
        gl = sb("hid_lo", [P, 2 * IC * G], F16)
        gb1 = sb("gelu_b1", [P, NE * IC])
        gb1h = sb("gelu_b1_hi", [P, NE * IC], F16)
        gb1l = sb("gelu_b1_lo", [P, NE * IC], F16)
        tail_r = sb("tail_rhs", [2 * NE, H])
        tail_l = sb("tail_lhs", [2 * NE, N])
        cg = sb("cg", [1, NE * H])

        hid_ps = [c.enter_context(nc.psum_tensor(f"hid_ps{i}", [P, G], F32)) for i in range(2)]
        out_ps = c.enter_context(nc.psum_tensor("ffn_ps", [P, 2 * TG * H], F32))
        cg_ps = c.enter_context(nc.psum_tensor("cg_ps", [P, 512], F32))
        tail_ps = c.enter_context(nc.psum_tensor("tail_ps", [P, 512], F32))

        s_raw = sem("expert_loaded")
        s_split = sem("expert_split")
        s_gb = sem("gelu_b1_done")
        s_gbl = sem("gelu_b1_lo_written")
        s_hid = sem("hidden_in_psum")
        s_g32 = sem("hidden_gelu")
        s_gh = sem("hidden_hi")
        s_gl = sem("hidden_lo")
        s_out = sem("expert_out_in_psum")
        s_acc = sem("expert_out_added")
        s_cg = sem("bias_only_out_in_psum")
        s_cgc = sem("bias_only_out_copied")
        s_cgd = sem("bias_only_out_placed")
        s_tl = sem("tail_lhs_in_psum")
        s_tlc = sem("tail_lhs_copied")
        s_to = sem("tail_in_psum")
        s_toa = sem("tail_added")
        s_b2 = sem("b2_loaded")
        s_sg = sem("gate_silu")
        block = c.enter_context(nc.Block())
        NTL = NT // 4

        @block.sync
        def _(sp):
            sp.dma_start(tail_r[0:NE, :], A["b2"]).then_inc(s_b2, 16)
            sp.dma_start(raw[:], A["wffn"][0]).then_inc(s_raw, 16)
            with sp.Fori(1, NE) as e:
                sp.wait_ge(s_split, e * 2)
                sp.wait_ge(s_raw, 16)
                sp.dma_start(raw[:], A["wffn"][ds(e, 1)].rearrange("e p n -> (e p) n")).then_inc(s_raw, 16)
            with sp.Fori(0, NE) as e:
                sp.wait_ge(s_cgc, e + 2)
                sp.wait_ge(s_raw, 16)
                sp.dma_start(A["cgscr"][ds(e, 1), :], cg[:, ds(e * H, H)]).then_inc(s_cgd, 16)
            sp.wait_ge(s_cgd, 16 * NE)
            sp.dma_start(tail_r[NE:2 * NE, :], A["cgscr"]).then_inc(s_b2, 16)
            sp.wait_ge(s_b2, 32)

        @block.gpsimd
        def _(pool):
            def split(e):
                pool.wait_ge(s_raw, e * 16 + 16)
                pool.wait_ge(s_raw, 16)
                nc.gpsimd.tensor_copy(wh[:, ds((e % 2) * WX, WX)], raw[:]).then_inc(s_split, 1)
                pool.wait_ge(s_split, e * 2 + 1)
                nc.gpsimd.tensor_tensor(wl[:, ds((e % 2) * WX, WX)], raw[:], wh[:, ds((e % 2) * WX, WX)],
                                        ALU.subtract).then_inc(s_split, 1)

            split(0)
            split(1)
            with pool.Fori(2, NE) as e:
                pool.wait_ge(s_cg, e - 1)
                split(e)

        @block.scalar
        def _(act):
            act.sem_inc(s_g32, 2)
            nc.scalar.activation(gb1[:], S["b1"][:], ACT.Gelu).then_inc(s_gb, 1)
            act.wait_ge(s_gb, 1)
            nc.scalar.copy(gb1h[:], gb1[:]).then_inc(s_gb, 1)
            with act.Fori(0, NE) as e:
                with act.Fori(0, NG) as g:
                    for k in range(IC):
                        n = e * (NG * IC) + g * IC + k
                        act.wait_ge(s_hid, n + 1)
                        act.wait_ge(s_gl, n + 1)
                        nc.scalar.activation(g32[k % 2][:], hid_ps[k % 2][:], ACT.Gelu,
                                             bias=S["b1"][:, ds(e * IC + k, 1)]).then_inc(s_g32, 1)
                        if k == 0:
                            act.wait_ge(s_out, e * NG + g + 1)
                        act.wait_ge(s_g32, n + 3)
                        nc.scalar.copy(gh[:, ds(g % 2 * (IC * G) + k * G, G)], g32[k % 2][:]).then_inc(s_gh, 1)
            for i in range(NT // 2):
                act.wait_ge(s_toa, i + 1)
                nc.scalar.activation(accf[:, 2 * i:2 * i + 2, :], accf[:, 2 * i:2 * i + 2, :], ACT.Silu).then_inc(s_sg, 1)

        @block.vector
        def _(dve):
            dve.sem_inc(s_gl, 2)
            dve.sem_inc(s_acc, 2)
            dve.sem_inc(s_cgc, 1)
            dve.wait_ge(s_gb, 2)
            nc.vector.tensor_tensor(gb1l[:], gb1[:], gb1h[:], ALU.subtract).then_inc(s_gbl, 1)

            def add(e, g):
                dve.wait_ge(s_out, e * NG + g + 3)
                dve.wait_ge(s_acc, e * NG + g + 2)
                for t in range(TG):
                    dst = accf[:].rearrange("p n h -> p (n h)")[:, ds(g * (TG * H) + t * H, H)]
                    last = nc.vector.scalar_tensor_tensor(
                        dst, out_ps[:, ds(g % 2 * (TG * H) + t * H, H)], gate[:, ds(e + g * (TG * NE) + t * NE, 1)],
                        dst, ALU.mult, ALU.add)
                last.then_inc(s_acc, 1)

            def low(e, g, k):
                dve.wait_ge(s_gh, e * (NG * IC) + g * IC + (k + 1))
                part = ds(g % 2 * (IC * G) + k * G, G)
                nc.vector.tensor_tensor(gl[:, part], g32[k % 2][:], gh[:, part], ALU.subtract).then_inc(s_gl, 1)

            with dve.Fori(0, NE) as e:
                for k in range(IC):
                    low(e, 0, k)
                with dve.Fori(1, NG) as g:
                    for k in range(IC):
                        low(e, g, k)
                    add(e, g - 1)
                add(e, NG - 1)
                dve.wait_ge(s_cg, e + 1)
                nc.vector.tensor_copy(cg[:, ds(e * H, H)], cg_ps[0:1, 0:H]).then_inc(s_cgc, 1)
            for q in range(NTL):
                dve.wait_ge(s_tl, q + 1)
                nc.vector.tensor_copy(tail_l[:, q * 512:(q + 1) * 512], tail_ps[0:2 * NE, :]).then_inc(s_tlc, 1)
            dve.wait_ge(s_acc, NE * NG + 2)
            for i in range(NT // 2):
                dve.wait_ge(s_to, i + 1)
                nc.vector.tensor_tensor(accf[:, 2 * i:2 * i + 2, :].rearrange("p t h -> p (t h)"),
                                        accf[:, 2 * i:2 * i + 2, :].rearrange("p t h -> p (t h)"),
                                        hid_ps[i % 2][:], ALU.add).then_inc(s_toa, 1)
            dve.wait_ge(s_sg, NT // 2)

        @block.tensor
        def _(pe):
            pe.sem_inc(s_out, 2)

            def hidden(e, g, k):
                pe.wait_ge(s_g32, e * (NG * IC) + g * IC + (k + 1))
                for m, (w, x) in enumerate(((wh, xh), (wl, xh), (wh, xl))):
                    for kk in range(KH):
                        last = nc.tensor.matmul(hid_ps[k % 2][:], w[:, ds((e % 2) * WX + kk * I + k * P, P)],
                                                x[:, kk, ds(g * G, G)],
                                                start=(m == 0 and kk == 0), stop=(m == 2 and kk == KH - 1))
                last.then_inc(s_hid, 1)

            def product(e, g, k):
                pe.wait_ge(s_gl, e * (NG * IC) + g * IC + (k + 3))
                if k == 0:
                    pe.wait_ge(s_acc, e * NG + g + 1)
                for t in range(TG):
                    for m, (x, w) in enumerate(((gh, wh), (gh, wl), (gl, wh))):
                        last = nc.tensor.matmul(out_ps[:, ds(g % 2 * (TG * H) + t * H, H)],
                                                x[:, ds(g % 2 * (IC * G) + (k * G + t * P), P)],
                                                w[:, ds((e % 2) * WX + W1 + k * H, H)],
                                                start=(k == 0 and m == 0 and t % 2 == 0), stop=(k == IC - 1 and m == 2),
                                                skip_group_check=True)
                if k == IC - 1:
                    last.then_inc(s_out, 1)

            with pe.Fori(0, NE) as e:
                pe.wait_ge(s_split, e * 2 + 2)
                for k in range(IC):
                    hidden(e, 0, k)
                with pe.Fori(1, NG) as g:
                    for k in range(IC):
                        hidden(e, g, k)
                        product(e, g - 1, k)
                for k in range(IC):
                    product(e, NG - 1, k)
                pe.wait_ge(s_gbl, 1)
                pe.wait_ge(s_cgc, e + 1)
                for k in range(IC):
                    for m, (x, w) in enumerate(((gb1h, wh), (gb1h, wl), (gb1l, wh))):
                        last = nc.tensor.matmul(cg_ps[0:1, 0:H], x[:, ds(e * IC + k, 1)],
                                                w[:, ds((e % 2) * WX + W1 + k * H, H)],
                                                start=(k == 0 and m == 0), stop=(k == IC - 1 and m == 2))
                last.then_inc(s_cg, 1)
            for q in range(NTL):
                if q:
                    pe.wait_ge(s_tlc, q)
                for t in range(4 * q, 4 * q + 4):
                    last = nc.tensor.transpose(tail_ps[0:2 * NE, (t % 4) * P:(t % 4 + 1) * P], S["gc"][:, t, :], S["ident"][:])
                last.then_inc(s_tl, 1)
            pe.wait_ge(s_b2, 32)
            pe.wait_ge(s_tlc, NTL)
            for t in range(NT):
                if t % 2 == 0 and t >= 4:
                    pe.wait_ge(s_toa, t // 2 - 1)
                last = nc.tensor.matmul(hid_ps[t // 2 % 2][:, (t % 2) * H:(t % 2 + 1) * H],
                                        tail_l[:, t * P:(t + 1) * P], tail_r[:], start=True, stop=True)
                if t % 2:
                    last.then_inc(s_to, 1)


def attention_phase(nc, A, S, NB, NHK):
    NT = NB * 2
    NJ = NB * NHK
    C0 = 8
    ident, id16 = S["ident"], S["id16"]
    xh, xl, acca, accf, xs = S["xh"], S["xl"], S["acca"], S["accf"], S["xs"]

    with ExitStack() as c:
        def sb(name, shape, dt=F32):
            return c.enter_context(nc.sbuf_tensor(name, shape, dt))

        def ring(name, shape, dt=F32):
            return [sb(f"{name}{i}", shape, dt) for i in range(RING)]

        owners = {"pe": [], "dve": [], "act": [], "pool": []}

        def sem(name, owner):
            s = c.enter_context(nc.semaphore(name))
            owners[owner].append(s)
            return s

        wraw = sb("w_raw", [P, 8 * (FCH + OCH)])
        wscl = sb("w_scaled", [P, OCH])
        wfh = sb("wf_hi", [P, 2 * FW], F16)
        wfl = sb("wf_lo", [P, 2 * FW], F16)
        woh = sb("wo_hi", [P, 2 * OW], F16)
        wol = sb("wo_lo", [P, 2 * OW], F16)
        pad = sb("qkv_padded", [P, 4, T + 3])
        cv = sb("conv", [P, 4, T])
        act4 = sb("conv_silu", [P, 4, T])
        sq = sb("squares", [P, 4, P])
        ssq = sb("ssq", [P, 4])
        rn = sb("rnorm", [P, 4])
        qkn = sb("qk_unit", [P, 4, P])
        qkh = sb("qk_unit_hi", [P, 4, P], F16)
        qkl = sb("qk_unit_lo", [P, 4, P], F16)
        qkT = ring("qkT", [P, 2, 2, 2, P], F16)
        vtok = ring("v_tok", [P, 2, 2, P])
        sz = ring("silu_z", [P, 2, 2, P])
        beta = sb("beta4", [P, 2, 2])
        gin = ring("gin2", [P, 2])
        ngin = ring("ngin2", [P, 2])
        dbc = ring("decay_rows", [P, 2, T])
        Es = sb("E_strict", [P, 4, P])
        E1 = sb("E_incl", [P, 4, P])
        Eb = sb("E_strict_beta", [P, 4, P])
        E1b = sb("E_incl_beta", [P, 4, P])
        kw = sb("k_weighted", [P, 2, P])
        kwh = ring("k_weighted_hi", [P, 2, P], F16)
        kwl = ring("k_weighted_lo", [P, 2, P], F16)
        A32 = sb("A32", [P, 4, P])
        M32 = sb("M32", [P, 4, P])
        Ah = ring("A_hi", [P, 4, P], F16)
        Al = ring("A_lo", [P, 4, P], F16)
        Mh = ring("M_hi", [P, 4, P], F16)
        Ml = ring("M_lo", [P, 4, P], F16)
        XX = [sb(f"X_XT{i}", [P, 4, 2, P], F16) for i in range(2)]
        nP = sb("neg_P", [P, 4, P], F16)
        XF = ring("XT_final", [P, 4, P], F16)
        Rh = sb("R_hi", [P, 2, P], F16)
        R1 = sb("R1", [P, 2, P])
        Dh = [sb(f"D_hi{i}", [P, 2, P], F16) for i in range(2)]
        rh = sb("residual", [P, 2, P], F16)
        Dl = [sb(f"D_lo{i}", [P, 2, P], F16) for i in range(2)]
        Sh = sb("S_hi", [P, 2, P], F16)
        Sl = sb("S_lo", [P, 2, P], F16)
        QS = sb("q_state", [P, 2, P])
        o1 = sb("o_chunk1", [P, 2, P])
        y = ring("y", [P, 2, 2, P])
        ysq = sb("y_sq", [P, 4, P])
        yss = sb("y_ss", [P, 4])
        yr = sb("y_rms", [P, 4])
        yn = sb("y_unit", [P, 4, P])
        yh = sb("y_hi", [P, 4, P], F16)
        yl = sb("y_lo", [P, 4, P], F16)
        yT = sb("yT", [P, 2, 4, P], F16)

        def bank(name, shape, dt=F32):
            return c.enter_context(nc.psum_tensor(name, shape, dt))

        b_qk = bank("b_qk", [P, 512])
        b_v = bank("b_v", [P, 512])
        b_z = bank("b_z", [P, 512])
        b_P = bank("b_P", [P, 512])
        b_X = bank("b_X", [P, 4, 2, P])
        b_s = bank("b_s", [P, 512])
        b_o = bank("b_o", [P, 512])
        b_qk4 = b_qk[:].rearrange("p (u t) -> p u t", u=4)
        b_v4 = b_v[:].rearrange("p (u t) -> p u t", u=4)
        b_qk16 = b_qk[:].bitcast(F16).rearrange("p (n t) -> p n t", t=P)
        b_o16 = b_o[:].bitcast(F16).rearrange("p (n t) -> p n t", t=P)
        b_s4 = b_s[:].rearrange("p (u t) -> p u t", u=4)
        b_o4 = b_o[:].rearrange("p (c v t) -> p c v t", c=2, v=2)
        b_P4 = b_P[:].rearrange("p (u t) -> p u t", u=4)

        s_wld0 = c.enter_context(nc.semaphore("first_weights_loaded"))
        s_wld = [c.enter_context(nc.semaphore(f"weight_chunk_loaded{i}")) for i in range(RING)]
        s_dbc = [c.enter_context(nc.semaphore(f"decay_rows_loaded{i}")) for i in range(RING)]
        s_done = c.enter_context(nc.semaphore("output_stored"))
        s_settled = c.enter_context(nc.semaphore("waits_settled"))
        s_pz = c.enter_context(nc.semaphore("padding_zeroed"))
        s_ssum = c.enter_context(nc.semaphore("ssq_summed"))
        s_ysum = c.enter_context(nc.semaphore("y_ss_summed"))
        s_mul = c.enter_context(nc.semaphore("branches_multiplied"))
        s_wf = sem("front_weights_split", "pool")
        s_wo = sem("out_weights_split", "pool")
        s_wt = sem("weight_step", "pool")
        s_ws = sem("out_weight_step", "pool")
        s_rn = sem("rnorm_ready", "pool")
        s_E1 = sem("E_incl_ready", "pool")
        s_Eb = sem("E_strict_beta_ready", "pool")
        s_E1b = sem("E_incl_beta_ready", "pool")
        s_kws = sem("k_weighted_step", "pool")
        s_kw = sem("k_weighted_ready", "pool")
        s_Al = sem("A_lo_ready", "pool")
        s_Ml = sem("M_lo_ready", "pool")
        s_yr = sem("y_rms_ready", "pool")
        s_rqk = sem("qk_raw_in_psum", "pe")
        s_rv = sem("v_raw_in_psum", "pe")
        s_z = sem("z_in_psum", "pe")
        s_tqk = sem("qk_tok_in_psum", "pe")
        s_tv = sem("v_tok_in_psum", "pe")
        s_T = sem("qkT_in_psum", "pe")
        s_kk = sem("kk_qk_in_psum", "pe")
        s_P = sem("inv_P_in_psum", "pe")
        s_Z = sem("inv_X_in_psum", "pe")
        s_d0 = sem("first_solve_in_psum", "pe")
        s_rs = sem("residual_in_psum", "pe")
        s_dd = sem("correction_in_psum", "pe")
        s_o = sem("o_in_psum", "pe")
        s_S = sem("state_in_psum", "pe")
        s_KQ = sem("k_q_state_in_psum", "pe")
        s_yT = sem("yT_in_psum", "pe")
        s_out = sem("out_in_psum", "pe")
        s_pqk = sem("qk_padded", "act")
        s_pv = sem("v_padded", "act")
        s_sqk = sem("qk_silu", "act")
        s_sv = sem("v_silu", "act")
        s_sz = sem("z_silu", "act")
        s_sq = sem("qk_squared", "act")
        s_vt = sem("v_tok_copied", "act")
        s_qkh = sem("qk_hi_ready", "act")
        s_Ah = sem("A_hi_ready", "act")
        s_Mh = sem("M_hi_ready", "act")
        s_X = sem("inv_X_copied", "act")
        s_Rh = sem("R_hi_ready", "act")
        s_Dh = sem("D_hi_ready", "act")
        s_Dl = sem("D_lo_ready", "act")
        s_Sh = sem("S_hi_ready", "act")
        s_QS = sem("q_state_ready", "act")
        s_ysq = sem("y_squared", "act")
        s_yh = sem("y_hi_ready", "act")
        s_tap = sem("conv_tap", "dve")
        s_cqk = sem("conv_qk_ready", "dve")
        s_cv = sem("conv_v_ready", "dve")
        s_ssq = sem("ssq_ready", "dve")
        s_qkn = sem("qk_unit_ready", "dve")
        s_qkl = sem("qk_lo_ready", "dve")
        s_qkT = sem("qkT_ready", "dve")
        s_g = sem("gates_ready", "dve")
        s_Es = sem("E_strict_ready", "dve")
        s_A = sem("A_ready", "dve")
        s_M = sem("M_ready", "dve")
        s_nP = sem("neg_P_ready", "dve")
        s_r = sem("residual_ready", "dve")
        s_Sl = sem("S_lo_ready", "dve")
        s_R1 = sem("R1_ready", "dve")
        s_o1 = sem("o_chunk1_ready", "dve")
        s_y = sem("y_ready", "dve")
        s_yss = sem("y_ss_ready", "dve")
        s_yn = sem("y_unit_ready", "dve")
        s_yl = sem("y_lo_ready", "dve")
        s_yTc = sem("yT_ready", "dve")
        s_acc = sem("out_added", "dve")
        s_fin = sem("final_step", "dve")

        def ready(eng, s, n):
            eng.wait_ge(s, n + (1 + C0))

        def spare(eng, s, n, slots=1):
            eng.wait_ge(s, n + (1 + C0 - slots))

        def settle(eng):
            eng.sem_inc(s_settled, 1)

        def start(eng, owner):
            for s in owners[owner]:
                eng.sem_inc(s, C0)

        def at(s, i, u):
            return Step(s, u % RING, i, s // 8, s % 8)

        def drive(eng, step):
            def peeled(s):
                step(*(at(s - d, (s - d) // RING, s - d) if 0 <= s - d < NJ else None for d in range(LAG + 1)))

            for s in range(RING):
                peeled(s)
            with eng.Fori(1, NJ // RING) as i:
                for u in range(RING):
                    step(*(at(3 * i + (u - d), i if u >= d else i - 1, u - d) for d in range(LAG + 1)))
            for s in range(NJ // RING * RING, NJ + LAG):
                peeled(s)

        block = c.enter_context(nc.Block())

        @block.sync
        def _(sp):
            CH = FCH + OCH
            sp.dma_start(wraw[:].rearrange("p (b n) -> p b n", b=8),
                         A["wattn"][0:8].rearrange("b p n -> p b n")).then_inc(s_wld0, 16)
            def step(F, V, B, O):
                if not F:
                    return
                spare(sp, s_Es, F.j, RING)
                settle(sp)
                sp.dma_start(dbc[F.p][:], A["dscr"][ds(F.hk * 2, 2), ds(F.b * T, T)]
                             .partition_broadcast(P)).then_inc(s_dbc[F.p], 16)
                spare(sp, s_wf, F.j + 8, RING)
                settle(sp)
                spare(sp, s_wo, F.j + 8, 8)
                settle(sp)
                sp.dma_start(wraw[:, ds(F.b * CH, CH)],
                             A["wattn"][ds(F.j + 8, 1)].rearrange("b p n -> (b p) n")).then_inc(s_wld[F.p], 16)

            drive(sp, step)
            for t in range(0, NT, 4):
                sp.wait_ge(s_fin, C0 + t // 4 + 1)
                sp.dma_start(A["out"].rearrange("(n p) h -> p n h", p=P)[:, t:t + 4, :], xs[:, t:t + 4, :]).then_inc(s_done, 16)
            sp.wait_ge(s_done, 16 * (NT // 4))

        @block.gpsimd
        def _(pool):
            start(pool, "pool")
            CH = FCH + OCH
            g = nc.gpsimd

            def split_front(q, head, part):
                src = wraw[:, ds(part * CH, FCH)]
                dst = ds(head % 2 * FW + part * FCH, FCH)
                settle(pool)
                g.tensor_copy(wfh[:, dst], src).then_inc(s_wt, 1)
                ready(pool, s_wt, q)
                g.tensor_tensor(wfl[:, dst], src, wfh[:, dst], ALU.subtract).then_inc(s_wf, 1)

            def split_out(q, head, part):
                dst = ds(head % 2 * OW + part * OCH, OCH)
                spare(pool, s_wo, q)
                g.tensor_tensor(wscl[:], wraw[:, ds(part * CH + FCH, OCH)], S["nw"][:, 0:1].to_broadcast([P, OCH]),
                                ALU.mult).then_inc(s_ws, 1)
                ready(pool, s_ws, q * 2)
                settle(pool)
                g.tensor_copy(woh[:, dst], wscl[:]).then_inc(s_ws, 1)
                ready(pool, s_ws, q * 2 + 1)
                g.tensor_tensor(wol[:, dst], wscl[:], woh[:, dst], ALU.subtract).then_inc(s_wo, 1)

            pool.wait_ge(s_wld0, 16)
            for q in range(8):
                split_front(q, 0, q)
            for q in range(8 - LAG):
                split_out(q, 0, q)

            def decays(j, p):
                ready(pool, s_Es, j)
                ready(pool, s_g, j)
                spare(pool, s_M, j)
                spare(pool, s_kws, j * 2, 2)
                g.tensor_tensor(E1[:], Es[:], S["ident4"][:].rearrange("p (u t) -> p u t", u=4), ALU.add).then_inc(s_E1, 1)
                b = beta[:].rearrange("p v c -> p (v c)").unsqueeze(2).to_broadcast([P, 4, P])
                spare(pool, s_A, j)
                g.tensor_tensor(Eb[:], Es[:], b, ALU.mult).then_inc(s_Eb, 1)
                ready(pool, s_E1, j)
                g.tensor_tensor(E1b[:], E1[:], b, ALU.mult).then_inc(s_E1b, 1)

            def unit(j):
                ready(pool, s_ssq, j)
                spare(pool, s_qkn, j)
                g.tensor_tensor(rn[:], ssq[:], S["half"][:], ALU.pow).then_inc(s_rn, 1)

            def weigh_k(j, p):
                ready(pool, s_qkn, j)
                ready(pool, s_E1b, j)
                spare(pool, s_kw, j)
                wend = E1b[:].rearrange("p (v c) t -> p v c t", v=2)[:, :, 0, P - 1:P].to_broadcast([P, 2, P])
                g.tensor_tensor(kw[:], qkn[:, 0:1, :].to_broadcast([P, 2, P]), wend, ALU.mult).then_inc(s_kws, 1)
                ready(pool, s_kws, j * 2)
                spare(pool, s_S, j, RING)
                settle(pool)
                g.tensor_copy(kwh[p][:], kw[:]).then_inc(s_kws, 1)
                ready(pool, s_kws, j * 2 + 1)
                g.tensor_tensor(kwl[p][:], kw[:], kwh[p][:], ALU.subtract).then_inc(s_kw, 1)

            def low_parts(j, p):
                ready(pool, s_Ah, j)
                g.tensor_tensor(Al[p][:], A32[:], Ah[p][:], ALU.subtract).then_inc(s_Al, 1)
                ready(pool, s_Mh, j)
                g.tensor_tensor(Ml[p][:], M32[:], Mh[p][:], ALU.subtract).then_inc(s_Ml, 1)

            def rms(j):
                ready(pool, s_yss, j)
                spare(pool, s_yn, j)
                g.tensor_tensor(yr[:], yss[:], S["half"][:], ALU.pow).then_inc(s_yr, 1)

            def weights(F):
                pool.wait_ge(s_wld[F.p], F.q * 16 + 16)
                spare(pool, s_z, F.hk * 8 + 7, 8)
                split_front(F.j + 8, F.hk + 1, F.b)
                q = F.j + (8 - LAG)
                if not isinstance(q, int) or q // 8 > 1:
                    spare(pool, s_out, q // 8 * 8 + 7, 16)
                split_out(q, q // 8, q % 8)

            def step(F, V, B, O):
                if O:
                    rms(O.j)
                if F:
                    weights(F)
                    decays(F.j, F.p)
                    unit(F.j)
                    weigh_k(F.j, F.p)
                    low_parts(F.j, F.p)

            drive(pool, step)

        @block.scalar
        def _(act):
            start(act, "act")
            a = nc.scalar

            def pad_qk(j):
                ready(act, s_rqk, j)
                spare(act, s_cqk, j)
                a.copy(pad[:, 0:2, 3:T + 3], b_qk[:].rearrange("p (m t) -> p m t", m=2)).then_inc(s_pqk, 1)

            def pad_v(j):
                ready(act, s_rv, j)
                spare(act, s_cv, j)
                a.copy(pad[:, 2:4, 3:T + 3], b_v[:].rearrange("p (m t) -> p m t", m=2)).then_inc(s_pv, 1)

            def silu_z(j, p):
                ready(act, s_z, j)
                spare(act, s_y, j * 2 + 1, 2 * RING)
                a.activation(sz[p][:], b_z[:].rearrange("p (c v t) -> p c v t", c=2, v=2), ACT.Silu).then_inc(s_sz, 1)

            def silu_qk(j):
                ready(act, s_cqk, j)
                spare(act, s_tqk, j)
                a.activation(act4[:, 0:2, :], cv[:, 0:2, :], ACT.Silu).then_inc(s_sqk, 1)

            def silu_v(j):
                ready(act, s_cv, j)
                spare(act, s_tv, j)
                a.activation(act4[:, 2:4, :], cv[:, 2:4, :], ACT.Silu).then_inc(s_sv, 1)

            def squares(j):
                ready(act, s_tqk, j)
                spare(act, s_ssq, j)
                a.activation(sq[:], b_qk4, ACT.Square).then_inc(s_sq, 1)

            def v_tok(j, p):
                ready(act, s_tv, j)
                spare(act, s_R1, j, RING)
                spare(act, s_r, j * 2, 2 * RING)
                a.copy(vtok[p][:].rearrange("p v c t -> p (v c) t"), b_v4).then_inc(s_vt, 1)

            def qk_hi(j):
                ready(act, s_qkn, j)
                spare(act, s_T, j)
                spare(act, s_qkl, j)
                a.copy(qkh[:], qkn[:]).then_inc(s_qkh, 1)

            def A_hi(j, p):
                ready(act, s_A, j)
                spare(act, s_rs, j * 2 + 1, 2 * RING)
                a.copy(Ah[p][:], A32[:]).then_inc(s_Ah, 1)

            def M_hi(j, p):
                ready(act, s_M, j)
                spare(act, s_o, j * 2 + 1, 2 * RING)
                a.copy(Mh[p][:], M32[:]).then_inc(s_Mh, 1)

            def grow(j, p, k):
                n = j * NLEV + k
                ready(act, s_Z, n)
                if k < NLEV - 1:
                    a.copy(XX[(k + 1) % 2][:], b_X[:]).then_inc(s_X, 1)
                else:
                    spare(act, s_dd, j * 2 + 1, 2 * RING)
                    a.copy(XF[p][:], b_X[:, :, 1, :]).then_inc(s_X, 1)

            def right_side(j, p, ch):
                n = j * 2 + ch
                spare(act, s_d0, n)
                if ch == 0:
                    ready(act, s_vt, j)
                    a.copy(Rh[:], vtok[p][:, :, 0, :]).then_inc(s_Rh, 1)
                else:
                    ready(act, s_R1, j)
                    a.copy(Rh[:], R1[:]).then_inc(s_Rh, 1)

            def D_hi(j, ch):
                n = j * 2 + ch
                ready(act, s_d0, n)
                spare(act, s_o, n, 2)
                if ch == 0:
                    spare(act, s_S, j)
                a.copy(Dh[ch][:], b_s4[:, 0:2, :]).then_inc(s_Dh, 1)

            def D_lo(j, ch):
                n = j * 2 + ch
                ready(act, s_dd, n)
                a.copy(Dl[ch][:], b_s4[:, 0:2, :]).then_inc(s_Dl, 1)

            def S_hi(j):
                ready(act, s_S, j)
                spare(act, s_KQ, j)
                a.copy(Sh[:], b_s4[:, 0:2, :]).then_inc(s_Sh, 1)

            def q_state(j, p):
                ready(act, s_KQ, j)
                ready(act, s_R1, j)
                spare(act, s_o1, j)
                a.activation(QS[:, 0, :], b_s4[:, 2, :], ACT.Copy, scale=gin[p][:, 0:1])
                a.activation(QS[:, 1, :], b_s4[:, 3, :], ACT.Copy, scale=gin[p][:, 1:2]).then_inc(s_QS, 1)

            def y_square(j, p):
                ready(act, s_y, j * 2 + 1)
                spare(act, s_yss, j)
                a.activation(ysq[:], y[p][:].rearrange("p c v t -> p (c v) t"), ACT.Square).then_inc(s_ysq, 1)

            def y_hi(j):
                ready(act, s_yn, j)
                spare(act, s_yT, j)
                spare(act, s_yl, j)
                a.copy(yh[:], yn[:]).then_inc(s_yh, 1)

            def step(F, V, B, O):
                if O:
                    y_square(O.j, O.p)
                if B:
                    right_side(B.j, B.p, 0)
                    D_hi(B.j, 0)
                if F:
                    pad_qk(F.j)
                if V:
                    grow(V.j, V.p, 0)
                if F:
                    pad_v(F.j)
                if B:
                    D_lo(B.j, 0)
                if F:
                    silu_z(F.j, F.p)
                if V:
                    grow(V.j, V.p, 1)
                if O:
                    y_hi(O.j)
                if B:
                    S_hi(B.j)
                if F:
                    silu_qk(F.j)
                if V:
                    grow(V.j, V.p, 2)
                if F:
                    silu_v(F.j)
                    squares(F.j)
                if B:
                    q_state(B.j, B.p)
                    right_side(B.j, B.p, 1)
                if F:
                    v_tok(F.j, F.p)
                if V:
                    grow(V.j, V.p, 3)
                if B:
                    D_hi(B.j, 1)
                if F:
                    qk_hi(F.j)
                if V:
                    grow(V.j, V.p, 4)
                if B:
                    D_lo(B.j, 1)
                if V:
                    grow(V.j, V.p, 5)
                if F:
                    A_hi(F.j, F.p)
                    M_hi(F.j, F.p)
                if V:
                    grow(V.j, V.p, 6)

            drive(act, step)

        @block.vector
        def _(dve):
            start(dve, "dve")
            v = nc.vector
            v.memset(pad[:, :, 0:3], 0.0).then_inc(s_pz, 1)
            dve.wait_ge(s_pz, 1)

            def conv(j, hk, half, src, out):
                ready(dve, src, j)
                spare(dve, (s_sqk, s_sv)[half], j)
                for tap in range(3, -1, -1):
                    for m in range(2 * half, 2 * half + 2):
                        n = (3 - tap) * 2 + m % 2 + 7 * half
                        w = S["cw"][:, ds(hk * 16 + (m * 4 + tap), 1)]
                        if tap == 3:
                            ins = v.tensor_scalar(cv[:, m, :], pad[:, m, 3:T + 3], w, None, ALU.mult)
                        else:
                            ready(dve, s_tap, j * 14 + (n - 2))
                            ins = v.scalar_tensor_tensor(cv[:, m, :], pad[:, m, tap:tap + T], w, cv[:, m, :],
                                                         ALU.mult, ALU.add)
                        ins.then_inc(s_tap if (tap, m % 2) != (0, 1) else out, 1)

            def norms(j):
                ready(dve, s_sq, j)
                spare(dve, s_rn, j)
                v.tensor_reduce(ssq[:], sq[:], AX_X, ALU.add).then_inc(s_ssum, 1)
                dve.wait_ge(s_ssum, j + 1)
                v.tensor_scalar(ssq[:], ssq[:], 1e-24, None, ALU.max).then_inc(s_ssq, 1)

            def unit(j):
                ready(dve, s_rn, j)
                spare(dve, s_qkh, j)
                spare(dve, s_kws, j * 2, 2)
                v.tensor_tensor(qkn[:], b_qk4, rn[:].unsqueeze(2).to_broadcast([P, 4, P]), ALU.mult).then_inc(s_qkn, 1)

            def qk_lo(j):
                ready(dve, s_qkh, j)
                spare(dve, s_T, j)
                v.tensor_tensor(qkl[:], qkn[:], qkh[:], ALU.subtract).then_inc(s_qkl, 1)

            def qk_T(j, p):
                ready(dve, s_T, j)
                spare(dve, s_KQ, j, RING)
                v.tensor_copy(qkT[p][:].rearrange("p a c x t -> p (a c x) t"), b_qk16).then_inc(s_qkT, 1)

            def gates(q, j, hk, b, p):
                spare(dve, s_Eb, j)
                spare(dve, s_E1b, j)
                spare(dve, s_QS, j, RING)
                spare(dve, s_R1, j, RING)
                col = S["col"][:].rearrange("p n w -> p (n w)")
                hk2, tile = hk * 2, b * 2
                for ch in range(2):
                    v.tensor_copy(beta[:, :, ch], col[:, ds((tile + ch) * 64 + (hk2 + 32), 2)])
                v.tensor_copy(gin[p][:], col[:, ds((tile + 1) * 64 + hk2, 2)])
                v.tensor_copy(ngin[p][:], S["ngin"][:].rearrange("p n w -> p (n w)")[:, ds((tile + 1) * 32 + hk2, 2)]).then_inc(s_g, 1)
                dve.wait_ge(s_dbc[p], q * 16 + 16)
                spare(dve, s_E1, j)
                v.tensor_tensor_scan(Es[:].rearrange("p u t -> p (u t)"), S["inj"][:],
                                     dbc[p][:].rearrange("p v t -> p (v t)"), 0.0, ALU.add, ALU.mult).then_inc(s_Es, 1)

            def matrix_A(j):
                kk = b_v[:].rearrange("p (c x t) -> p c x t", c=2, x=2)
                four = lambda m: m[:].rearrange("p (v c) t -> p v c t", v=2)
                ready(dve, s_kk, j)
                ready(dve, s_Eb, j)
                spare(dve, s_Al, j)
                for w in range(2):
                    ins = v.tensor_tensor(four(A32)[:, w], kk[:, :, 0, :], four(Eb)[:, w], ALU.mult)
                ins.then_inc(s_A, 1)

            def matrix_M(j):
                kk = b_v[:].rearrange("p (c x t) -> p c x t", c=2, x=2)
                four = lambda m: m[:].rearrange("p (v c) t -> p v c t", v=2)
                ready(dve, s_E1b, j)
                spare(dve, s_Ml, j)
                for w in range(2):
                    ins = v.tensor_tensor(four(M32)[:, w], kk[:, :, 1, :], four(E1b)[:, w], ALU.mult)
                ins.then_inc(s_M, 1)

            def mask(j, k):
                n = j * NLEV + k
                ready(dve, s_P, n)
                spare(dve, s_Z, n)
                v.tensor_tensor(nP[:], b_P4, S["nmask"][:, k, :].unsqueeze(1).to_broadcast([P, 4, P]),
                                ALU.mult).then_inc(s_nP, 1)

            def residual(j, p, ch):
                n = j * 2 + ch
                ready(dve, s_rs, n)
                spare(dve, s_dd, n)
                v.tensor_tensor(rh[:], vtok[p][:, :, 0, :] if ch == 0 else R1[:], b_s4[:, 0:2, :],
                                ALU.subtract).then_inc(s_r, 1)

            def S_lo(j):
                ready(dve, s_Sh, j)
                spare(dve, s_KQ, j)
                v.tensor_tensor(Sl[:], b_s4[:, 0:2, :], Sh[:], ALU.subtract).then_inc(s_Sl, 1)

            def right_side_1(j, p):
                ready(dve, s_KQ, j)
                spare(dve, s_r, j * 2 + 1, 2)
                spare(dve, s_Rh, j * 2 + 1, 2)
                for w in range(2):
                    ins = v.scalar_tensor_tensor(R1[:, w, :], b_s4[:, w, :], ngin[p][:, w:w + 1], vtok[p][:, w, 1, :],
                                                 ALU.mult, ALU.add)
                ins.then_inc(s_R1, 1)

            def gated(j, p, ch):
                ready(dve, s_o, j * 2 + ch)
                ready(dve, s_sz, j)
                spare(dve, s_yn, j, RING)
                spare(dve, s_ysq, j, RING)
                o = b_o4[:, ch]
                if ch:
                    ready(dve, s_QS, j)
                    v.tensor_tensor(o1[:], o, QS[:], ALU.add).then_inc(s_o1, 1)
                    ready(dve, s_o1, j)
                    o = o1[:]
                v.tensor_tensor(y[p][:, ch], o, sz[p][:, ch], ALU.mult).then_inc(s_y, 1)

            def y_norm(j):
                ready(dve, s_ysq, j)
                spare(dve, s_yr, j)
                v.tensor_reduce(yss[:], ysq[:], AX_X, ALU.add).then_inc(s_ysum, 1)
                dve.wait_ge(s_ysum, j + 1)
                v.tensor_scalar(yss[:], yss[:], 1.0 / P, 1e-6, ALU.mult, ALU.add).then_inc(s_yss, 1)

            def y_unit(j, p):
                ready(dve, s_yr, j)
                spare(dve, s_yh, j)
                v.tensor_tensor(yn[:], y[p][:].rearrange("p c v t -> p (c v) t"),
                                yr[:].unsqueeze(2).to_broadcast([P, 4, P]), ALU.mult).then_inc(s_yn, 1)

            def y_lo(j):
                ready(dve, s_yh, j)
                spare(dve, s_yT, j)
                v.tensor_tensor(yl[:], yn[:], yh[:], ALU.subtract).then_inc(s_yl, 1)

            def y_T(j):
                ready(dve, s_yT, j)
                spare(dve, s_out, j)
                v.tensor_copy(yT[:].rearrange("p a u t -> p (a u) t"), b_o16).then_inc(s_yTc, 1)

            def add(j, b):
                ready(dve, s_out, j)
                spare(dve, s_acc, j)
                dst = acca[:].rearrange("p n h -> p (n h)")[:, ds(b * 2 * H, 2 * H)]
                v.tensor_tensor(dst, dst, b_z[:], ALU.add).then_inc(s_acc, 1)

            def step(F, V, B, O):
                if V:
                    mask(V.j, 0)
                if O:
                    y_norm(O.j)
                if B:
                    residual(B.j, B.p, 0)
                if O:
                    y_unit(O.j, O.p)
                if F:
                    conv(F.j, F.hk, 0, s_pqk, s_cqk)
                if V:
                    mask(V.j, 1)
                if B:
                    gated(B.j, B.p, 0)
                if O:
                    y_lo(O.j)
                if V:
                    mask(V.j, 2)
                if B:
                    S_lo(B.j)
                if F:
                    conv(F.j, F.hk, 1, s_pv, s_cv)
                if B:
                    right_side_1(B.j, B.p)
                if V:
                    mask(V.j, 3)
                if F:
                    gates(F.q, F.j, F.hk, F.b, F.p)
                    norms(F.j)
                if O:
                    y_T(O.j)
                if B:
                    residual(B.j, B.p, 1)
                if V:
                    mask(V.j, 4)
                if F:
                    unit(F.j)
                    qk_lo(F.j)
                if V:
                    mask(V.j, 5)
                if O:
                    add(O.j, O.b)
                if F:
                    qk_T(F.j, F.p)
                    matrix_A(F.j)
                if V:
                    mask(V.j, 6)
                if F:
                    matrix_M(F.j)
                if B:
                    gated(B.j, B.p, 1)

            drive(dve, step)
            ready(dve, s_acc, NJ - 1)
            for t in range(0, NT, 4):
                v.tensor_tensor(acca[:, t:t + 4, :], acca[:, t:t + 4, :], accf[:, t:t + 4, :], ALU.mult).then_inc(s_mul, 1)
                dve.wait_ge(s_mul, t // 4 + 1)
                v.tensor_tensor(xs[:, t:t + 4, :], xs[:, t:t + 4, :], acca[:, t:t + 4, :], ALU.add).then_inc(s_fin, 1)

        @block.tensor
        def _(pe):
            start(pe, "pe")
            mm = nc.tensor.matmul

            def block_of(out, hk, b, m):
                for n, (w, x) in enumerate(((wfh, xh), (wfl, xh), (wfh, xl))):
                    for k in range(KH):
                        last = mm(out, w[:, ds(hk % 2 * FW + k * 768 + m * P, P)], x[:, k, ds(b * T, T)],
                                  start=(n == 0 and k == 0), stop=(n == 2 and k == KH - 1))
                return last

            def project_qk(j, hk, b):
                pe.wait_ge(s_wf, hk * 8 + (8 + C0))
                spare(pe, s_qkT, j)
                block_of(b_qk[:, 0:T], hk, b, 0)
                block_of(b_qk[:, T:2 * T], hk, b, 1).then_inc(s_rqk, 1)

            def project_v(j, hk, b):
                spare(pe, s_A, j)
                spare(pe, s_M, j)
                block_of(b_v[:, 0:T], hk, b, 2)
                block_of(b_v[:, T:2 * T], hk, b, 3).then_inc(s_rv, 1)

            def project_z(j, hk, b):
                base, tok = hk % 2 * FW, b * T
                spare(pe, s_acc, j, LAG + 1)
                for t in range(2):
                    for n, (w, x) in enumerate(((wfh, xh), (wfl, xh), (wfh, xl))):
                        for k in range(KH):
                            last = mm(b_z[:, t * H:(t + 1) * H], x[:, k, ds(tok + t * P, P)], w[:, ds(base + k * 768 + 512, H)],
                                      start=(n == 0 and k == 0), stop=(n == 2 and k == KH - 1))
                last.then_inc(s_z, 1)

            def qk_to_tokens(j):
                ready(pe, s_sqk, j)
                ready(pe, s_pqk, j)
                for n, (m, ch) in enumerate(((1, 0), (1, 1), (0, 0), (0, 1))):
                    last = nc.tensor.transpose(b_qk4[:, n, :], act4[:, m, ch * P:(ch + 1) * P], ident[:])
                last.then_inc(s_tqk, 1)

            def v_to_tokens(j):
                ready(pe, s_sv, j)
                ready(pe, s_pv, j)
                for w in range(2):
                    for ch in range(2):
                        last = nc.tensor.transpose(b_v4[:, 2 * w + ch, :], act4[:, 2 + w, ch * P:(ch + 1) * P], ident[:])
                last.then_inc(s_tv, 1)

            def to_channels(j):
                ready(pe, s_qkl, j)
                for a, src in enumerate((qkh, qkl)):
                    for ch in range(2):
                        for x in range(2):
                            last = nc.tensor.transpose(b_qk16[:, a * 4 + ch * 2 + x, :], src[:, 2 * x + ch, :], id16[:, 0:P])
                last.then_inc(s_T, 1)

            def similarities(j, p):
                ready(pe, s_qkT, j)
                ready(pe, s_vt, j)
                for ch in range(2):
                    for n, (a, b) in enumerate(((0, 0), (0, 1), (1, 0))):
                        last = mm(b_v[:, ch * 2 * P:(ch + 1) * 2 * P], qkT[p][:, a, ch, 0, :],
                                  qkT[p][:, b, ch].rearrange("p x t -> p (x t)"), start=(n == 0), stop=(n == 2))
                last.then_inc(s_kk, 1)

            def level_P(j, p, k):
                n = j * NLEV + k
                if k == 0:
                    ready(pe, s_Ah, j)
                else:
                    ready(pe, s_X, n - 1)
                spare(pe, s_nP, n)
                for w in range(4):
                    last = mm(b_P4[:, w, :], Ah[p][:, w, :], XX[k % 2][:, w, 0, :] if k else id16[:, 0:P],
                              start=True, stop=True)
                last.then_inc(s_P, 1)

            def level_X(j, p, k):
                n = j * NLEV + k
                ready(pe, s_nP, n)
                spare(pe, s_X, n)
                X = XX[k % 2]
                for w in range(4):
                    xt = X[:, w, 1, :] if k else id16[:, 0:P]
                    both = X[:, w].rearrange("p a t -> p (a t)") if k else id16[:, 0:2 * P]
                    if k < NLEV - 1:
                        mm(b_X[:, w].rearrange("p a t -> p (a t)"), id16[:, 0:P], both, start=True, stop=False,
                           skip_group_check=True)
                        mm(b_X[:, w, 0, :], xt, nP[:, w, :], start=False, stop=False, skip_group_check=True)
                    else:
                        mm(b_X[:, w, 1, :], id16[:, 0:P], xt, start=True, stop=False, skip_group_check=True)
                    last = mm(b_X[:, w, 1, :], nP[:, w, :], xt, start=False, stop=True, skip_group_check=True)
                last.then_inc(s_Z, 1)

            def unit(ch, w):
                return 2 * w + ch

            def solve(j, p, ch):
                n = j * 2 + ch
                ready(pe, s_Rh, n)
                if ch == 0:
                    ready(pe, s_X, j * NLEV + NLEV - 1)
                    spare(pe, s_Dl, n)
                else:
                    ready(pe, s_QS, j)
                for w in range(2):
                    last = mm(b_s4[:, w, :], XF[p][:, unit(ch, w), :], Rh[:, w, :], start=True, stop=True)
                last.then_inc(s_d0, 1)

            def residual(j, p, ch):
                n = j * 2 + ch
                ready(pe, s_Dh, n)
                ready(pe, s_Al, j)
                for w in range(2):
                    for m, lhs in enumerate((id16[:, 0:P], Ah[p][:, unit(ch, w), :], Al[p][:, unit(ch, w), :])):
                        last = mm(b_s4[:, w, :], lhs, Dh[ch][:, w, :], start=(m == 0), stop=(m == 2))
                last.then_inc(s_rs, 1)

            def correct(j, p, ch):
                n = j * 2 + ch
                ready(pe, s_r, n)
                for w in range(2):
                    last = mm(b_s4[:, w, :], XF[p][:, unit(ch, w), :], rh[:, w, :], start=True, stop=True)
                last.then_inc(s_dd, 1)

            def outputs(j, p, ch):
                n = j * 2 + ch
                ready(pe, s_Dl, n)
                ready(pe, s_Ml, j)
                if ch == 0:
                    spare(pe, s_y, n)
                else:
                    spare(pe, s_yTc, j)
                    ready(pe, s_y, n - 1)
                for w in range(2):
                    for m, (a, d) in enumerate(((Mh, Dh), (Ml, Dh), (Mh, Dl))):
                        last = mm(b_o4[:, ch, w, :], a[p][:, unit(ch, w), :], d[ch][:, w, :], start=(m == 0), stop=(m == 2))
                last.then_inc(s_o, 1)

            def state(j, p):
                ready(pe, s_kw, j)
                for w in range(2):
                    for m, (a, d) in enumerate(((kwh, Dh), (kwl, Dh), (kwh, Dl))):
                        last = mm(b_s4[:, w, :], a[p][:, w, :], d[0][:, w, :], start=(m == 0), stop=(m == 2))
                last.then_inc(s_S, 1)

            def on_state(j, p):
                ready(pe, s_Sl, j)
                for x in range(2):
                    for m, (a, d) in enumerate(((0, Sh), (0, Sl), (1, Sh))):
                        last = mm(b_s[:, x * 2 * P:(x + 1) * 2 * P], qkT[p][:, a, 1, x, :],
                                  d[:].rearrange("p v t -> p (v t)"), start=(m == 0), stop=(m == 2))
                last.then_inc(s_KQ, 1)

            def y_T(j):
                ready(pe, s_yl, j)
                if isinstance(j, int) and j == NJ - 1:
                    ready(pe, s_y, 2 * NJ - 1)
                else:
                    ready(pe, s_y, j * 2 + 2)
                for a, src in enumerate((yh, yl)):
                    for w in range(4):
                        last = nc.tensor.transpose(b_o16[:, a * 4 + w, :], src[:, w, :], id16[:, 0:P])
                last.then_inc(s_yT, 1)

            def out(j, hk):
                ready(pe, s_yTc, j)
                ready(pe, s_sz, min(j + LAG, NJ - 1) if isinstance(j, int) else j + LAG)
                pe.wait_ge(s_wo, hk * 8 + (8 + C0))
                base = hk % 2 * OW
                for ch in range(2):
                    for w in range(2):
                        for m, (a, wt) in enumerate(((0, woh), (0, wol), (1, woh))):
                            last = mm(b_z[:, ch * H:(ch + 1) * H], yT[:, a, 2 * ch + w, :], wt[:, ds(base + w * H, H)],
                                      start=(w == 0 and m == 0), stop=(w == 1 and m == 2))
                last.then_inc(s_out, 1)

            def step(F, V, B, O):
                if V:
                    level_P(V.j, V.p, 0)
                if B:
                    solve(B.j, B.p, 0)
                if F:
                    project_qk(F.j, F.hk, F.b)
                if V:
                    level_X(V.j, V.p, 0)
                if B:
                    residual(B.j, B.p, 0)
                if F:
                    project_v(F.j, F.hk, F.b)
                if V:
                    level_P(V.j, V.p, 1)
                if B:
                    correct(B.j, B.p, 0)
                if F:
                    project_z(F.j, F.hk, F.b)
                if V:
                    level_X(V.j, V.p, 1)
                if B:
                    outputs(B.j, B.p, 0)
                    state(B.j, B.p)
                if V:
                    level_P(V.j, V.p, 2)
                if F:
                    qk_to_tokens(F.j)
                if V:
                    level_X(V.j, V.p, 2)
                if B:
                    on_state(B.j, B.p)
                if O:
                    y_T(O.j)
                if V:
                    level_P(V.j, V.p, 3)
                if F:
                    v_to_tokens(F.j)
                if V:
                    level_X(V.j, V.p, 3)
                if B:
                    solve(B.j, B.p, 1)
                if V:
                    level_P(V.j, V.p, 4)
                if B:
                    residual(B.j, B.p, 1)
                if O:
                    out(O.j, O.hk)
                if V:
                    level_X(V.j, V.p, 4)
                if F:
                    to_channels(F.j)
                if V:
                    level_P(V.j, V.p, 5)
                if B:
                    correct(B.j, B.p, 1)
                if V:
                    level_X(V.j, V.p, 5)
                if F:
                    similarities(F.j, F.p)
                if V:
                    level_P(V.j, V.p, 6)
                if B:
                    outputs(B.j, B.p, 1)
                if V:
                    level_X(V.j, V.p, 6)

            drive(pe, step)


def build(nc, A, NB, NHK):
    NT, N = NB * 2, NB * T
    with ExitStack() as c:
        def sb(name, shape, dt=F32):
            return c.enter_context(nc.sbuf_tensor(name, shape, dt))

        S = {
            "xs": sb("x_tok", [P, NT, H]),
            "xh": sb("xT_hi", [P, KH, N], F16),
            "xl": sb("xT_lo", [P, KH, N], F16),
            "accf": sb("ffn_sum", [P, NT, H]),
            "acca": sb("attn_sum", [P, NT, H]),
            "ident": sb("identity", [P, P]),
            "ident4": sb("identity4", [P, 4 * P]),
            "id16": sb("identity4_16", [P, 4 * P], F16),
            "inj": sb("scan_starts", [P, 4 * P]),
            "nmask32": sb("level_masks32", [P, NLEV, P]),
            "nmask": sb("level_masks", [P, NLEV, P], F16),
            "cw": sb("conv_w", [P, NHK * 16]),
            "nw": sb("norm_w", [P, 1]),
            "b1": sb("b1", [P, NE * IC]),
            "half": sb("minus_half", [P, 4]),
            "tiny": sb("tiny", [P, 4]),
            "col": sb("gin_beta_cols", [P, NT, 64]),
            "ngin": sb("neg_gin_cols", [P, NT, 32]),
            "gate": sb("gate", [P, NT, NE]),
            "gc": sb("gate_and_bias_weight", [P, NT, 2 * NE]),
        }
        setup_phase(nc, c, A, S, NB, NHK)
        ffn_phase(nc, A, S, NB, NHK)
        attention_phase(nc, A, S, NB, NHK)


def shape_constants():
    t = np.arange(P)
    ident = np.eye(P, dtype=np.float32)
    ident4 = np.tile(ident, (1, 4))
    starts = np.tile(np.eye(P, k=1, dtype=np.float32), (1, 4))
    masks = np.zeros((P, NLEV, P), np.float32)
    for k in range(NLEV):
        b = t >> k
        masks[:, k, :] = -((b[:, None] % 2 == 1) & (b[None, :] == b[:, None] - 1)).astype(np.float32)
    rank = np.tile(np.arange(NE, 0, -1, dtype=np.float32), (P, 1))
    return {"ident": ident, "ident4": ident4, "inj": starts, "nmask": masks, "rank": rank}


def kernel(L0_attn_x, L0_attn_W_qkv, L0_attn_W_z, L0_attn_W_b, L0_attn_W_a, L0_attn_conv_w, L0_attn_dt_bias,
           L0_attn_A_log, L0_attn_norm_w, L0_attn_W_out, L0_ffn_rw1, L0_ffn_rw2, L0_ffn_w1, L0_ffn_b1, L0_ffn_w2,
           L0_ffn_b2):
    import numpy as np
    import concourse.bacc as bacc
    from concourse.bass_utils import run_bass_kernel_spmd

    g = lambda a: np.asarray(a)
    x = g(L0_attn_x)
    NB = x.shape[0]
    wqkv, wz, wout = g(L0_attn_W_qkv), g(L0_attn_W_z), g(L0_attn_W_out)
    NHK = wz.shape[0] // 256
    K = NHK * P
    q, k, v = wqkv[:K].reshape(NHK, P, H), wqkv[K:2 * K].reshape(NHK, P, H), wqkv[2 * K:].reshape(NHK, 2 * P, H)
    front = np.concatenate([q, k, v, wz.reshape(NHK, 2 * P, H)], axis=1)
    front = front.reshape(NHK, 768, KH, P).transpose(0, 3, 2, 1).reshape(NHK, P, FW)
    outw = wout.T.reshape(NHK, 2, P, H).transpose(0, 2, 1, 3).reshape(NHK, P, OW)
    chunks = np.concatenate([front.reshape(NHK, P, 8, FCH), outw.reshape(NHK, P, 8, OCH)], axis=3)
    chunks = chunks.transpose(0, 2, 1, 3).reshape(NHK * 8, P, FCH + OCH)
    wattn = np.concatenate([chunks, np.zeros((8, P, FCH + OCH), np.float32)], axis=0)
    cw = g(L0_attn_conv_w)[:, 0, :]
    cw = np.stack([cw[:K].reshape(NHK, P, 4), cw[K:2 * K].reshape(NHK, P, 4),
                   cw[2 * K:].reshape(NHK, 2, P, 4)[:, 0], cw[2 * K:].reshape(NHK, 2, P, 4)[:, 1]], axis=1)
    cw = cw.transpose(2, 0, 1, 3).reshape(P, NHK * 16)

    def col32(a):
        out = np.zeros((32, 1), np.float32)
        out[:a.shape[0], 0] = a
        return out

    def rows32(w):
        out = np.zeros((32, H), np.float32)
        out[:w.shape[0]] = w
        return out

    wab = np.concatenate([rows32(g(L0_attn_W_a)), rows32(g(L0_attn_W_b))], axis=0).reshape(64, KH, P).transpose(2, 1, 0)
    w1 = g(L0_ffn_w1).reshape(NE, KH, P, I).transpose(0, 2, 1, 3).reshape(NE, P, KH * I)
    w2 = g(L0_ffn_w2).reshape(NE, IC, P, H).transpose(0, 2, 1, 3).reshape(NE, P, IC * H)
    arrays = {
        "x": x.reshape(NB * T, H),
        "wattn": wattn,
        "wffn": np.concatenate([w1, w2], axis=2),
        "cw": cw,
        "wab": wab,
        "dtb": col32(g(L0_attn_dt_bias)),
        "alog": col32(g(L0_attn_A_log)),
        "nw": g(L0_attn_norm_w).reshape(P, 1),
        "rw1": g(L0_ffn_rw1).reshape(KH, P, P).transpose(1, 0, 2),
        "rw2": g(L0_ffn_rw2),
        "b1": g(L0_ffn_b1).reshape(NE, IC, P).transpose(2, 0, 1).reshape(P, NE * IC),
        "b2": g(L0_ffn_b2),
        **shape_constants(),
    }
    arrays = {f"in_{n}": np.ascontiguousarray(a) for n, a in arrays.items()}
    nc = bacc.Bacc("TRN2", target_bir_lowering=False, num_devices=1)
    A = {n[3:]: nc.dram_tensor(n, a.shape, mybir.dt.from_np(a.dtype), kind="ExternalInput").ap() for n, a in arrays.items()}
    A["dscr"] = nc.dram_tensor("decay_scratch", (2 * NHK, NB * T), F32, kind="Internal").ap()
    A["cgscr"] = nc.dram_tensor("bias_only_scratch", (NE, H), F32, kind="Internal").ap()
    A["out"] = nc.dram_tensor("out", (NB * T, H), F32, kind="ExternalOutput").ap()
    build(nc, A, NB, NHK)
    r = run_bass_kernel_spmd(nc, [arrays], core_ids=[0])
    return r.results[0]["out"].reshape(NB, T, H)
```

```python
from collections import namedtuple
from contextlib import ExitStack

import numpy as np

import concourse.bass as bass
from concourse import mybir

F32 = mybir.dt.float32
F16 = mybir.dt.float16
ALU = mybir.AluOpType
ACT = mybir.ActivationFunctionType
AX_X = mybir.AxisListType.X
ds = bass.ds

P = 128
H = 256
KH = H // P
T = 256
NE = 8
I = 1024
IC = I // P
G = 512
NLEV = 7
FW = KH * 768
OW = 2 * H
FCH = FW // 8
OCH = OW // 8
RING = 3
LAG = 4
OLAG = 3


Step = namedtuple("Step", "j p q hk b")


def setup_phase(nc, ctx, A, S, NB, NHK):
    NT = NB * 2
    N = NB * T
    NG = N // G
    NV = 2 * NHK
    W2 = 64

    with ExitStack() as c:
        def sb(name, shape, dt=F32):
            return c.enter_context(nc.sbuf_tensor(name, shape, dt))

        def sem(name):
            return c.enter_context(nc.semaphore(name))

        stats = sb("ln_stats", [P, NT, 6])
        mv = sb("ln_mean_var", [P, NT, 2])
        rstd = sb("ln_rstd", [P, NT])
        std = sb("ln_std", [P, NT])
        xn = sb("xn", [P, NT, H])
        wab = sb("wab", [P, KH, W2])
        wabh = sb("wabh", [P, KH, W2], F16)
        wabl = sb("wabl", [P, KH, W2], F16)
        rw1 = sb("rw1", [P, KH, P])
        rw1h = sb("rw1h", [P, KH, P], F16)
        rw1l = sb("rw1l", [P, KH, P], F16)
        rw2 = sb("rw2", [P, NE])
        dtb = sb("dtb", [32, 1])
        alog = sb("alog", [32, 1])
        expa = sb("expa", [32, 1])
        nega = sb("nega", [32, 1])
        eps = sb("eps", [P, 1])
        ab = sb("ab", [W2, N])
        zrow = sb("zrow", [32, N])
        erow = sb("erow", [W2, N])
        drow = sb("drow", [32, N])
        dcut = sb("dcut", [32, N])
        gb = sb("gin_beta", [W2, N])
        h1 = sb("h1", [P, N])
        lg = sb("lg", [P, NT, NE])
        pr = sb("pr", [P, NT, NE])
        t0 = sb("t0", [P, NT, NE])
        m0 = sb("m0", [P, NT, NE])
        m1 = sb("m1", [P, NT, NE])
        red = sb("red", [P, NT])
        w0 = sb("w0", [P, NT])
        w1 = sb("w1", [P, NT])
        cnt = sb("cnt", [P, 2 * NE])
        actv = sb("actv", [P, 2 * NE])
        ones = sb("ones", [P, P])
        rank = sb("rank", [P, NE])

        s_x = sem("x_loaded")
        s_c = sem("small_inputs_loaded")
        s_v = sem("vector_step")
        s_a = sem("scalar_step")
        s_p = sem("pool_step")
        s_tr = sem("xn_transposed")
        s_xh = sem("xn_hi_written")
        s_xl = sem("xn_lo_written")
        s_xn = sem("xn_ready")
        s_ab = sem("ab_ready")
        s_abc = sem("ab_copied")
        s_h1 = sem("h1_ready")
        s_h1c = sem("h1_copied")
        s_lg = sem("logits_ready")
        s_gt = sem("gin_beta_transposed")
        s_cnt = sem("counts_summed")
        s_ct = sem("gates_transposed")
        s_st = sem("decay_stored")

        pt = [c.enter_context(nc.psum_tensor(f"tr{i}", [P, 2, KH, P], F32)) for i in range(2)]
        pab = [c.enter_context(nc.psum_tensor(f"ab_ps{i}", [P, G], F32)) for i in range(2)]
        plg = c.enter_context(nc.psum_tensor("lg_ps", [P, NT, NE], F32))
        pgt = c.enter_context(nc.psum_tensor("gt_ps", [P, 2, 8, W2], F32))
        pct = c.enter_context(nc.psum_tensor("ct_ps", [P, 512], F32))

        xs, xh, xl, ident, ident4 = S["xs"], S["xh"], S["xl"], S["ident"], S["ident4"]
        NSMALL = 13
        block = c.enter_context(nc.Block())

        @block.sync
        def _(sp):
            for t in range(0, NT, 4):
                k = min(4, NT - t)
                sp.dma_start(xs[:, t:t + k, :], A["x"].rearrange("(n p) h -> p n h", p=P)[:, t:t + k, :]).then_inc(s_x, 16)
            for dst, src in ((wab, "wab"), (rw1, "rw1"), (rw2, "rw2"), (dtb, "dtb"), (alog, "alog"),
                             (ident, "ident"), (ident4, "ident4"), (S["inj"], "inj"), (S["nmask32"], "nmask"),
                             (S["cw"], "cw"), (S["nw"], "nw"), (S["b1"], "b1"), (rank, "rank")):
                sp.dma_start(dst[:], A[src]).then_inc(s_c, 16)
            sp.wait_ge(s_v, 16)
            sp.dma_start(A["dscr"], dcut[0:NV, :]).then_inc(s_st, 16)
            sp.wait_ge(s_st, 16)

        @block.gpsimd
        def _(pool):
            nc.gpsimd.memset(ones[:], 1.0).then_inc(s_p, 1)
            nc.gpsimd.memset(S["half"][:], -0.5).then_inc(s_p, 1)
            nc.gpsimd.memset(S["tiny"][:], 1e-24).then_inc(s_p, 1)
            nc.gpsimd.memset(eps[:], 1e-5).then_inc(s_p, 1)

        @block.scalar
        def _(act):
            act.wait_ge(s_v, 1)
            act.wait_ge(s_p, 4)
            nc.scalar.activation(std[:], mv[:, :, 1], ACT.Sqrt, bias=eps[:, 0:1]).then_inc(s_a, 1)
            for i in range(NT // 2):
                act.wait_ge(s_tr, i + 1)
                nc.scalar.copy(xh[:, :, 2 * i * P:(2 * i + 2) * P].rearrange("p k (t c) -> p t k c", t=2),
                               pt[i % 2][:]).then_inc(s_xh, 1)
            for i in range(NG):
                act.wait_ge(s_ab, i + 1)
                nc.scalar.copy(ab[:, i * G:(i + 1) * G], pab[i % 2][0:W2, :]).then_inc(s_abc, 1)
            act.wait_ge(s_c, 16 * NSMALL)
            nc.scalar.activation(expa[:], alog[:], ACT.Exp).then_inc(s_a, 1)
            act.wait_ge(s_v, 5)
            nc.scalar.activation(erow[0:32, :], zrow[:], ACT.Abs).then_inc(s_a, 1)
            act.wait_ge(s_a, 3)
            nc.scalar.activation(erow[0:32, :], erow[0:32, :], ACT.Exp, scale=-1.0).then_inc(s_a, 1)
            act.wait_ge(s_abc, NG)
            nc.scalar.activation(erow[32:64, :], ab[32:64, :], ACT.Exp, scale=-1.0).then_inc(s_a, 1)
            act.wait_ge(s_a, 4)
            nc.scalar.activation(drow[:], erow[0:32, :], ACT.Ln, bias=1.0).then_inc(s_a, 1)
            act.wait_ge(s_v, 9)
            nc.scalar.activation(drow[:], drow[:], ACT.Exp, scale=nega[:, 0:1]).then_inc(s_a, 1)
            for i in range(NG):
                act.wait_ge(s_h1, i + 1)
                nc.scalar.activation(h1[:, i * G:(i + 1) * G], pab[i % 2][:], ACT.Gelu).then_inc(s_h1c, 1)
            act.wait_ge(s_v, 21)
            nc.scalar.activation(t0[:], t0[:], ACT.Exp).then_inc(s_a, 1)

        @block.vector
        def _(dve):
            n = [0]

            def step(ins):
                n[0] += 1
                ins.then_inc(s_v, 1)
                dve.wait_ge(s_v, n[0])

            v = nc.vector
            dve.wait_ge(s_x, 16 * ((NT + 3) // 4))
            for t in range(NT):
                last = v.bn_stats(stats[:, t, :], xs[:, t, :])
            last.then_inc(s_xn, 1)
            dve.wait_ge(s_xn, 1)
            for t in range(NT):
                last = v.bn_aggr(mv[:, t, :], stats[:, t, :])
            step(last)
            dve.wait_ge(s_a, 1)
            step(v.reciprocal(rstd[:], std[:]))
            for t in range(NT):
                v.tensor_scalar(xn[:, t, :], xs[:, t, :], mv[:, t, 0:1], rstd[:, t:t + 1],
                                ALU.subtract, ALU.mult).then_inc(s_xn, 1)
            dve.wait_ge(s_c, 16 * NSMALL)
            v.tensor_copy(wabh[:], wab[:])
            v.tensor_copy(rw1h[:], rw1[:])
            v.tensor_copy(S["id16"][:], ident4[:])
            step(v.tensor_copy(S["nmask"][:], S["nmask32"][:]))
            v.tensor_tensor(wabl[:], wab[:], wabh[:], ALU.subtract)
            step(v.tensor_tensor(rw1l[:], rw1[:], rw1h[:], ALU.subtract))
            for i in range(NT // 2):
                dve.wait_ge(s_xh, i + 1)
                v.tensor_tensor(xl[:, :, 2 * i * P:(2 * i + 2) * P].rearrange("p k (t c) -> p t k c", t=2),
                                pt[i % 2][:],
                                xh[:, :, 2 * i * P:(2 * i + 2) * P].rearrange("p k (t c) -> p t k c", t=2),
                                ALU.subtract).then_inc(s_xl, 1)
            dve.wait_ge(s_abc, NG)
            step(v.tensor_scalar(zrow[:], ab[0:32, :], dtb[:, 0:1], None, ALU.add))
            dve.wait_ge(s_a, 6)
            step(v.tensor_scalar(erow[32:64, :], erow[32:64, :], 1.0, None, ALU.add))
            step(v.reciprocal(gb[32:64, :], erow[32:64, :]))
            step(v.tensor_scalar(nega[:], expa[:], -1.0, None, ALU.mult))
            step(v.scalar_tensor_tensor(drow[:], zrow[:], 0.0, drow[:], ALU.max, ALU.add))
            dve.wait_ge(s_a, 7)
            first = lambda a: a[:].rearrange("p (n t) -> p n t", t=P)[:, :, 0:1]
            step(v.tensor_copy(dcut[:], drow[:]))
            step(v.memset(zrow[:], 0.0))
            step(v.tensor_copy(first(zrow), first(drow)))
            step(v.memset(first(dcut), 0.0))
            step(v.tensor_tensor_scan(gb[0:32, :], dcut[:], zrow[:], 0.0, ALU.mult, ALU.add))
            step(v.memset(cnt[:], 0.0))
            step(v.memset(S["accf"][:], 0.0))
            for q in range((NT + 7) // 8):
                k = min(8, NT - 8 * q)
                dve.wait_ge(s_gt, q + 1)
                v.tensor_copy(S["col"][:, 8 * q:8 * q + k, :], pgt[:, q, 0:k, :])
            step(v.memset(S["acca"][:], 0.0))
            step(v.tensor_scalar(S["ngin"][:], S["col"][:, :, 0:32], -1.0, None, ALU.mult))
            dve.wait_ge(s_lg, 1)
            bc = lambda a: a[:].unsqueeze(2).to_broadcast([P, NT, NE])
            rk = rank[:].unsqueeze(1).to_broadcast([P, NT, NE])
            step(v.tensor_copy(lg[:], plg[:]))
            step(v.tensor_reduce(red[:], lg[:], AX_X, ALU.max))
            step(v.tensor_tensor(t0[:], lg[:], bc(red), ALU.subtract))
            dve.wait_ge(s_a, 8)
            step(v.tensor_reduce(red[:], t0[:], AX_X, ALU.add))
            step(v.reciprocal(red[:], red[:]))
            step(v.tensor_tensor(pr[:], t0[:], bc(red), ALU.mult))
            for m, w in ((m0, w0), (m1, w1)):
                step(v.tensor_reduce(w[:], pr[:], AX_X, ALU.max))
                step(v.tensor_tensor(m[:], pr[:], bc(w), ALU.is_equal))
                step(v.tensor_tensor(m[:], m[:], rk, ALU.mult))
                step(v.tensor_reduce(red[:], m[:], AX_X, ALU.max))
                step(v.tensor_tensor(m[:], m[:], bc(red), ALU.is_equal))
                if m is m0:
                    step(v.scalar_tensor_tensor(pr[:], m[:], -4.0, pr[:], ALU.mult, ALU.add))
            step(v.tensor_reduce(cnt[:, 0:NE], m0[:].rearrange("p n e -> p e n"), AX_X, ALU.add))
            step(v.tensor_reduce(cnt[:, NE:2 * NE], m1[:].rearrange("p n e -> p e n"), AX_X, ALU.add))
            step(v.tensor_tensor(m0[:], m0[:], bc(w0), ALU.mult))
            step(v.tensor_tensor(m1[:], m1[:], bc(w1), ALU.mult))
            step(v.tensor_tensor(S["gate"][:], m0[:], m1[:], ALU.add))
            dve.wait_ge(s_cnt, 1)
            step(v.tensor_scalar(actv[:], pct[:, 0:2 * NE], 0.0, None, ALU.is_gt))
            act0 = actv[:, 0:NE].unsqueeze(1).to_broadcast([P, NT, NE])
            act1 = actv[:, NE:2 * NE].unsqueeze(1).to_broadcast([P, NT, NE])
            step(v.tensor_tensor(m0[:], act0, bc(w0), ALU.mult))
            step(v.tensor_tensor(m1[:], act1, bc(w1), ALU.mult))
            step(v.tensor_tensor(S["gc"][:, :, 0:NE], m0[:], m1[:], ALU.add))
            v.tensor_tensor(S["gc"][:, :, NE:2 * NE], S["gc"][:, :, 0:NE], S["gate"][:], ALU.subtract).then_inc(s_ct, 1)

        @block.tensor
        def _(pe):
            pe.wait_ge(s_c, 16 * NSMALL)
            for i in range(NT // 2):
                pe.wait_ge(s_xn, 1 + 2 * i + 2)
                if i >= 2:
                    pe.wait_ge(s_xl, i - 1)
                for t in range(2):
                    for k in range(KH):
                        last = nc.tensor.transpose(pt[i % 2][:, t, k, :], xn[:, 2 * i + t, k * P:(k + 1) * P], ident[:])
                last.then_inc(s_tr, 1)
            pe.wait_ge(s_xl, NT // 2)
            pe.wait_ge(s_v, 4)

            def project(out, wh, wl, i):
                for n, (w, x) in enumerate(((wh, xh), (wl, xh), (wh, xl))):
                    for k in range(KH):
                        last = nc.tensor.matmul(out, w[:, k, :], x[:, k, i * G:(i + 1) * G],
                                                start=(n == 0 and k == 0), stop=(n == 2 and k == KH - 1))
                return last

            for i in range(NG):
                if i >= 2:
                    pe.wait_ge(s_abc, i - 1)
                project(pab[i % 2][0:W2, :], wabh, wabl, i).then_inc(s_ab, 1)
            pe.wait_ge(s_abc, NG)
            for i in range(NG):
                if i >= 2:
                    pe.wait_ge(s_h1c, i - 1)
                project(pab[i % 2][:], rw1h, rw1l, i).then_inc(s_h1, 1)
            pe.wait_ge(s_h1c, NG)
            for t in range(NT):
                last = nc.tensor.matmul(plg[:, t, :], h1[:, t * P:(t + 1) * P], rw2[:], start=True, stop=True)
            last.then_inc(s_lg, 1)
            pe.wait_ge(s_v, 14)
            for t in range(NT):
                last = nc.tensor.transpose(pgt[:, t // 8, t % 8, :], gb[:, t * P:(t + 1) * P], ident[0:W2, 0:W2])
                if t % 8 == 7 or t == NT - 1:
                    last.then_inc(s_gt, 1)
            pe.wait_ge(s_v, 37)
            pe.wait_ge(s_p, 4)
            nc.tensor.matmul(pct[:, 0:2 * NE], ones[:], cnt[:], start=True, stop=True).then_inc(s_cnt, 1)
            pe.wait_ge(s_ct, 1)


def ffn_phase(nc, A, S, NB, NHK):
    NT, N = NB * 2, NB * T
    NG = N // G
    TG = G // P
    W1 = KH * I
    WX = W1 + IC * H
    NJ = NE * NG
    xh, xl, accf = S["xh"], S["xl"], S["accf"]
    gate = S["gate"][:].rearrange("p n e -> p (n e)")

    with ExitStack() as c:
        def sb(name, shape, dt=F32):
            return c.enter_context(nc.sbuf_tensor(name, shape, dt))

        def sem(name):
            return c.enter_context(nc.semaphore(name))

        raw = sb("ffn_raw", [P, WX])
        wh = sb("ffn_wh", [P, 2 * WX], F16)
        wl = sb("ffn_wl", [P, 2 * WX], F16)
        g32 = [sb(f"hid{i}", [P, G]) for i in range(2)]
        gh = sb("hid_hi", [P, 2 * IC * G], F16)
        gl = sb("hid_lo", [P, 2 * IC * G], F16)
        gb1 = sb("gelu_b1", [P, NE * IC])
        gb1h = sb("gelu_b1_hi", [P, NE * IC], F16)
        gb1l = sb("gelu_b1_lo", [P, NE * IC], F16)
        tail_r = sb("tail_rhs", [2 * NE, H])
        tail_l = sb("tail_lhs", [2 * NE, N])
        cg = sb("cg", [1, NE * H])

        hid_ps = [c.enter_context(nc.psum_tensor(f"hid_ps{i}", [P, G], F32)) for i in range(2)]
        out_ps = c.enter_context(nc.psum_tensor("ffn_ps", [P, 2 * TG * H], F32))
        cg_ps = c.enter_context(nc.psum_tensor("cg_ps", [P, 512], F32))
        tail_ps = c.enter_context(nc.psum_tensor("tail_ps", [P, 512], F32))

        s_raw = sem("expert_loaded")
        s_split = sem("expert_split")
        s_gb = sem("gelu_b1_done")
        s_gbl = sem("gelu_b1_lo_written")
        s_hid = sem("hidden_in_psum")
        s_g32 = sem("hidden_gelu")
        s_gh = sem("hidden_hi")
        s_gl = sem("hidden_lo")
        s_out = sem("expert_out_in_psum")
        s_acc = sem("expert_out_added")
        s_cg = sem("bias_only_out_in_psum")
        s_cgc = sem("bias_only_out_copied")
        s_cgd = sem("bias_only_out_placed")
        s_tl = sem("tail_lhs_in_psum")
        s_tlc = sem("tail_lhs_copied")
        s_to = sem("tail_in_psum")
        s_toa = sem("tail_added")
        s_b2 = sem("b2_loaded")
        s_sg = sem("gate_silu")
        block = c.enter_context(nc.Block())
        NTL = NT // 4

        @block.sync
        def _(sp):
            sp.dma_start(tail_r[0:NE, :], A["b2"]).then_inc(s_b2, 16)
            sp.dma_start(raw[:], A["wffn"][0]).then_inc(s_raw, 16)
            with sp.Fori(1, NE) as e:
                sp.wait_ge(s_split, e * 2)
                sp.wait_ge(s_raw, 16)
                sp.dma_start(raw[:], A["wffn"][ds(e, 1)].rearrange("e p n -> (e p) n")).then_inc(s_raw, 16)
            with sp.Fori(0, NE) as e:
                sp.wait_ge(s_cgc, e + 2)
                sp.wait_ge(s_raw, 16)
                sp.dma_start(A["cgscr"][ds(e, 1), :], cg[:, ds(e * H, H)]).then_inc(s_cgd, 16)
            sp.wait_ge(s_cgd, 16 * NE)
            sp.dma_start(tail_r[NE:2 * NE, :], A["cgscr"]).then_inc(s_b2, 16)
            sp.wait_ge(s_b2, 32)

        @block.gpsimd
        def _(pool):
            def split(e):
                pool.wait_ge(s_raw, e * 16 + 16)
                pool.wait_ge(s_raw, 16)
                nc.gpsimd.tensor_copy(wh[:, ds((e % 2) * WX, WX)], raw[:]).then_inc(s_split, 1)
                pool.wait_ge(s_split, e * 2 + 1)
                nc.gpsimd.tensor_tensor(wl[:, ds((e % 2) * WX, WX)], raw[:], wh[:, ds((e % 2) * WX, WX)],
                                        ALU.subtract).then_inc(s_split, 1)

            split(0)
            split(1)
            with pool.Fori(2, NE) as e:
                pool.wait_ge(s_cg, e - 1)
                split(e)

        @block.scalar
        def _(act):
            act.sem_inc(s_g32, 2)
            nc.scalar.activation(gb1[:], S["b1"][:], ACT.Gelu).then_inc(s_gb, 1)
            act.wait_ge(s_gb, 1)
            nc.scalar.copy(gb1h[:], gb1[:]).then_inc(s_gb, 1)
            with act.Fori(0, NE) as e:
                with act.Fori(0, NG) as g:
                    for k in range(IC):
                        n = e * (NG * IC) + g * IC + k
                        act.wait_ge(s_hid, n + 1)
                        act.wait_ge(s_gl, n + 1)
                        nc.scalar.activation(g32[k % 2][:], hid_ps[k % 2][:], ACT.Gelu,
                                             bias=S["b1"][:, ds(e * IC + k, 1)]).then_inc(s_g32, 1)
                        if k == 0:
                            act.wait_ge(s_out, e * NG + g + 1)
                        act.wait_ge(s_g32, n + 3)
                        nc.scalar.copy(gh[:, ds(g % 2 * (IC * G) + k * G, G)], g32[k % 2][:]).then_inc(s_gh, 1)
            for i in range(NT // 2):
                act.wait_ge(s_toa, i + 1)
                nc.scalar.activation(accf[:, 2 * i:2 * i + 2, :], accf[:, 2 * i:2 * i + 2, :], ACT.Silu).then_inc(s_sg, 1)

        @block.vector
        def _(dve):
            dve.sem_inc(s_gl, 2)
            dve.sem_inc(s_acc, 2)
            dve.sem_inc(s_cgc, 1)
            dve.wait_ge(s_gb, 2)
            nc.vector.tensor_tensor(gb1l[:], gb1[:], gb1h[:], ALU.subtract).then_inc(s_gbl, 1)

            def add(e, g):
                dve.wait_ge(s_out, e * NG + g + 3)
                dve.wait_ge(s_acc, e * NG + g + 2)
                for t in range(TG):
                    dst = accf[:].rearrange("p n h -> p (n h)")[:, ds(g * (TG * H) + t * H, H)]
                    last = nc.vector.scalar_tensor_tensor(
                        dst, out_ps[:, ds(g % 2 * (TG * H) + t * H, H)], gate[:, ds(e + g * (TG * NE) + t * NE, 1)],
                        dst, ALU.mult, ALU.add)
                last.then_inc(s_acc, 1)

            def low(e, g, k):
                dve.wait_ge(s_gh, e * (NG * IC) + g * IC + (k + 1))
                part = ds(g % 2 * (IC * G) + k * G, G)
                nc.vector.tensor_tensor(gl[:, part], g32[k % 2][:], gh[:, part], ALU.subtract).then_inc(s_gl, 1)

            with dve.Fori(0, NE) as e:
                for k in range(IC):
                    low(e, 0, k)
                with dve.Fori(1, NG) as g:
                    for k in range(IC):
                        low(e, g, k)
                    add(e, g - 1)
                add(e, NG - 1)
                dve.wait_ge(s_cg, e + 1)
                nc.vector.tensor_copy(cg[:, ds(e * H, H)], cg_ps[0:1, 0:H]).then_inc(s_cgc, 1)
            for q in range(NTL):
                dve.wait_ge(s_tl, q + 1)
                nc.vector.tensor_copy(tail_l[:, q * 512:(q + 1) * 512], tail_ps[0:2 * NE, :]).then_inc(s_tlc, 1)
            dve.wait_ge(s_acc, NE * NG + 2)
            for i in range(NT // 2):
                dve.wait_ge(s_to, i + 1)
                nc.vector.tensor_tensor(accf[:, 2 * i:2 * i + 2, :].rearrange("p t h -> p (t h)"),
                                        accf[:, 2 * i:2 * i + 2, :].rearrange("p t h -> p (t h)"),
                                        hid_ps[i % 2][:], ALU.add).then_inc(s_toa, 1)
            dve.wait_ge(s_sg, NT // 2)

        @block.tensor
        def _(pe):
            pe.sem_inc(s_out, 2)

            def hidden(e, g, k):
                pe.wait_ge(s_g32, e * (NG * IC) + g * IC + (k + 1))
                for m, (w, x) in enumerate(((wh, xh), (wl, xh), (wh, xl))):
                    for kk in range(KH):
                        last = nc.tensor.matmul(hid_ps[k % 2][:], w[:, ds((e % 2) * WX + kk * I + k * P, P)],
                                                x[:, kk, ds(g * G, G)],
                                                start=(m == 0 and kk == 0), stop=(m == 2 and kk == KH - 1))
                last.then_inc(s_hid, 1)

            def product(e, g, k):
                pe.wait_ge(s_gl, e * (NG * IC) + g * IC + (k + 3))
                if k == 0:
                    pe.wait_ge(s_acc, e * NG + g + 1)
                for t in range(TG):
                    for m, (x, w) in enumerate(((gh, wh), (gh, wl), (gl, wh))):
                        last = nc.tensor.matmul(out_ps[:, ds(g % 2 * (TG * H) + t * H, H)],
                                                x[:, ds(g % 2 * (IC * G) + (k * G + t * P), P)],
                                                w[:, ds((e % 2) * WX + W1 + k * H, H)],
                                                start=(k == 0 and m == 0 and t % 2 == 0), stop=(k == IC - 1 and m == 2),
                                                skip_group_check=True)
                if k == IC - 1:
                    last.then_inc(s_out, 1)

            with pe.Fori(0, NE) as e:
                pe.wait_ge(s_split, e * 2 + 2)
                for k in range(IC):
                    hidden(e, 0, k)
                with pe.Fori(1, NG) as g:
                    for k in range(IC):
                        hidden(e, g, k)
                        product(e, g - 1, k)
                for k in range(IC):
                    product(e, NG - 1, k)
                pe.wait_ge(s_gbl, 1)
                pe.wait_ge(s_cgc, e + 1)
                for k in range(IC):
                    for m, (x, w) in enumerate(((gb1h, wh), (gb1h, wl), (gb1l, wh))):
                        last = nc.tensor.matmul(cg_ps[0:1, 0:H], x[:, ds(e * IC + k, 1)],
                                                w[:, ds((e % 2) * WX + W1 + k * H, H)],
                                                start=(k == 0 and m == 0), stop=(k == IC - 1 and m == 2))
                last.then_inc(s_cg, 1)
            for q in range(NTL):
                if q:
                    pe.wait_ge(s_tlc, q)
                for t in range(4 * q, 4 * q + 4):
                    last = nc.tensor.transpose(tail_ps[0:2 * NE, (t % 4) * P:(t % 4 + 1) * P], S["gc"][:, t, :], S["ident"][:])
                last.then_inc(s_tl, 1)
            pe.wait_ge(s_b2, 32)
            pe.wait_ge(s_tlc, NTL)
            for t in range(NT):
                if t % 2 == 0 and t >= 4:
                    pe.wait_ge(s_toa, t // 2 - 1)
                last = nc.tensor.matmul(hid_ps[t // 2 % 2][:, (t % 2) * H:(t % 2 + 1) * H],
                                        tail_l[:, t * P:(t + 1) * P], tail_r[:], start=True, stop=True)
                if t % 2:
                    last.then_inc(s_to, 1)


def attention_phase(nc, A, S, NB, NHK):
    NT = NB * 2
    NJ = NB * NHK
    PEEL = -(-LAG // RING) * RING
    C0 = 8
    ident, id16 = S["ident"], S["id16"]
    xh, xl, acca, accf, xs = S["xh"], S["xl"], S["acca"], S["accf"], S["xs"]

    with ExitStack() as c:
        def sb(name, shape, dt=F32):
            return c.enter_context(nc.sbuf_tensor(name, shape, dt))

        def ring(name, shape, dt=F32):
            return [sb(f"{name}{i}", shape, dt) for i in range(RING)]

        owners = {"pe": [], "dve": [], "act": [], "pool": []}

        def sem(name, owner):
            s = c.enter_context(nc.semaphore(name))
            owners[owner].append(s)
            return s

        wraw = sb("w_raw", [P, 8 * (FCH + OCH)])
        wscl = sb("w_scaled", [P, OCH])
        wfh = sb("wf_hi", [P, 2 * FW], F16)
        wfl = sb("wf_lo", [P, 2 * FW], F16)
        woh = sb("wo_hi", [P, 2 * OW], F16)
        wol = sb("wo_lo", [P, 2 * OW], F16)
        pad = sb("qkv_padded", [P, 4, T + 3])
        cv = sb("conv", [P, 4, T])
        act4 = sb("conv_silu", [P, 4, T])
        sq = sb("squares", [P, 4, P])
        ssq = sb("ssq", [P, 4])
        rn = sb("rnorm", [P, 4])
        qkn = sb("qk_unit", [P, 4, P])
        qkh = sb("qk_unit_hi", [P, 4, P], F16)
        qkl = sb("qk_unit_lo", [P, 4, P], F16)
        qkT = ring("qkT", [P, 2, 2, 2, P], F16)
        vtok = ring("v_tok", [P, 2, 2, P])
        sz = ring("silu_z", [P, 2, 2, P])
        beta = sb("beta4", [P, 2, 2])
        gin = ring("gin2", [P, 2])
        ngin = ring("ngin2", [P, 2])
        dbc = ring("decay_rows", [P, 2, T])
        Es = sb("E_strict", [P, 4, P])
        E1 = sb("E_incl", [P, 4, P])
        Eb = sb("E_strict_beta", [P, 4, P])
        E1b = sb("E_incl_beta", [P, 4, P])
        kw = sb("k_weighted", [P, 2, P])
        kwh = ring("k_weighted_hi", [P, 2, P], F16)
        kwl = ring("k_weighted_lo", [P, 2, P], F16)
        A32 = sb("A32", [P, 4, P])
        M32 = sb("M32", [P, 4, P])
        Ah = ring("A_hi", [P, 4, P], F16)
        Al = ring("A_lo", [P, 4, P], F16)
        Mh = ring("M_hi", [P, 4, P], F16)
        Ml = ring("M_lo", [P, 4, P], F16)
        XX = [sb(f"X_XT{i}", [P, 4, 2, P], F16) for i in range(2)]
        nP = sb("neg_P", [P, 4, P], F16)
        XF = ring("XT_final", [P, 4, P], F16)
        Rh = sb("R_hi", [P, 2, P], F16)
        R1 = sb("R1", [P, 2, P])
        Dh = [sb(f"D_hi{i}", [P, 2, P], F16) for i in range(2)]
        rh = sb("residual", [P, 2, P], F16)
        Dl = [sb(f"D_lo{i}", [P, 2, P], F16) for i in range(2)]
        Sh = sb("S_hi", [P, 2, P], F16)
        Sl = sb("S_lo", [P, 2, P], F16)
        QS = sb("q_state", [P, 2, P])
        o1 = sb("o_chunk1", [P, 2, P])
        y = ring("y", [P, 2, 2, P])
        ysq = sb("y_sq", [P, 4, P])
        yss = sb("y_ss", [P, 4])
        yr = sb("y_rms", [P, 4])
        yn = sb("y_unit", [P, 4, P])
        yh = sb("y_hi", [P, 4, P], F16)
        yl = sb("y_lo", [P, 4, P], F16)
        yT = sb("yT", [P, 2, 4, P], F16)

        def bank(name, shape, dt=F32):
            return c.enter_context(nc.psum_tensor(name, shape, dt))

        b_P = bank("b_P", [P, 4, P])
        b_X = bank("b_X", [P, 4, 2, P])
        b_s = bank("b_s", [P, 4, P])
        shared = [bank(f"b_shared{i}", [P, 512]) for i in range(4)]
        units = lambda bk: bk[:].rearrange("p (u t) -> p u t", u=4)
        units16 = lambda bk: bk[:].bitcast(F16).rearrange("p (n t) -> p n t", t=P)
        raw = [shared[0], shared[3]]
        raw_z = shared[1]
        tok_qk, tok_v = units(shared[2]), units(shared[0])
        chan_qk = units16(shared[3])
        sims = shared[2][:].rearrange("p (c x t) -> p c x t", c=2, x=2)
        outs = [units(shared[1])[:, 0:2], units(shared[3])[:, 0:2]]
        chan_y = units16(shared[3])
        prod = shared[3]

        s_wld0 = c.enter_context(nc.semaphore("first_weights_loaded"))
        s_wld = [c.enter_context(nc.semaphore(f"weight_chunk_loaded{i}")) for i in range(RING)]
        s_dbc = [c.enter_context(nc.semaphore(f"decay_rows_loaded{i}")) for i in range(RING)]
        s_done = c.enter_context(nc.semaphore("output_stored"))
        s_settled = c.enter_context(nc.semaphore("waits_settled"))
        s_pz = c.enter_context(nc.semaphore("padding_zeroed"))
        s_ssum = c.enter_context(nc.semaphore("ssq_summed"))
        s_ysum = c.enter_context(nc.semaphore("y_ss_summed"))
        s_mul = c.enter_context(nc.semaphore("branches_multiplied"))
        s_wf = sem("front_weights_split", "pool")
        s_wo = sem("out_weights_split", "pool")
        s_wt = sem("weight_step", "pool")
        s_ws = sem("out_weight_step", "pool")
        s_rn = sem("rnorm_ready", "pool")
        s_qkl = sem("qk_lo_ready", "pool")
        s_E1 = sem("E_incl_ready", "pool")
        s_Eb = sem("E_strict_beta_ready", "pool")
        s_E1b = sem("E_incl_beta_ready", "pool")
        s_kws = sem("k_weighted", "pool")
        s_kwh = sem("k_weighted_hi_ready", "pool")
        s_kw = sem("k_weighted_lo_ready", "pool")
        s_Al = sem("A_lo_ready", "pool")
        s_Ml = sem("M_lo_ready", "pool")
        s_yr = sem("y_rms_ready", "pool")
        s_yn = sem("y_unit_ready", "pool")
        s_yl = sem("y_lo_ready", "pool")
        s_raw = [sem(f"qk_v_raw_in_psum{i}", "pe") for i in range(2)]
        s_z = sem("z_in_psum", "pe")
        s_tqk = sem("qk_tok_in_psum", "pe")
        s_tv = sem("v_tok_in_psum", "pe")
        s_T = sem("qkT_in_psum", "pe")
        s_kk = sem("kk_qk_in_psum", "pe")
        s_P = [sem(f"inv_P_in_psum{i}", "pe") for i in range(2)]
        s_Z = [sem(f"inv_X_in_psum{i}", "pe") for i in range(2)]
        s_d = [sem(f"solve_in_psum{i}", "pe") for i in range(2)]
        s_rs = [sem(f"residual_in_psum{i}", "pe") for i in range(2)]
        s_dd = [sem(f"correction_in_psum{i}", "pe") for i in range(2)]
        s_o = [sem(f"o_in_psum{i}", "pe") for i in range(2)]
        s_S = sem("state_in_psum", "pe")
        s_KQ = sem("k_q_state_in_psum", "pe")
        s_yT = sem("yT_in_psum", "pe")
        s_out = sem("out_in_psum", "pe")
        s_pad = [sem(f"padded{i}", "act") for i in range(2)]
        s_t3 = [sem(f"newest_tap{i}", "act") for i in range(2)]
        s_silu = [sem(f"silu{i}", "act") for i in range(2)]
        s_sz = sem("z_silu", "act")
        s_sq = sem("qk_squared", "act")
        s_vt = sem("v_tok_copied", "act")
        s_qkh = sem("qk_hi_ready", "act")
        s_Ah = sem("A_hi_ready", "act")
        s_Mh = sem("M_hi_ready", "act")
        s_X = [sem(f"inv_X_copied{i}", "act") for i in range(2)]
        s_Rh = [sem(f"R_hi_ready{i}", "act") for i in range(2)]
        s_Dh = [sem(f"D_hi_ready{i}", "act") for i in range(2)]
        s_Dl = [sem(f"D_lo_ready{i}", "act") for i in range(2)]
        s_Sh = sem("S_hi_ready", "act")
        s_QS = sem("q_state_ready", "act")
        s_ysq = sem("y_squared", "act")
        s_yh = sem("y_hi_ready", "act")
        s_yTc = sem("yT_ready", "act")
        s_t2 = [sem(f"conv_tap2{i}", "dve") for i in range(2)]
        s_t1 = [sem(f"conv_tap1{i}", "dve") for i in range(2)]
        s_cv = [sem(f"conv_ready{i}", "dve") for i in range(2)]
        s_ssq = sem("ssq_ready", "dve")
        s_qkn = sem("qk_unit_ready", "dve")
        s_qkT = sem("qkT_ready", "dve")
        s_g = sem("gates_ready", "dve")
        s_Es = sem("E_strict_ready", "dve")
        s_A = sem("A_ready", "dve")
        s_M = sem("M_ready", "dve")
        s_nP = [sem(f"neg_P_ready{i}", "dve") for i in range(2)]
        s_r = [sem(f"residual_ready{i}", "dve") for i in range(2)]
        s_Sl = sem("S_lo_ready", "dve")
        s_R1 = sem("R1_ready", "dve")
        s_o1 = sem("o_chunk1_ready", "dve")
        s_y = [sem(f"y_ready{i}", "dve") for i in range(2)]
        s_yss = sem("y_ss_ready", "dve")
        s_acc = sem("out_added", "dve")
        s_fin = sem("final_step", "dve")

        def ready(eng, s, n):
            eng.wait_ge(s, n + (1 + C0))

        def spare(eng, s, n, slots=1):
            eng.wait_ge(s, n + (1 + C0 - slots))

        def settle(eng):
            eng.sem_inc(s_settled, 1)

        def start(eng, owner):
            for s in owners[owner]:
                eng.sem_inc(s, C0)

        def at(s, i, u):
            return Step(s, u % RING, i, s // 8, s % 8)

        def take(x, last, others=()):
            for s, back, *which in (*last, *others) if isinstance(x.j, int) else last:
                per, k = which or (1, 0)
                if not isinstance(x.j, int):
                    nc.tensor.wait_ge(s, x.j * per + (k + 1 + C0 - back * per))
                elif x.j - back >= NJ:
                    nc.tensor.wait_ge(s, NJ * per + C0)
                elif x.j >= back:
                    nc.tensor.wait_ge(s, (x.j - back) * per + (k + 1 + C0))

        def drive(eng, step):
            def run(item):
                def at_lag(d, f, *args):
                    if item(d):
                        f(item(d), *args)
                step(at_lag)

            def peeled(s):
                run(lambda d: at(s - d, (s - d) // RING, s - d) if 0 <= s - d < NJ else None)

            for s in range(PEEL):
                peeled(s)
            with eng.Fori(PEEL // RING, NJ // RING) as i:
                for u in range(RING):
                    run(lambda d: at(3 * i + (u - d), i + (u - d) // RING, u - d))
            for s in range(NJ // RING * RING, NJ + LAG):
                peeled(s)

        block = c.enter_context(nc.Block())

        @block.sync
        def _(sp):
            CH = FCH + OCH
            sp.dma_start(wraw[:].rearrange("p (b n) -> p b n", b=8),
                         A["wattn"][0:8].rearrange("b p n -> p b n")).then_inc(s_wld0, 16)
            def load(x):
                spare(sp, s_Es, x.j, RING)
                settle(sp)
                sp.dma_start(dbc[x.p][:], A["dscr"][ds(x.hk * 2, 2), ds(x.b * T, T)]
                             .partition_broadcast(P)).then_inc(s_dbc[x.p], 16)
                spare(sp, s_wf, x.j + 8, RING)
                settle(sp)
                spare(sp, s_wo, x.j + 8, 8)
                settle(sp)
                sp.dma_start(wraw[:, ds(x.b * CH, CH)],
                             A["wattn"][ds(x.j + 8, 1)].rearrange("b p n -> (b p) n")).then_inc(s_wld[x.p], 16)

            def step(at_lag):
                at_lag(0, load)

            drive(sp, step)
            for t in range(0, NT, 4):
                sp.wait_ge(s_fin, C0 + t // 4 + 1)
                sp.dma_start(A["out"].rearrange("(n p) h -> p n h", p=P)[:, t:t + 4, :], xs[:, t:t + 4, :]).then_inc(s_done, 16)
            sp.wait_ge(s_done, 16 * (NT // 4))

        @block.gpsimd
        def _(pool):
            start(pool, "pool")
            CH = FCH + OCH
            g = nc.gpsimd

            def split_front(q, head, part):
                src = wraw[:, ds(part * CH, FCH)]
                dst = ds(head % 2 * FW + part * FCH, FCH)
                settle(pool)
                g.tensor_copy(wfh[:, dst], src).then_inc(s_wt, 1)
                ready(pool, s_wt, q)
                g.tensor_tensor(wfl[:, dst], src, wfh[:, dst], ALU.subtract).then_inc(s_wf, 1)

            def split_out(q, head, part):
                dst = ds(head % 2 * OW + part * OCH, OCH)
                spare(pool, s_wo, q)
                g.tensor_tensor(wscl[:], wraw[:, ds(part * CH + FCH, OCH)], S["nw"][:, 0:1].to_broadcast([P, OCH]),
                                ALU.mult).then_inc(s_ws, 1)
                ready(pool, s_ws, q * 2)
                settle(pool)
                g.tensor_copy(woh[:, dst], wscl[:]).then_inc(s_ws, 1)
                ready(pool, s_ws, q * 2 + 1)
                g.tensor_tensor(wol[:, dst], wscl[:], woh[:, dst], ALU.subtract).then_inc(s_wo, 1)

            pool.wait_ge(s_wld0, 16)
            for q in range(8):
                split_front(q, 0, q)
            for q in range(8 - OLAG):
                split_out(q, 0, q)

            def front_weights(x):
                pool.wait_ge(s_wld[x.p], x.q * 16 + 16)
                for s in (s_raw[0], s_raw[1], s_z):
                    spare(pool, s, x.hk * 8 + 7, 8)
                split_front(x.j + 8, x.hk + 1, x.b)

            def out_weights(x):
                q = x.j + (8 - OLAG)
                if not isinstance(q, int) or q // 8 > 1:
                    spare(pool, s_out, q // 8 * 8 + 7, 16)
                split_out(q, q // 8, q % 8)

            by_beta = beta[:].rearrange("p v c -> p (v c)").unsqueeze(2).to_broadcast([P, 4, P])

            def decays_incl(x):
                ready(pool, s_Es, x.j)
                spare(pool, s_E1b, x.j)
                spare(pool, s_M, x.j)
                spare(pool, s_kws, x.j)
                g.tensor_tensor(E1[:], Es[:], S["ident4"][:].rearrange("p (u t) -> p u t", u=4), ALU.add).then_inc(s_E1, 1)

            def decays_strict_beta(x):
                ready(pool, s_g, x.j)
                ready(pool, s_Es, x.j)
                spare(pool, s_A, x.j)
                g.tensor_tensor(Eb[:], Es[:], by_beta, ALU.mult).then_inc(s_Eb, 1)

            def decays_incl_beta(x):
                ready(pool, s_g, x.j)
                ready(pool, s_E1, x.j)
                spare(pool, s_M, x.j)
                spare(pool, s_kws, x.j)
                g.tensor_tensor(E1b[:], E1[:], by_beta, ALU.mult).then_inc(s_E1b, 1)

            def unit(x):
                ready(pool, s_ssq, x.j)
                spare(pool, s_qkn, x.j)
                g.tensor_tensor(rn[:], ssq[:], S["half"][:], ALU.pow).then_inc(s_rn, 1)

            def qk_lo(x):
                ready(pool, s_qkh, x.j)
                spare(pool, s_T, x.j)
                g.tensor_tensor(qkl[:], qkn[:], qkh[:], ALU.subtract).then_inc(s_qkl, 1)

            def weigh_k(x):
                ready(pool, s_qkn, x.j)
                ready(pool, s_E1b, x.j)
                spare(pool, s_kw, x.j)
                wend = E1b[:].rearrange("p (v c) t -> p v c t", v=2)[:, :, 0, P - 1:P].to_broadcast([P, 2, P])
                g.tensor_tensor(kw[:], qkn[:, 0:1, :].to_broadcast([P, 2, P]), wend, ALU.mult).then_inc(s_kws, 1)

            def split_k(x):
                ready(pool, s_kws, x.j)
                spare(pool, s_S, x.j, RING)
                settle(pool)
                g.tensor_copy(kwh[x.p][:], kw[:]).then_inc(s_kwh, 1)
                ready(pool, s_kwh, x.j)
                g.tensor_tensor(kwl[x.p][:], kw[:], kwh[x.p][:], ALU.subtract).then_inc(s_kw, 1)

            def A_lo(x):
                ready(pool, s_Ah, x.j)
                spare(pool, s_rs[1], x.j, RING)
                g.tensor_tensor(Al[x.p][:], A32[:], Ah[x.p][:], ALU.subtract).then_inc(s_Al, 1)

            def M_lo(x):
                ready(pool, s_Mh, x.j)
                spare(pool, s_o[1], x.j, RING)
                g.tensor_tensor(Ml[x.p][:], M32[:], Mh[x.p][:], ALU.subtract).then_inc(s_Ml, 1)

            def rms(x):
                ready(pool, s_yss, x.j)
                spare(pool, s_yn, x.j)
                g.tensor_tensor(yr[:], yss[:], S["half"][:], ALU.pow).then_inc(s_yr, 1)

            def y_unit(x):
                ready(pool, s_yr, x.j)
                spare(pool, s_yh, x.j)
                spare(pool, s_yl, x.j)
                g.tensor_tensor(yn[:], y[x.p][:].rearrange("p c v t -> p (c v) t"),
                                yr[:].unsqueeze(2).to_broadcast([P, 4, P]), ALU.mult).then_inc(s_yn, 1)

            def y_lo(x):
                ready(pool, s_yh, x.j)
                spare(pool, s_yT, x.j)
                g.tensor_tensor(yl[:], yn[:], yh[:], ALU.subtract).then_inc(s_yl, 1)

            def step(at_lag):
                at_lag(2, A_lo)
                at_lag(2, weigh_k)
                at_lag(1, decays_incl)
                at_lag(1, out_weights)
                at_lag(4, rms)
                at_lag(4, y_unit)
                at_lag(1, unit)
                at_lag(4, y_lo)
                at_lag(0, front_weights)
                at_lag(2, M_lo)
                at_lag(1, decays_strict_beta)
                at_lag(1, qk_lo)
                at_lag(1, decays_incl_beta)
                at_lag(2, split_k)

            drive(pool, step)

        @block.scalar
        def _(act):
            start(act, "act")
            a = nc.scalar

            def pad_block(x, half):
                ready(act, s_raw[half], x.j)
                spare(act, s_cv[half], x.j)
                a.copy(pad[:, 2 * half:2 * half + 2, 3:T + 3],
                       raw[half][:].rearrange("p (m t) -> p m t", m=2)).then_inc(s_pad[half], 1)

            def newest_tap(x, half):
                ready(act, s_raw[half], x.j)
                spare(act, s_silu[half], x.j)
                for m in range(2):
                    ins = a.activation(cv[:, 2 * half + m, :], raw[half][:, m * T:(m + 1) * T], ACT.Copy,
                                       scale=S["cw"][:, ds(x.hk * 16 + ((2 * half + m) * 4 + 3), 1)])
                ins.then_inc(s_t3[half], 1)

            def silu_z(x):
                ready(act, s_z, x.j)
                spare(act, s_y[0], x.j, RING)
                spare(act, s_y[1], x.j, RING)
                a.activation(sz[x.p][:], raw_z[:].rearrange("p (c v t) -> p c v t", c=2, v=2), ACT.Silu).then_inc(s_sz, 1)

            def silu(x, half):
                ready(act, s_cv[half], x.j)
                spare(act, (s_tqk, s_tv)[half], x.j)
                a.activation(act4[:, 2 * half:2 * half + 2, :], cv[:, 2 * half:2 * half + 2, :],
                             ACT.Silu).then_inc(s_silu[half], 1)

            def squares(x):
                ready(act, s_tqk, x.j)
                spare(act, s_ssq, x.j)
                a.activation(sq[:], tok_qk, ACT.Square).then_inc(s_sq, 1)

            def v_tok(x):
                ready(act, s_tv, x.j)
                spare(act, s_R1, x.j, RING)
                spare(act, s_r[0], x.j, RING)
                a.copy(vtok[x.p][:].rearrange("p v c t -> p (v c) t"), tok_v).then_inc(s_vt, 1)

            def qk_hi(x):
                ready(act, s_qkn, x.j)
                spare(act, s_T, x.j)
                spare(act, s_qkl, x.j)
                a.copy(qkh[:], qkn[:]).then_inc(s_qkh, 1)

            def A_hi(x):
                ready(act, s_A, x.j)
                spare(act, s_rs[1], x.j, RING)
                a.copy(Ah[x.p][:], A32[:]).then_inc(s_Ah, 1)

            def M_hi(x):
                ready(act, s_M, x.j)
                spare(act, s_o[1], x.j, RING)
                a.copy(Mh[x.p][:], M32[:]).then_inc(s_Mh, 1)

            def grow(x, k, ch):
                ready(act, s_Z[ch], x.j * NLEV + k)
                u = slice(2 * ch, 2 * ch + 2)
                if k < NLEV - 1:
                    a.copy(XX[(k + 1) % 2][:, u], b_X[:, u]).then_inc(s_X[ch], 1)
                else:
                    spare(act, s_dd[ch], x.j, RING)
                    a.copy(XF[x.p][:, u], b_X[:, u, 1, :]).then_inc(s_X[ch], 1)

            def right_side(x, ch):
                if ch == 0:
                    ready(act, s_vt, x.j)
                    spare(act, s_d[1], x.j)
                    a.copy(Rh[:], vtok[x.p][:, :, 0, :]).then_inc(s_Rh[0], 1)
                else:
                    ready(act, s_R1, x.j)
                    a.copy(Rh[:], R1[:]).then_inc(s_Rh[1], 1)

            def D_hi(x, ch):
                ready(act, s_d[ch], x.j)
                spare(act, s_o[ch], x.j)
                if ch == 0:
                    spare(act, s_S, x.j)
                a.copy(Dh[ch][:], b_s[:, 0:2, :]).then_inc(s_Dh[ch], 1)

            def D_lo(x, ch):
                ready(act, s_dd[ch], x.j)
                a.copy(Dl[ch][:], b_s[:, 0:2, :]).then_inc(s_Dl[ch], 1)

            def S_hi(x):
                ready(act, s_S, x.j)
                spare(act, s_KQ, x.j)
                a.copy(Sh[:], b_s[:, 0:2, :]).then_inc(s_Sh, 1)

            def q_state(x):
                ready(act, s_KQ, x.j)
                ready(act, s_R1, x.j)
                spare(act, s_o1, x.j)
                a.activation(QS[:, 0, :], b_s[:, 2, :], ACT.Copy, scale=gin[x.p][:, 0:1])
                a.activation(QS[:, 1, :], b_s[:, 3, :], ACT.Copy, scale=gin[x.p][:, 1:2]).then_inc(s_QS, 1)

            def y_square(x):
                ready(act, s_y[0], x.j)
                ready(act, s_y[1], x.j)
                spare(act, s_yss, x.j)
                a.activation(ysq[:], y[x.p][:].rearrange("p c v t -> p (c v) t"), ACT.Square).then_inc(s_ysq, 1)

            def y_hi(x):
                ready(act, s_yn, x.j)
                spare(act, s_yT, x.j)
                spare(act, s_yl, x.j)
                a.copy(yh[:], yn[:]).then_inc(s_yh, 1)

            def y_T(x):
                ready(act, s_yT, x.j)
                spare(act, s_out, x.j)
                a.copy(yT[:].rearrange("p a u t -> p (a u) t"), chan_y).then_inc(s_yTc, 1)

            def step(at_lag):
                at_lag(3, grow, 3, 0)
                at_lag(2, qk_hi)
                at_lag(4, S_hi)
                at_lag(4, grow, 5, 1)
                at_lag(2, v_tok)
                at_lag(1, silu, 0)
                at_lag(3, grow, 4, 0)
                at_lag(1, silu, 1)
                at_lag(4, grow, 6, 1)
                at_lag(4, right_side, 1)
                at_lag(4, q_state)
                at_lag(0, pad_block, 0)
                at_lag(3, grow, 5, 0)
                at_lag(4, D_hi, 1)
                at_lag(3, grow, 0, 1)
                at_lag(2, A_hi)
                at_lag(3, right_side, 0)
                at_lag(4, D_lo, 1)
                at_lag(3, grow, 6, 0)
                at_lag(3, grow, 1, 1)
                at_lag(0, newest_tap, 0)
                at_lag(2, grow, 0, 0)
                at_lag(4, y_square)
                at_lag(1, squares)
                at_lag(3, D_hi, 0)
                at_lag(3, grow, 2, 1)
                at_lag(2, M_hi)
                at_lag(2, grow, 1, 0)
                at_lag(0, newest_tap, 1)
                at_lag(3, grow, 3, 1)
                at_lag(4, y_hi)
                at_lag(0, pad_block, 1)
                at_lag(2, grow, 2, 0)
                at_lag(1, silu_z)
                at_lag(3, D_lo, 0)
                at_lag(3, grow, 4, 1)
                at_lag(4, y_T)

            drive(act, step)

        @block.vector
        def _(dve):
            start(dve, "dve")
            v = nc.vector
            v.memset(pad[:, :, 0:3], 0.0).then_inc(s_pz, 1)
            dve.wait_ge(s_pz, 1)

            def conv(x, half, tap):
                if tap == 2:
                    ready(dve, s_pad[half], x.j)
                ready(dve, (s_t1, s_t2, s_t3)[tap][half], x.j)
                for m in range(2 * half, 2 * half + 2):
                    w = S["cw"][:, ds(x.hk * 16 + (m * 4 + tap), 1)]
                    ins = v.scalar_tensor_tensor(cv[:, m, :], pad[:, m, tap:tap + T], w, cv[:, m, :], ALU.mult, ALU.add)
                ins.then_inc((s_cv, s_t1, s_t2)[tap][half], 1)

            def norms(x):
                ready(dve, s_sq, x.j)
                spare(dve, s_rn, x.j)
                v.tensor_reduce(ssq[:], sq[:], AX_X, ALU.add).then_inc(s_ssum, 1)
                dve.wait_ge(s_ssum, x.j + 1)
                v.tensor_scalar(ssq[:], ssq[:], 1e-24, None, ALU.max).then_inc(s_ssq, 1)

            def unit(x):
                ready(dve, s_rn, x.j)
                spare(dve, s_qkh, x.j)
                spare(dve, s_qkl, x.j)
                spare(dve, s_kws, x.j)
                v.tensor_tensor(qkn[:], tok_qk, rn[:].unsqueeze(2).to_broadcast([P, 4, P]), ALU.mult).then_inc(s_qkn, 1)

            def qk_T(x):
                ready(dve, s_T, x.j)
                spare(dve, s_KQ, x.j, RING)
                spare(dve, s_kk, x.j, RING)
                v.tensor_copy(qkT[x.p][:].rearrange("p a c x t -> p (a c x) t"), chan_qk).then_inc(s_qkT, 1)

            def gates(x):
                spare(dve, s_Eb, x.j)
                spare(dve, s_E1b, x.j)
                spare(dve, s_QS, x.j, RING)
                spare(dve, s_R1, x.j, RING)
                col = S["col"][:].rearrange("p n w -> p (n w)")
                hk2, tile = x.hk * 2, x.b * 2
                for ch in range(2):
                    v.tensor_copy(beta[:, :, ch], col[:, ds((tile + ch) * 64 + (hk2 + 32), 2)])
                v.tensor_copy(gin[x.p][:], col[:, ds((tile + 1) * 64 + hk2, 2)])
                v.tensor_copy(ngin[x.p][:], S["ngin"][:].rearrange("p n w -> p (n w)")[:, ds((tile + 1) * 32 + hk2, 2)]).then_inc(s_g, 1)
                dve.wait_ge(s_dbc[x.p], x.q * 16 + 16)
                spare(dve, s_E1, x.j)
                v.tensor_tensor_scan(Es[:].rearrange("p u t -> p (u t)"), S["inj"][:],
                                     dbc[x.p][:].rearrange("p v t -> p (v t)"), 0.0, ALU.add, ALU.mult).then_inc(s_Es, 1)

            four = lambda m: m[:].rearrange("p (v c) t -> p v c t", v=2)

            def matrix_A(x):
                ready(dve, s_kk, x.j)
                ready(dve, s_Eb, x.j)
                spare(dve, s_Ah, x.j)
                spare(dve, s_Al, x.j)
                for w in range(2):
                    ins = v.tensor_tensor(four(A32)[:, w], sims[:, :, 0, :], four(Eb)[:, w], ALU.mult)
                ins.then_inc(s_A, 1)

            def matrix_M(x):
                ready(dve, s_kk, x.j)
                ready(dve, s_E1b, x.j)
                spare(dve, s_Mh, x.j)
                spare(dve, s_Ml, x.j)
                for w in range(2):
                    ins = v.tensor_tensor(four(M32)[:, w], sims[:, :, 1, :], four(E1b)[:, w], ALU.mult)
                ins.then_inc(s_M, 1)

            def mask(x, k, ch):
                n = x.j * NLEV + k
                spare(dve, s_Z[ch], n)
                if k == 0:
                    ready(dve, s_Ah, x.j)
                    src = four(Ah[x.p])[:, :, ch, :]
                else:
                    ready(dve, s_P[ch], x.j * (NLEV - 1) + (k - 1))
                    src = b_P[:, 2 * ch:2 * ch + 2, :]
                v.tensor_tensor(nP[:, 2 * ch:2 * ch + 2, :], src, S["nmask"][:, k:k + 1, :].to_broadcast([P, 2, P]),
                                ALU.mult).then_inc(s_nP[ch], 1)

            def residual(x, ch):
                ready(dve, s_rs[ch], x.j)
                v.tensor_tensor(rh[:], vtok[x.p][:, :, 0, :] if ch == 0 else R1[:], b_s[:, 0:2, :],
                                ALU.subtract).then_inc(s_r[ch], 1)

            def S_lo(x):
                ready(dve, s_Sh, x.j)
                v.tensor_tensor(Sl[:], b_s[:, 0:2, :], Sh[:], ALU.subtract).then_inc(s_Sl, 1)

            def right_side_1(x):
                ready(dve, s_KQ, x.j)
                for w in range(2):
                    ins = v.scalar_tensor_tensor(R1[:, w, :], b_s[:, w, :], ngin[x.p][:, w:w + 1], vtok[x.p][:, w, 1, :],
                                                 ALU.mult, ALU.add)
                ins.then_inc(s_R1, 1)

            def gated_0(x):
                ready(dve, s_o[0], x.j)
                ready(dve, s_sz, x.j)
                spare(dve, s_yn, x.j, RING)
                v.tensor_tensor(y[x.p][:, 0], outs[0], sz[x.p][:, 0], ALU.mult).then_inc(s_y[0], 1)

            def gated_1(x):
                ready(dve, s_o[1], x.j)
                ready(dve, s_QS, x.j)
                v.tensor_tensor(o1[:], outs[1], QS[:], ALU.add).then_inc(s_o1, 1)
                ready(dve, s_o1, x.j)
                ready(dve, s_sz, x.j)
                spare(dve, s_yn, x.j, RING)
                v.tensor_tensor(y[x.p][:, 1], o1[:], sz[x.p][:, 1], ALU.mult).then_inc(s_y[1], 1)

            def y_norm(x):
                ready(dve, s_ysq, x.j)
                spare(dve, s_yr, x.j)
                v.tensor_reduce(yss[:], ysq[:], AX_X, ALU.add).then_inc(s_ysum, 1)
                dve.wait_ge(s_ysum, x.j + 1)
                v.tensor_scalar(yss[:], yss[:], 1.0 / P, 1e-6, ALU.mult, ALU.add).then_inc(s_yss, 1)

            def add(x):
                ready(dve, s_out, x.j)
                dst = acca[:].rearrange("p n h -> p (n h)")[:, ds(x.b * 2 * H, 2 * H)]
                v.tensor_tensor(dst, dst, prod[:], ALU.add).then_inc(s_acc, 1)

            def step(at_lag):
                at_lag(3, mask, 5, 0)
                at_lag(2, qk_T)
                at_lag(3, mask, 0, 1)
                at_lag(1, gates)
                at_lag(2, matrix_A)
                at_lag(3, mask, 6, 0)
                at_lag(4, residual, 1)
                at_lag(3, mask, 1, 1)
                at_lag(2, mask, 0, 0)
                at_lag(2, matrix_M)
                at_lag(4, gated_1)
                at_lag(3, mask, 2, 1)
                at_lag(0, conv, 0, 2)
                at_lag(4, y_norm)
                at_lag(2, mask, 1, 0)
                at_lag(1, norms)
                at_lag(3, mask, 3, 1)
                at_lag(0, conv, 0, 1)
                at_lag(2, mask, 2, 0)
                at_lag(0, conv, 0, 0)
                at_lag(3, residual, 0)
                at_lag(3, mask, 4, 1)
                at_lag(1, unit)
                at_lag(2, mask, 3, 0)
                at_lag(0, conv, 1, 2)
                at_lag(3, mask, 5, 1)
                at_lag(0, conv, 1, 1)
                at_lag(0, conv, 1, 0)
                at_lag(2, mask, 4, 0)
                at_lag(3, S_lo)
                at_lag(4, add)
                at_lag(3, mask, 6, 1)
                at_lag(3, gated_0)
                at_lag(3, right_side_1)

            drive(dve, step)
            ready(dve, s_acc, NJ - 1)
            for t in range(0, NT, 4):
                v.tensor_tensor(acca[:, t:t + 4, :], acca[:, t:t + 4, :], accf[:, t:t + 4, :], ALU.mult).then_inc(s_mul, 1)
                dve.wait_ge(s_mul, t // 4 + 1)
                v.tensor_tensor(xs[:, t:t + 4, :], xs[:, t:t + 4, :], acca[:, t:t + 4, :], ALU.add).then_inc(s_fin, 1)

        @block.tensor
        def _(pe):
            start(pe, "pe")
            mm = nc.tensor.matmul

            def block_of(out, hk, b, m):
                for n, (w, x) in enumerate(((wfh, xh), (wfl, xh), (wfh, xl))):
                    for k in range(KH):
                        last = mm(out, w[:, ds(hk % 2 * FW + k * 768 + m * P, P)], x[:, k, ds(b * T, T)],
                                  start=(n == 0 and k == 0), stop=(n == 2 and k == KH - 1))
                return last

            def project_qk(x):
                take(x, [(s_vt, 2)], [(s_pad[0], 1), (s_t3[0], 1)])
                pe.wait_ge(s_wf, x.hk * 8 + (8 + C0))
                block_of(raw[0][:, 0:T], x.hk, x.b, 0)
                block_of(raw[0][:, T:2 * T], x.hk, x.b, 1).then_inc(s_raw[0], 1)

            def project_v(x):
                take(x, [(s_y[1], 4)], [(s_qkT, 2), (s_acc, 5), (s_yTc, 5), (s_pad[1], 1), (s_t3[1], 1)])
                pe.wait_ge(s_wf, x.hk * 8 + (8 + C0))
                block_of(raw[1][:, 0:T], x.hk, x.b, 2)
                block_of(raw[1][:, T:2 * T], x.hk, x.b, 3).then_inc(s_raw[1], 1)

            def project_z(x):
                base, tok = x.hk % 2 * FW, x.b * T
                take(x, [(s_y[0], 3)], [(s_sz, 1)])
                pe.wait_ge(s_wf, x.hk * 8 + (8 + C0))
                for t in range(2):
                    for n, (w, xn) in enumerate(((wfh, xh), (wfl, xh), (wfh, xl))):
                        for k in range(KH):
                            last = mm(raw_z[:, t * H:(t + 1) * H], xn[:, k, ds(tok + t * P, P)], w[:, ds(base + k * 768 + 512, H)],
                                      start=(n == 0 and k == 0), stop=(n == 2 and k == KH - 1))
                last.then_inc(s_z, 1)

            def qk_to_tokens(x):
                take(x, [(s_A, 1), (s_M, 1)], [(s_sq, 1), (s_qkn, 1)])
                ready(pe, s_silu[0], x.j)
                for n, (m, ch) in enumerate(((1, 0), (1, 1), (0, 0), (0, 1))):
                    last = nc.tensor.transpose(tok_qk[:, n, :], act4[:, m, ch * P:(ch + 1) * P], ident[:])
                last.then_inc(s_tqk, 1)

            def v_to_tokens(x):
                take(x, [(s_pad[0], -1), (s_t3[0], -1)], [(s_vt, 1)])
                ready(pe, s_silu[1], x.j)
                for w in range(2):
                    for ch in range(2):
                        last = nc.tensor.transpose(tok_v[:, 2 * w + ch, :], act4[:, 2 + w, ch * P:(ch + 1) * P], ident[:])
                last.then_inc(s_tv, 1)

            def to_channels(x):
                take(x, [(s_acc, 3)], [(s_yTc, 3), (s_pad[1], -1), (s_t3[1], -1), (s_y[1], 3), (s_qkT, 1)])
                ready(pe, s_qkl, x.j)
                for a, src in enumerate((qkh, qkl)):
                    for ch in range(2):
                        for n in range(2):
                            last = nc.tensor.transpose(chan_qk[:, a * 4 + ch * 2 + n, :], src[:, 2 * n + ch, :], id16[:, 0:P])
                last.then_inc(s_T, 1)

            def similarities(x):
                take(x, [(s_sq, 0), (s_qkn, 0)], [(s_A, 1), (s_M, 1)])
                ready(pe, s_qkT, x.j)
                for ch in range(2):
                    for n, (a, b) in enumerate(((0, 0), (0, 1), (1, 0))):
                        last = mm(sims[:, ch].rearrange("p x t -> p (x t)"), qkT[x.p][:, a, ch, 0, :],
                                  qkT[x.p][:, b, ch].rearrange("p x t -> p (x t)"), start=(n == 0), stop=(n == 2))
                last.then_inc(s_kk, 1)

            def unit(ch, w):
                return 2 * w + ch


            other_before = [
                {1: (2, 1), 2: (3, 1), 3: (4, 1), 4: (5, 1), 5: (6, 1), 6: (6, 1)},
                {1: (6, 0), 2: (6, 0), 3: (1, -1), 4: (2, -1), 5: (3, -1), 6: (4, -1)}]

            def level_P(x, k, ch):
                level, back = other_before[ch][k]
                take(x, [(s_nP[1 - ch], back, NLEV, level)])
                ready(pe, s_X[ch], x.j * NLEV + (k - 1))
                for w in range(2):
                    last = mm(b_P[:, 2 * ch + w, :], Ah[x.p][:, unit(ch, w), :], XX[k % 2][:, 2 * ch + w, 0, :],
                              start=True, stop=True)
                last.then_inc(s_P[ch], 1)

            def level_X(x, k, ch):
                ready(pe, s_nP[ch], x.j * NLEV + k)
                if k == 0:
                    spare(pe, s_X[ch], x.j * NLEV)
                    mm(b_X[:, 2 * ch:2 * ch + 2].rearrange("p u a t -> p (u a t)"), id16[:, 0:P], id16[:],
                       start=True, stop=False, skip_group_check=True)
                for u in range(2 * ch, 2 * ch + 2):
                    side = lambda a: b_X[:, u, a, :]
                    grow = lambda a, lhs, rhs: mm(side(a), lhs, rhs, start=False, stop=True, skip_group_check=True)
                    if k == 0:
                        grow(0, nP[:, u, :], id16[:, 0:P])
                        last = grow(1, id16[:, 0:P], nP[:, u, :])
                    else:
                        xt = XX[k % 2][:, u, 1, :]
                        if k < NLEV - 1:
                            grow(0, xt, nP[:, u, :])
                        last = grow(1, nP[:, u, :], xt)
                last.then_inc(s_Z[ch], 1)

            def solve(x, ch):
                ready(pe, s_Rh[ch], x.j)
                ready(pe, s_X[ch], x.j * NLEV + (NLEV - 1))
                if ch == 0:
                    spare(pe, s_Dl[1], x.j)
                else:
                    ready(pe, s_QS, x.j)
                for w in range(2):
                    last = mm(b_s[:, w, :], XF[x.p][:, 2 * ch + w, :], Rh[:, w, :], start=True, stop=True)
                last.then_inc(s_d[ch], 1)

            def residual(x, ch):
                ready(pe, s_Dh[ch], x.j)
                ready(pe, s_Al, x.j)
                for w in range(2):
                    for m, lhs in enumerate((id16[:, 0:P], Ah[x.p][:, unit(ch, w), :], Al[x.p][:, unit(ch, w), :])):
                        last = mm(b_s[:, w, :], lhs, Dh[ch][:, w, :], start=(m == 0), stop=(m == 2))
                last.then_inc(s_rs[ch], 1)

            def correct(x, ch):
                ready(pe, s_r[ch], x.j)
                for w in range(2):
                    last = mm(b_s[:, w, :], XF[x.p][:, 2 * ch + w, :], rh[:, w, :], start=True, stop=True)
                last.then_inc(s_dd[ch], 1)

            def outputs(x, ch):
                if ch == 0:
                    take(x, [(s_sz, -2)], [(s_y[0], 1)])
                else:
                    take(x, [(s_qkT, -2)], [(s_acc, 1), (s_yTc, 1), (s_pad[1], -3), (s_t3[1], -3), (s_y[1], 1)])
                ready(pe, s_Dl[ch], x.j)
                ready(pe, s_Ml, x.j)
                for w in range(2):
                    for m, (a, d) in enumerate(((Mh, Dh), (Ml, Dh), (Mh, Dl))):
                        last = mm(outs[ch][:, w, :], a[x.p][:, unit(ch, w), :], d[ch][:, w, :], start=(m == 0), stop=(m == 2))
                last.then_inc(s_o[ch], 1)

            def state(x):
                ready(pe, s_Dl[0], x.j)
                ready(pe, s_kw, x.j)
                for w in range(2):
                    for m, (a, d) in enumerate(((kwh, Dh), (kwl, Dh), (kwh, Dl))):
                        last = mm(b_s[:, w, :], a[x.p][:, w, :], d[0][:, w, :], start=(m == 0), stop=(m == 2))
                last.then_inc(s_S, 1)

            def on_state(x):
                ready(pe, s_Sl, x.j)
                for n in range(2):
                    for m, (a, d) in enumerate(((0, Sh), (0, Sl), (1, Sh))):
                        last = mm(b_s[:, 2 * n:2 * n + 2, :].rearrange("p v t -> p (v t)"), qkT[x.p][:, a, 1, n, :],
                                  d[:].rearrange("p v t -> p (v t)"), start=(m == 0), stop=(m == 2))
                last.then_inc(s_KQ, 1)

            def y_T(x):
                take(x, [(s_pad[1], -4), (s_t3[1], -4)], [(s_y[1], 0), (s_qkT, -2), (s_acc, 1), (s_yTc, 1)])
                ready(pe, s_yl, x.j)
                for a, src in enumerate((yh, yl)):
                    for w in range(4):
                        last = nc.tensor.transpose(chan_y[:, a * 4 + w, :], src[:, w, :], id16[:, 0:P])
                last.then_inc(s_yT, 1)

            def out(x):
                take(x, [(s_yTc, 0)], [(s_pad[1], -4), (s_t3[1], -4), (s_y[1], 0), (s_qkT, -2), (s_acc, 1)])
                ready(pe, s_yTc, x.j)
                pe.wait_ge(s_wo, x.hk * 8 + (8 + C0))
                base = x.hk % 2 * OW
                for ch in range(2):
                    for w in range(2):
                        for m, (a, wt) in enumerate(((0, woh), (0, wol), (1, woh))):
                            last = mm(prod[:, ch * H:(ch + 1) * H], yT[:, a, 2 * ch + w, :], wt[:, ds(base + w * H, H)],
                                      start=(w == 0 and m == 0), stop=(w == 1 and m == 2))
                last.then_inc(s_out, 1)

            def step(at_lag):
                at_lag(4, level_P, 6, 1)
                at_lag(3, level_X, 4, 0)
                at_lag(4, on_state)
                at_lag(2, to_channels)
                at_lag(3, level_P, 5, 0)
                at_lag(4, level_X, 6, 1)
                at_lag(0, project_qk)
                at_lag(3, level_X, 5, 0)
                at_lag(2, similarities)
                at_lag(4, solve, 1)
                at_lag(3, level_X, 0, 1)
                at_lag(3, level_P, 6, 0)
                at_lag(4, residual, 1)
                at_lag(3, level_P, 1, 1)
                at_lag(3, level_X, 6, 0)
                at_lag(4, correct, 1)
                at_lag(3, level_X, 1, 1)
                at_lag(4, outputs, 1)
                at_lag(2, level_X, 0, 0)
                at_lag(3, level_P, 2, 1)
                at_lag(1, qk_to_tokens)
                at_lag(1, v_to_tokens)
                at_lag(3, solve, 0)
                at_lag(2, level_P, 1, 0)
                at_lag(3, level_X, 2, 1)
                at_lag(0, project_v)
                at_lag(3, level_P, 3, 1)
                at_lag(2, level_X, 1, 0)
                at_lag(3, residual, 0)
                at_lag(3, level_X, 3, 1)
                at_lag(2, level_P, 2, 0)
                at_lag(1, project_z)
                at_lag(2, level_X, 2, 0)
                at_lag(3, level_P, 4, 1)
                at_lag(3, correct, 0)
                at_lag(2, level_P, 3, 0)
                at_lag(3, level_X, 4, 1)
                at_lag(4, y_T)
                at_lag(2, level_X, 3, 0)
                at_lag(3, level_P, 5, 1)
                at_lag(3, outputs, 0)
                at_lag(3, state)
                at_lag(3, level_X, 5, 1)
                at_lag(2, level_P, 4, 0)
                at_lag(4, out)

            drive(pe, step)


def build(nc, A, NB, NHK):
    NT, N = NB * 2, NB * T
    with ExitStack() as c:
        def sb(name, shape, dt=F32):
            return c.enter_context(nc.sbuf_tensor(name, shape, dt))

        S = {
            "xs": sb("x_tok", [P, NT, H]),
            "xh": sb("xT_hi", [P, KH, N], F16),
            "xl": sb("xT_lo", [P, KH, N], F16),
            "accf": sb("ffn_sum", [P, NT, H]),
            "acca": sb("attn_sum", [P, NT, H]),
            "ident": sb("identity", [P, P]),
            "ident4": sb("identity4", [P, 4 * P]),
            "id16": sb("identity4_16", [P, 4 * P], F16),
            "inj": sb("scan_starts", [P, 4 * P]),
            "nmask32": sb("level_masks32", [P, NLEV, P]),
            "nmask": sb("level_masks", [P, NLEV, P], F16),
            "cw": sb("conv_w", [P, NHK * 16]),
            "nw": sb("norm_w", [P, 1]),
            "b1": sb("b1", [P, NE * IC]),
            "half": sb("minus_half", [P, 4]),
            "tiny": sb("tiny", [P, 4]),
            "col": sb("gin_beta_cols", [P, NT, 64]),
            "ngin": sb("neg_gin_cols", [P, NT, 32]),
            "gate": sb("gate", [P, NT, NE]),
            "gc": sb("gate_and_bias_weight", [P, NT, 2 * NE]),
        }
        setup_phase(nc, c, A, S, NB, NHK)
        ffn_phase(nc, A, S, NB, NHK)
        attention_phase(nc, A, S, NB, NHK)


def shape_constants():
    t = np.arange(P)
    ident = np.eye(P, dtype=np.float32)
    ident4 = np.tile(ident, (1, 4))
    starts = np.tile(np.eye(P, k=1, dtype=np.float32), (1, 4))
    masks = np.zeros((P, NLEV, P), np.float32)
    for k in range(NLEV):
        b = t >> k
        masks[:, k, :] = -((b[:, None] % 2 == 1) & (b[None, :] == b[:, None] - 1)).astype(np.float32)
    masks[:, 0, :] = masks[:, 0, :].T
    rank = np.tile(np.arange(NE, 0, -1, dtype=np.float32), (P, 1))
    return {"ident": ident, "ident4": ident4, "inj": starts, "nmask": masks, "rank": rank}


def kernel(L0_attn_x, L0_attn_W_qkv, L0_attn_W_z, L0_attn_W_b, L0_attn_W_a, L0_attn_conv_w, L0_attn_dt_bias,
           L0_attn_A_log, L0_attn_norm_w, L0_attn_W_out, L0_ffn_rw1, L0_ffn_rw2, L0_ffn_w1, L0_ffn_b1, L0_ffn_w2,
           L0_ffn_b2):
    import numpy as np
    import concourse.bacc as bacc
    from concourse.bass_utils import run_bass_kernel_spmd

    g = lambda a: np.asarray(a)
    x = g(L0_attn_x)
    NB = x.shape[0]
    wqkv, wz, wout = g(L0_attn_W_qkv), g(L0_attn_W_z), g(L0_attn_W_out)
    NHK = wz.shape[0] // 256
    K = NHK * P
    q, k, v = wqkv[:K].reshape(NHK, P, H), wqkv[K:2 * K].reshape(NHK, P, H), wqkv[2 * K:].reshape(NHK, 2 * P, H)
    front = np.concatenate([q, k, v, wz.reshape(NHK, 2 * P, H)], axis=1)
    front = front.reshape(NHK, 768, KH, P).transpose(0, 3, 2, 1).reshape(NHK, P, FW)
    outw = wout.T.reshape(NHK, 2, P, H).transpose(0, 2, 1, 3).reshape(NHK, P, OW)
    chunks = np.concatenate([front.reshape(NHK, P, 8, FCH), outw.reshape(NHK, P, 8, OCH)], axis=3)
    chunks = chunks.transpose(0, 2, 1, 3).reshape(NHK * 8, P, FCH + OCH)
    wattn = np.concatenate([chunks, np.zeros((8, P, FCH + OCH), np.float32)], axis=0)
    cw = g(L0_attn_conv_w)[:, 0, :]
    cw = np.stack([cw[:K].reshape(NHK, P, 4), cw[K:2 * K].reshape(NHK, P, 4),
                   cw[2 * K:].reshape(NHK, 2, P, 4)[:, 0], cw[2 * K:].reshape(NHK, 2, P, 4)[:, 1]], axis=1)
    cw = cw.transpose(2, 0, 1, 3).reshape(P, NHK * 16)

    def col32(a):
        out = np.zeros((32, 1), np.float32)
        out[:a.shape[0], 0] = a
        return out

    def rows32(w):
        out = np.zeros((32, H), np.float32)
        out[:w.shape[0]] = w
        return out

    wab = np.concatenate([rows32(g(L0_attn_W_a)), rows32(g(L0_attn_W_b))], axis=0).reshape(64, KH, P).transpose(2, 1, 0)
    w1 = g(L0_ffn_w1).reshape(NE, KH, P, I).transpose(0, 2, 1, 3).reshape(NE, P, KH * I)
    w2 = g(L0_ffn_w2).reshape(NE, IC, P, H).transpose(0, 2, 1, 3).reshape(NE, P, IC * H)
    arrays = {
        "x": x.reshape(NB * T, H),
        "wattn": wattn,
        "wffn": np.concatenate([w1, w2], axis=2),
        "cw": cw,
        "wab": wab,
        "dtb": col32(g(L0_attn_dt_bias)),
        "alog": col32(g(L0_attn_A_log)),
        "nw": g(L0_attn_norm_w).reshape(P, 1),
        "rw1": g(L0_ffn_rw1).reshape(KH, P, P).transpose(1, 0, 2),
        "rw2": g(L0_ffn_rw2),
        "b1": g(L0_ffn_b1).reshape(NE, IC, P).transpose(2, 0, 1).reshape(P, NE * IC),
        "b2": g(L0_ffn_b2),
        **shape_constants(),
    }
    arrays = {f"in_{n}": np.ascontiguousarray(a) for n, a in arrays.items()}
    nc = bacc.Bacc("TRN2", target_bir_lowering=False, num_devices=1)
    A = {n[3:]: nc.dram_tensor(n, a.shape, mybir.dt.from_np(a.dtype), kind="ExternalInput").ap() for n, a in arrays.items()}
    A["dscr"] = nc.dram_tensor("decay_scratch", (2 * NHK, NB * T), F32, kind="Internal").ap()
    A["cgscr"] = nc.dram_tensor("bias_only_scratch", (NE, H), F32, kind="Internal").ap()
    A["out"] = nc.dram_tensor("out", (NB * T, H), F32, kind="ExternalOutput").ap()
    build(nc, A, NB, NHK)
    r = run_bass_kernel_spmd(nc, [arrays], core_ids=[0])
    return r.results[0]["out"].reshape(NB, T, H)
```
